# Optimizing a Trainium2 kernel written in Bass

```python
import numpy as np
import jax
import jax.numpy as jnp

def _softmax(x, axis=-1):
    return jax.nn.softmax(x, axis=axis)

def _gelu(x):
    return jax.nn.gelu(x, approximate=True)

def _silu(x):
    return jax.nn.silu(x)

def _sigmoid(x):
    return jax.nn.sigmoid(x)

def _layernorm(x, axis=-1, eps=1e-05):
    m = jnp.mean(x, axis=axis, keepdims=True)
    v = jnp.var(x, axis=axis, keepdims=True)
    return (x - m) / jnp.sqrt(v + eps)

def _scatter_add(tgt, idx, src, axis=0):
    return tgt.at[idx].add(src)

def _segment_sum(src, seg, n):
    return jax.ops.segment_sum(src, seg, n)
kernel_name = 'mk_vit_tower_d1_tok_img768_r4_4aaa94'

def setup_inputs(seed: int=0):
    np.random.seed(seed)
    _w = jnp.asarray

    def _rec_inputs():
        import jax
        import jax.numpy as jnp
        _rk = jax.random.key(seed)
        x = 7.57192e-06 + 1.00007 * jax.random.normal(jax.random.fold_in(_rk, 1), (64, 3, 224, 224), jnp.float32)
        return x
    x = _rec_inputs()

    def _L0_tok_setup():
        import jax, jax.numpy as jnp
        import numpy as np
        B, C, H, W_IMG, P, D = (64, 3, 224, 224, 16, 192)
        N_PATCH = H // P * (W_IMG // P)
        SEQ = N_PATCH + 1

        def _patchify(x):
            b = x.shape[0]
            hp, wp = (H // P, W_IMG // P)
            x = x.reshape(b, C, hp, P, wp, P)
            x = x.transpose(0, 2, 4, 1, 3, 5)
            return x.reshape(b, hp * wp, C * P * P)
        key = jax.random.key(seed)
        k1, k2, k3, k4, k5 = jax.random.split(key, 5)
        in_feat = P * P * C
        return {'x': jax.random.normal(k1, (B, C, H, W_IMG), dtype=jnp.float32), 'W': jax.random.normal(k2, (in_feat, D), dtype=jnp.float32) * (1.0 / np.sqrt(in_feat)), 'b': jax.random.normal(k3, (D,), dtype=jnp.float32) * 0.02, 'pos_table': jax.random.normal(k4, (SEQ, D), dtype=jnp.float32) * 0.02, 'class_token': jax.random.normal(k5, (1, 1, D), dtype=jnp.float32)}
    _L0_tok_all = _L0_tok_setup()
    _L0_tok_in = {k: v for k, v in _L0_tok_all.items() if k in ('W', 'b', 'pos_table', 'class_token')}
    del _L0_tok_all

    def _L0_attn_setup():
        import jax, jax.numpy as jnp
        import numpy as np
        NUM_HEADS = 12
        SCRA_SCALING = 10.0
        EPS = 1e-12
        key = jax.random.key(seed)
        ks = jax.random.split(key, 5)
        B, N, C = (2, 512, 192)
        return {'x': jax.random.normal(ks[0], (B, N, C), dtype=jnp.float32), 'qkv_w': jax.random.normal(ks[1], (3 * C, C), dtype=jnp.float32) * 0.02, 'qkv_b': jax.random.normal(ks[2], (3 * C,), dtype=jnp.float32) * 0.02, 'proj_w': jax.random.normal(ks[3], (C, C), dtype=jnp.float32) * 0.02, 'proj_b': jax.random.normal(ks[4], (C,), dtype=jnp.float32) * 0.02}
    _L0_attn_all = _L0_attn_setup()
    _L0_attn_in = {k: v for k, v in _L0_attn_all.items() if k in ('qkv_w', 'qkv_b', 'proj_w', 'proj_b')}
    del _L0_attn_all

    def _L0_ffn_setup():
        import jax, jax.numpy as jnp
        import numpy as np
        B, S, D = (2, 512, 192)
        E, K, F = (8, 2, 384)

        def _swiglu(xf, wg, wu, wd):
            return jax.nn.silu(xf @ wg.T) * (xf @ wu.T) @ wd.T
        key = jax.random.key(seed)
        ks = jax.random.split(key, 9)
        scale = 0.02
        x = jax.random.normal(ks[0], (B, S, D), dtype=jnp.float32)
        w_router = jax.random.normal(ks[1], (E, D), dtype=jnp.float32) * scale
        expert_bias = jnp.zeros((E,), dtype=jnp.float32)
        Wg = jax.random.normal(ks[2], (E, F, D), dtype=jnp.float32) * scale
        Wu = jax.random.normal(ks[3], (E, F, D), dtype=jnp.float32) * scale
        Wd = jax.random.normal(ks[4], (E, D, F), dtype=jnp.float32) * scale
        sg = jax.random.normal(ks[5], (F, D), dtype=jnp.float32) * scale
        su = jax.random.normal(ks[6], (F, D), dtype=jnp.float32) * scale
        sd = jax.random.normal(ks[7], (D, F), dtype=jnp.float32) * scale
        return {'x': x, 'w_router': w_router, 'expert_bias': expert_bias, 'Wg': Wg, 'Wu': Wu, 'Wd': Wd, 'sg': sg, 'su': su, 'sd': sd}
    _L0_ffn_all = _L0_ffn_setup()
    _L0_ffn_in = {k: v for k, v in _L0_ffn_all.items() if k in ('w_router', 'expert_bias', 'Wg', 'Wu', 'Wd', 'sg', 'su', 'sd')}
    del _L0_ffn_all
    return {'x': x, 'L0_tok_W': _L0_tok_in['W'], 'L0_tok_b': _L0_tok_in['b'], 'L0_tok_pos_table': _L0_tok_in['pos_table'], 'L0_tok_class_token': _L0_tok_in['class_token'], 'L0_attn_qkv_w': _L0_attn_in['qkv_w'], 'L0_attn_qkv_b': _L0_attn_in['qkv_b'], 'L0_attn_proj_w': _L0_attn_in['proj_w'], 'L0_attn_proj_b': _L0_attn_in['proj_b'], 'L0_ffn_w_router': _L0_ffn_in['w_router'], 'L0_ffn_expert_bias': _L0_ffn_in['expert_bias'], 'L0_ffn_Wg': _L0_ffn_in['Wg'], 'L0_ffn_Wu': _L0_ffn_in['Wu'], 'L0_ffn_Wd': _L0_ffn_in['Wd'], 'L0_ffn_sg': _L0_ffn_in['sg'], 'L0_ffn_su': _L0_ffn_in['su'], 'L0_ffn_sd': _L0_ffn_in['sd']}

def reference(x, L0_tok_W, L0_tok_b, L0_tok_pos_table, L0_tok_class_token, L0_attn_qkv_w, L0_attn_qkv_b, L0_attn_proj_w, L0_attn_proj_b, L0_ffn_w_router, L0_ffn_expert_bias, L0_ffn_Wg, L0_ffn_Wu, L0_ffn_Wd, L0_ffn_sg, L0_ffn_su, L0_ffn_sd):
    import jax
    import jax.numpy as jnp

    def _L0_tok_ref(x, W, b, pos_table, class_token):
        import jax, jax.numpy as jnp
        import numpy as np
        B, C, H, W_IMG, P, D = (64, 3, 224, 224, 16, 192)
        N_PATCH = H // P * (W_IMG // P)
        SEQ = N_PATCH + 1

        def _patchify(x):
            b = x.shape[0]
            hp, wp = (H // P, W_IMG // P)
            x = x.reshape(b, C, hp, P, wp, P)
            x = x.transpose(0, 2, 4, 1, 3, 5)
            return x.reshape(b, hp * wp, C * P * P)
        patches = _patchify(x)
        tokens = jnp.einsum('bnf,fd->bnd', patches, W) + b
        cls = jnp.broadcast_to(class_token, (x.shape[0], 1, D))
        seq = jnp.concatenate([cls, tokens], axis=1)
        return seq + pos_table[None, :, :]

    def _L0_attn_ref(x, qkv_w, qkv_b, proj_w, proj_b):
        import jax, jax.numpy as jnp
        import numpy as np
        NUM_HEADS = 12
        SCRA_SCALING = 10.0
        EPS = 1e-12
        B, N, C = x.shape
        H = NUM_HEADS
        D = C // H
        scale = D ** (-0.5)
        xt = jnp.transpose(x, (1, 0, 2))
        qkv = xt @ qkv_w.T + qkv_b
        q, k, v = jnp.split(qkv, 3, axis=-1)

        def to_bh(t):
            return jnp.transpose(t.reshape(N, B * H, D), (1, 0, 2))
        q, k, v = (to_bh(q), to_bh(k), to_bh(v))
        attn = jax.nn.softmax(jnp.einsum('bnd,bmd->bnm', q, k) * scale, axis=-1)
        out = jnp.einsum('bnm,bmd->bnd', attn, v)
        out = jnp.transpose(out, (1, 0, 2)).reshape(N, B, C)
        out = out @ proj_w.T + proj_b
        out = jnp.transpose(out.reshape(N, B * H, D), (1, 0, 2))
        norm = jnp.linalg.norm(out, axis=-1, keepdims=True)
        sim_tokens = out / jnp.maximum(norm, EPS)
        sim = jnp.einsum('bnd,bmd->bnm', sim_tokens, sim_tokens) * SCRA_SCALING
        sim = jnp.where(sim < 0, -jnp.inf, sim)
        sim = jax.nn.softmax(sim, axis=-1)
        out2 = jnp.einsum('bnm,bmd->bnd', sim, v)
        out2 = jnp.transpose(out2, (1, 0, 2)).reshape(N, B, C)
        out2 = out2 @ proj_w.T + proj_b
        return jnp.transpose(out2, (1, 0, 2))

    def _L0_ffn_ref(x, w_router, expert_bias, Wg, Wu, Wd, sg, su, sd):
        import jax, jax.numpy as jnp
        import numpy as np
        B, S, D = (2, 512, 192)
        E, K, F = (8, 2, 384)

        def _swiglu(xf, wg, wu, wd):
            return jax.nn.silu(xf @ wg.T) * (xf @ wu.T) @ wd.T
        b, s, d = x.shape
        xf = x.reshape(-1, d)
        T = xf.shape[0]
        e = w_router.shape[0]
        logits = xf @ w_router.T
        scores = jax.nn.softmax(logits, axis=-1)
        selection = scores + expert_bias[None, :]
        _, top_idx = jax.lax.top_k(selection, K)
        top_s = jnp.take_along_axis(scores, top_idx, axis=-1)
        top_s = top_s / (jnp.sum(top_s, axis=-1, keepdims=True) + 1e-09)
        comb = jnp.zeros((T, e), dtype=x.dtype).at[jnp.arange(T)[:, None], top_idx].add(top_s)

        def body(acc, p):
            wg, wu, wd, c = p
            return (acc + c[:, None] * _swiglu(xf, wg, wu, wd), None)
        routed, _ = jax.lax.scan(body, jnp.zeros_like(xf), (Wg, Wu, Wd, comb.T))
        out = routed + _swiglu(xf, sg, su, sd)
        return out.reshape(b, s, d)
    h = _L0_tok_ref(x, L0_tok_W, L0_tok_b, L0_tok_pos_table, L0_tok_class_token)
    h = h + _L0_attn_ref(_layernorm(h, axis=-1), L0_attn_qkv_w, L0_attn_qkv_b, L0_attn_proj_w, L0_attn_proj_b)
    h = h + _L0_ffn_ref(_layernorm(h, axis=-1), L0_ffn_w_router, L0_ffn_expert_bias, L0_ffn_Wg, L0_ffn_Wu, L0_ffn_Wd, L0_ffn_sg, L0_ffn_su, L0_ffn_sd)
    return h

_drawn_inputs = setup_inputs


def setup_inputs(seed=0):
    import zlib

    import numpy as np

    out = dict(_drawn_inputs(seed))
    spreads = {'L0_ffn_expert_bias': (0.0, 0.634)}
    factors = {'L0_tok_b': 2.797,
     'L0_tok_pos_table': 2.847,
     'L0_attn_qkv_w': 8.0,
     'L0_attn_qkv_b': 8.0,
     'L0_attn_proj_w': 6.719,
     'L0_attn_proj_b': 2.929,
     'L0_ffn_w_router': 8.0,
     'L0_ffn_Wg': 5.093,
     'L0_ffn_Wu': 5.06,
     'L0_ffn_Wd': 5.07,
     'L0_ffn_sg': 3.698,
     'L0_ffn_su': 3.644,
     'L0_ffn_sd': 3.658}
    for name, (base, spread) in spreads.items():
        noise = np.random.default_rng([zlib.crc32(name.encode()), seed]).standard_normal(out[name].shape)
        drawn = base * np.exp(spread * noise) if base else spread * noise
        out[name] = jnp.asarray(drawn.astype(out[name].dtype))
    for name, factor in factors.items():
        out[name] = (out[name] * factor).astype(out[name].dtype)
    return out
```

```python
from contextlib import ExitStack

import concourse.bass as bass
from concourse import mybir

F32 = mybir.dt.float32
F16 = mybir.dt.float16
I32 = mybir.dt.int32
ALU = mybir.AluOpType
ACT = mybir.ActivationFunctionType
AX = mybir.AxisListType

B, CH, IMG, P = 64, 3, 224, 16
D = 192
SIDE = IMG // P
SEQ = SIDE * SIDE + 1
FEAT = CH * P * P
KF = FEAT // 128
HEADS, HD = 12, 16
E, FF = 8, 384
DC = D // 2
HALF = 98
TR = SEQ - HALF
SP = SEQ + 1
SLOT = 64
NG = HEADS // 2
STEPS_A = 2 * 30
ATT_SCALE, SIM_SCALE = HD ** -0.5, 10.0
NORM_EPS2, LN_EPS = 1e-24, 1e-5
RSQRT_MAGIC = 1597463007.0

TOK = B * SEQ
GT = 512
NT = GT // 128
GROUPS = -(-TOK // GT)
PAD = GROUPS * GT - TOK
TAIL = TOK - (GROUPS - 1) * GT
KFF = FF // 128


class Ring:

    def __init__(self, full, free, jobs, freeing=None):
        self.full, self.free, self.n = full, free, len(full)
        self.place = {j: (k % self.n, k // self.n) for k, j in enumerate(jobs)}
        self.uses = [len(range(s, len(jobs), self.n)) for s in range(self.n)]
        signs = [freeing is None or j[0] in freeing for j in jobs]
        self.before = {j: sum(signs[k % self.n:k:self.n]) for k, j in enumerate(jobs)}
        self.frees = [sum(signs[s::self.n]) for s in range(self.n)]

    def slot(self, job):
        return self.place[job][0]

    def wait_free(self, eng, job, it):
        s = self.slot(job)
        eng.wait_ge(self.free[s], it * self.frees[s] + self.before[job] + 1)

    def wait_freed(self, eng, job, it):
        s = self.slot(job)
        eng.wait_ge(self.free[s], it * self.frees[s] + self.before[job] + 2)

    def wait_full(self, eng, job, it):
        s, k = self.place[job]
        eng.wait_ge(self.full[s], it * self.uses[s] + k + 1)

    def filled(self, ins, job):
        ins.then_inc(self.full[self.slot(job)], 1)

    def freed(self, ins, job):
        ins.then_inc(self.free[self.slot(job)], 1)


class Steps:

    def __init__(self, eng, sem):
        self.eng, self.sem, self.base, self.n = eng, sem, 0, 0

    def __call__(self, ins):
        ins.then_inc(self.sem, 1)
        self.n += 1
        self.eng.wait_ge(self.sem, self.base + self.n)

    def start(self, base):
        self.base, self.n = base, 0


def rsqrt(dve, step, y, v, tmp):
    step(dve.tensor_scalar(y.bitcast(I32), v.bitcast(I32), 1, None, ALU.logical_shift_right))
    step(dve.tensor_scalar(y.bitcast(I32), y.bitcast(I32), -1.0, RSQRT_MAGIC, ALU.mult, ALU.add))
    for _ in range(3):
        step(dve.scalar_tensor_tensor(tmp, y, -0.5, y, ALU.mult, ALU.mult))
        step(dve.tensor_tensor(tmp, tmp, v, ALU.mult))
        step(dve.scalar_tensor_tensor(y, tmp, 1.5, y, ALU.add, ALU.mult))


def attention_phase(nc, sems, xT, w_tok, addend, pos, w_qkv, w_proj, eye, key_mask, h1):
    with ExitStack() as ctx:
        def sb(name, shape, dt=F32):
            return ctx.enter_context(nc.sbuf_tensor(name, shape, dt))

        def ps(name, shape, dt=F32):
            return ctx.enter_context(nc.psum_tensor(name, shape, dt))

        def sem(name):
            return sems.enter_context(nc.semaphore(name))

        wt32 = sb("wt32", [128, KF * D])
        wt = sb("wt", [128, 2, KF, D], F16)
        wq32 = sb("wq32", [DC + 1, 2, 3 * D])
        wq = sb("wq", [DC + 1, 2, 2, 3 * D], F16)
        wp32 = sb("wp32", [DC + 1, 2, D])
        wp = sb("wp", [DC + 1, 2, 2, D], F16)
        base = sb("base", [TR, 2, D])
        pos_sb = sb("pos_sb", [TR, 2, D])
        eye32 = sb("eye32", [128, 128])
        eye16 = sb("eye16", [128, 128], F16)
        mask = sb("mask", [TR, 2])
        xt = [sb(f"xt{i}", [128, KF, SEQ]) for i in range(2)]
        xh = [sb(f"xh{i}", [128, KF, SEQ], F16) for i in range(2)]
        xl = [sb(f"xl{i}", [128, KF, SEQ], F16) for i in range(2)]
        h = [sb(f"h{i}", [TR, 2, D]) for i in range(2)]
        xn = [sb(f"xn{i}", [TR, 2, D]) for i in range(2)]
        th = [sb(f"th{i}", [DC + 1, 2, SEQ], F16) for i in range(2)]
        tl = [sb(f"tl{i}", [DC + 1, 2, SEQ], F16) for i in range(2)]
        st = [sb(f"st{i}", [TR, 2, 2, HEADS, SLOT], F16) for i in range(2)]
        lT = [sb(f"lT{i}", [128, NG, SP], F16) for i in range(2)]
        mT = [sb(f"mT{i}", [128, NG, SP], F16) for i in range(2)]
        rT = [sb(f"rT{i}", [128, NG, SP], F16) for i in range(2)]
        va = [sb(f"va{i}", [TR, 2, HEADS, HD + 1]) for i in range(2)]
        out = [sb(f"out{i}", [TR, 2, D]) for i in range(2)]
        probs = [sb(f"probs{k}", [TR, 2, 2 * SEQ]) for k in range(3)]
        stats = sb("stats", [TR, 2, 6])
        mv = sb("mv", [TR, 2, 2])
        var = sb("var", [TR, 2 * HEADS])
        rstd = sb("rstd", [TR, 2 * HEADS])
        tmp = sb("tmp", [TR, 2 * HEADS])
        den = sb("den", [TR, 2, HEADS])
        sq = sb("sq", [TR, 2, D])
        sn = sb("sn", [TR, 2, D])
        zrow = sb("zrow", [PAD // 2, 2 * D])

        bank = [ps(f"bank{k}", [128, 512]) for k in range(3)]
        score = [ps(f"score{k}", [128, 2, 512]) for k in range(2)]
        pv = ps("pv", [128, 512])

        weights_in = sem("weights_in")
        consts_done = sem("consts_done")
        act_setup = sem("act_setup")
        x_in = [sem(f"x_in{i}") for i in range(2)]
        x_split = sem("x_split")
        x_hi = sem("x_hi")
        dup_done = sem("dup_done")
        hi_done = sem("hi_done")
        hi_T = sem("hi_T")
        hi_qk = sem("hi_qk")
        sn_done = sem("sn_done")
        h_done = sem("h_done")
        waited = sem("waited")
        xn_done = sem("xn_done")
        st_done = sem("st_done")
        exp_done = sem("exp_done")
        stored = [sem(f"stored{i}") for i in range(2)]
        pad_in = sem("pad_in")
        dve_step = sem("dve_step")
        bank_full = [sem(f"bank_full{k}") for k in range(3)]
        bank_free = [sem(f"bank_free{k}") for k in range(3)]
        score_full = [sem(f"score_full{k}") for k in range(2)]
        score_free = [sem(f"score_free{k}") for k in range(2)]
        prob_full = [sem(f"prob_full{k}") for k in range(3)]
        prob_free = [sem(f"prob_free{k}") for k in range(3)]

        ORDER = [("tokens", 0), ("qkv", 0), ("rowmax", 0), ("tokens", 1), ("attend", 0),
                 ("qkv", 1), ("project", 0), ("rowmax", 1), ("attend", 1), ("similar", 0),
                 ("project", 1), ("finish", 0), ("similar", 1), ("finish", 1)]
        UNITS = [(gp, j) for gp in range(NG // 2) for j in range(2)]
        BANKS = {"tokens": ["tok", "xnT"],
                 "qkv": ["qk0", "qk1", "v", "lT0", "lT1", "rT0", "rT1"],
                 "rowmax": ["mT0", "mT1"], "attend": [],
                 "project": ["oT", "proj", "aT0", "aT1", "bT0", "bT1"],
                 "similar": [], "finish": ["o2T", "proj2"]}
        banks = Ring(bank_full, bank_free, [(j, i) for s, i in ORDER for j in BANKS[s]])
        scores = Ring(score_full, score_free, [(s, i, u) for s, i in ORDER
                                               if s in ("rowmax", "attend", "similar") for u in range(6)],
                      freeing=("rowmax",))
        probr = Ring(prob_full, prob_free, [(s, i, u) for s, i in ORDER
                                            if s in ("attend", "similar") for u in range(6)])
        PVS = [(s, i) for s, i in ORDER if s in ("attend", "similar")]
        PREVIOUS = {p: PVS[k - 1] if k else None for k, p in enumerate(PVS)}
        XNS = [(s, i) for s, i in ORDER if s in ("tokens", "attend", "similar")]
        HIS = [(s, i) for s, i in ORDER if s in ("tokens", "project", "finish")]
        STS = [(s, i) for s, i in ORDER if s in ("qkv", "project")]
        EXPS = [(s, i, u) for s, i in ORDER if s in ("similar",) for u in range(6)]

        def cnt(seq, key, it):
            return it * len(seq) + seq.index(key) + 1

        def cols(t):
            return slice(HALF * t, HALF * t + TR)

        def tok_view(b):
            return b[0:TR, 0:2 * D].rearrange("p (t d) -> p t d", t=2)

        def xT_view(b):
            return b[0:DC, 0:2 * SEQ].rearrange("p (c n) -> p c n", c=2)

        def stack_view(b):
            return b[:, :].bitcast(F16)[:, 0:3 * SP].rearrange("p (g n) -> p g n", g=3)

        def pv_view():
            return pv[0:TR, 0:2 * HEADS * (HD + 1)].rearrange("p (t h d) -> p t h d", t=2, h=HEADS)

        def score_view(k):
            return score[k][0:TR, :, 0:2 * SEQ]

        block = ctx.enter_context(nc.Block())

        @block.sync
        def _(sp):
            for dst, src in ((wt32[:, :], w_tok), (wq32[:, :, :], w_qkv), (wp32[:, :, :], w_proj),
                             (base[:, :, :], addend), (pos_sb[:, :, :], pos), (eye32[:, :], eye),
                             (mask[:, :], key_mask)):
                sp.dma_start(dst, src).then_inc(weights_in, 16)
            sp.wait_ge(consts_done, 1)
            sp.dma_start(h1[TOK:TOK + PAD, :].rearrange("(p a) d -> p (a d)", a=2), zrow[:, :]).then_inc(pad_in, 16)
            with sp.Fori(0, B // 2) as it:
                for i in range(2):
                    n = it * 2 + i
                    sp.wait_ge(x_split, n * 1 + 1)
                    sp.dma_start(xt[i][:, :, :], xT[n, :, :, :]).then_inc(x_in[i], 16)
            sp.wait_ge(pad_in, 16)

        @block.gpsimd
        def _(pool):
            for i in range(2):
                pool.memset(st[i][:, :, :, :, :], 0.0)
            pool.memset(zrow[:, :], 0.0).then_inc(consts_done, 1)
            pool.wait_ge(consts_done, 1)
            for i in range(2):
                last = pool.memset(st[i][:, :, 1, :, 48:49], 1.0)
            last.then_inc(consts_done, 1)
            pool.wait_ge(consts_done, 2)
            pool.wait_ge(act_setup, 1)
            pool.sem_inc(x_split, 2)

            def split_x(i, it):
                pool.wait_ge(x_in[i], it * 16 + 16)
                pool.wait_ge(h_done, it * 2 + i + 1)
                pool.sem_inc(waited, 1)
                pool.tensor_copy(xh[i][:, :, :], xt[i][:, :, :]).then_inc(x_hi, 1)
                pool.wait_ge(x_hi, it * 2 + i + 1)
                pool.tensor_tensor(xl[i][:, :, :], xt[i][:, :, :], xh[i][:, :, :],
                                   ALU.subtract).then_inc(x_split, 1)

            def copies(s, i, it):
                if s == "qkv":
                    pool.wait_ge(hi_qk, (it * 2 + i) * 2 + 2)
                else:
                    pool.wait_ge(hi_done, it * 2 + i + 1)
                pool.sem_inc(waited, 1)
                for t in range(2):
                    pool.tensor_copy(st[i][:, t, 0, :, 2 * HD:3 * HD], st[i][:, t, 0, :, 0:HD])
                    last = pool.tensor_copy(st[i][:, t, 1, :, HD:2 * HD], st[i][:, t, 1, :, 0:HD])
                last.then_inc(dup_done, 1)

            with pool.Fori(0, B // 2) as it:
                for s, i in ORDER:
                    if s == "tokens":
                        split_x(i, it)
                    if s in ("qkv", "project"):
                        copies(s, i, it)

        @block.tensor
        def _(pe):
            pe.wait_ge(consts_done, 2)
            pe.wait_ge(act_setup, 1)
            pe.wait_ge(dve_step, 4)
            for k in range(3):
                pe.sem_inc(prob_free[k], 1)

            def transposed(name, s, i, it):
                b = banks.slot((name, i))
                pe.wait_ge(xn_done, cnt(XNS, (s, i), it) + 1)
                banks.wait_free(pe, (name, i), it)
                for t in range(2):
                    for c in range(2):
                        last = pe.transpose(xT_view(bank[b])[:, c, cols(t)],
                                            xn[i][:, t, c * DC:(c + 1) * DC], eye32[0:TR, 0:TR])
                banks.filled(last, (name, i))

            def product(dst, w, i, t, lo, hi):
                parts = [(th, 0), (th, 1), (tl, 0)]
                for c in range(2):
                    rows = DC + 1 if c == 0 else DC
                    for a, x in parts:
                        last = pe.matmul(dst, a[i][0:rows, c, cols(t)], w[0:rows, x, c, lo:hi],
                                         start=(c == 0 and (a, x) == parts[0]),
                                         stop=(c == 1 and (a, x) == parts[2]))
                return last

            def stack_T_out(names, s, i, side, it):
                for half, name in enumerate(names):
                    b = banks.slot((name, i))
                    banks.wait_free(pe, (name, i), it)
                    for g in range(3):
                        for t in range(2):
                            src = st[i][:, t, side, :, :].rearrange("p (g x) s -> p g (x s)", g=NG)
                            last = pe.transpose(stack_view(bank[b])[:, g, cols(t)],
                                                src[:, 3 * half + g, :], eye16[0:TR, 0:TR])
                    banks.filled(last, (name, i))

            def tokens(i, it):
                b = banks.slot(("tok", i))
                pe.wait_ge(x_split, it * 2 + i + 3)
                banks.wait_free(pe, ("tok", i), it)
                parts = [(xh, 0), (xh, 1), (xl, 0)]
                for t in range(2):
                    for k in range(KF):
                        for a, x in parts:
                            last = pe.matmul(tok_view(bank[b])[:, t, :], a[i][:, k, cols(t)],
                                             wt[:, x, k, :], start=(k == 0 and (a, x) == parts[0]),
                                             stop=(k == KF - 1 and (a, x) == parts[2]))
                banks.filled(last, ("tok", i))
                transposed("xnT", "tokens", i, it)

            def qkv(i, it):
                banks.wait_freed(pe, ("xnT", i), it)
                for t in range(2):
                    b = banks.slot((f"qk{t}", i))
                    banks.wait_free(pe, (f"qk{t}", i), it)
                    banks.filled(product(bank[b][0:TR, 0:2 * D], wq, i, t, 0, 2 * D), (f"qk{t}", i))
                b = banks.slot(("v", i))
                banks.wait_free(pe, ("v", i), it)
                for t in range(2):
                    last = product(tok_view(bank[b])[:, t, :], wq, i, t, 2 * D, 3 * D)
                banks.filled(last, ("v", i))
                banks.wait_freed(pe, ("qk1", i), it)
                pe.wait_ge(dup_done, cnt(STS, ("qkv", i), it))
                stack_T_out(["lT0", "lT1"], "qkv", i, 0, it)
                stack_T_out(["rT0", "rT1"], "qkv", i, 1, it)

            def rowmax(i, it):
                banks.wait_freed(pe, ("rT1", i), it)
                for u, (gp, j) in enumerate(UNITS):
                    k = scores.slot(("rowmax", i, u))
                    scores.wait_free(pe, ("rowmax", i, u), it)
                    rows = slice(SLOT * j, SLOT * j + 48)
                    for t in range(2):
                        for gg in range(2):
                            g = 2 * gp + gg
                            last = pe.matmul(score_view(k)[:, t, gg * SEQ:(gg + 1) * SEQ],
                                             lT[i][rows, g, cols(t)], rT[i][rows, g, 0:SEQ],
                                             start=True, stop=True)
                    scores.filled(last, ("rowmax", i, u))
                scores.wait_freed(pe, ("rowmax", i, 5), it)
                stack_T_out(["mT0", "mT1"], "rowmax", i, 0, it)

            def weighted(s, i, it, left, rows_n):
                banks.wait_freed(pe, ("mT1" if s == "attend" else "bT1", i), it)
                if s == "attend":
                    banks.wait_freed(pe, ("v", i), it)

                def unit_scores(u):
                    gp, j = UNITS[u]
                    k = scores.slot((s, i, u))
                    scores.wait_free(pe, (s, i, u), it)
                    rows = slice(SLOT * j, SLOT * j + rows_n)
                    for t in range(2):
                        for gg in range(2):
                            g = 2 * gp + gg
                            last = pe.matmul(score_view(k)[:, t, gg * SEQ:(gg + 1) * SEQ],
                                             rT[i][rows, g, cols(t)], left[i][rows, g, 0:SEQ],
                                             start=True, stop=True)
                    scores.filled(last, (s, i, u))

                def unit_values(u):
                    gp, j = UNITS[u]
                    k = probr.slot((s, i, u))
                    probr.wait_full(pe, (s, i, u), it)
                    if u == 0:
                        done = PREVIOUS[(s, i)]
                        if done:
                            pe.wait_ge(xn_done, cnt(XNS, done, it) + 1)
                        else:
                            pe.wait_ge(xn_done, it * len(XNS) + 1)
                    for gg in range(2):
                        hd = 4 * gp + 2 * gg + j
                        for t in range(2):
                            for kt in range(2):
                                last = pe.matmul(pv_view()[:, t, hd, :],
                                                 probs[k][:, kt, gg * SEQ + HALF * t:gg * SEQ + HALF * t + TR],
                                                 va[i][:, kt, hd, :], start=(kt == 0), stop=(kt == 1))
                    probr.freed(last, (s, i, u))

                unit_scores(0)
                for u in range(6):
                    if u < 5:
                        unit_scores(u + 1)
                    unit_values(u)

            def project(i, it):
                transposed("oT", "attend", i, it)
                b = banks.slot(("proj", i))
                banks.wait_freed(pe, ("oT", i), it)
                banks.wait_free(pe, ("proj", i), it)
                for t in range(2):
                    last = product(tok_view(bank[b])[:, t, :], wp, i, t, 0, D)
                banks.filled(last, ("proj", i))
                pe.wait_ge(st_done, it * 2 + i + 1)
                pe.wait_ge(dup_done, cnt(STS, ("project", i), it))
                stack_T_out(["aT0", "aT1"], "project", i, 0, it)
                stack_T_out(["bT0", "bT1"], "project", i, 1, it)

            def finish(i, it):
                transposed("o2T", "similar", i, it)
                b = banks.slot(("proj2", i))
                banks.wait_freed(pe, ("o2T", i), it)
                banks.wait_free(pe, ("proj2", i), it)
                for t in range(2):
                    last = product(tok_view(bank[b])[:, t, :], wp, i, t, 0, D)
                banks.filled(last, ("proj2", i))

            with pe.Fori(0, B // 2) as it:
                for s, i in ORDER:
                    if s == "tokens":
                        tokens(i, it)
                    elif s == "qkv":
                        qkv(i, it)
                    elif s == "rowmax":
                        rowmax(i, it)
                    elif s == "attend":
                        weighted(s, i, it, mT, 49)
                    elif s == "project":
                        project(i, it)
                    elif s == "similar":
                        weighted(s, i, it, lT, 48)
                    else:
                        finish(i, it)

        @block.scalar
        def _(act):
            act.wait_ge(weights_in, 16 * 7)
            act.activation(wt[:, 0, :, :].rearrange("p k d -> p (k d)"), wt32[:, :], ACT.Copy)
            act.activation(wq[:, 0, :, :], wq32[:, :, :], ACT.Copy)
            act.activation(wp[:, 0, :, :], wp32[:, :, :], ACT.Copy)
            for i in range(2):
                for t in range(2):
                    act.activation(va[i][:, t, :, HD], eye32[0:TR, 0:HEADS], ACT.Identity,
                                   bias=mask[:, t:t + 1], scale=0.0)
            act.activation(eye16[:, :], eye32[:, :], ACT.Copy).then_inc(act_setup, 1)

            def hi_half(name, s, i, it):
                b = banks.slot((name, i))
                banks.wait_full(act, (name, i), it)
                act.activation(th[i][0:DC, :, :], xT_view(bank[b]), ACT.Copy).then_inc(hi_T, 1)

            def hi_slots(i, src, t, last):
                ins = act.activation(st[i][:, t, :, :, 0:HD], src, ACT.Copy)
                if last:
                    ins.then_inc(hi_done, 1)

            def exps(s, i, it, scale):
                for u in range(6):
                    k, q = scores.slot((s, i, u)), probr.slot((s, i, u))
                    scores.wait_full(act, (s, i, u), it)
                    probr.wait_free(act, (s, i, u), it)
                    ins = act.activation(probs[q][:, :, :], score_view(k), ACT.Exp, scale=scale)
                    if s == "attend":
                        probr.filled(ins, (s, i, u))
                    else:
                        ins.then_inc(exp_done, 1)

            def evac_stack(names, s, i, dst, it, only=None):
                for half, name in enumerate(names):
                    b = banks.slot((name, i))
                    banks.wait_full(act, (name, i), it)
                    ins = act.activation(dst[i][:, 3 * half:3 * half + 3, 0:SEQ],
                                         stack_view(bank[b])[:, :, 0:SEQ], ACT.Copy)
                    banks.freed(ins, (name, i))

            with act.Fori(0, B // 2) as it:
                for s, i in ORDER:
                    if s == "tokens":
                        hi_half("xnT", s, i, it)
                    elif s == "qkv":
                        for t in range(2):
                            b = banks.slot((f"qk{t}", i))
                            banks.wait_full(act, (f"qk{t}", i), it)
                            ins = act.activation(
                                st[i][:, t, :, :, 0:HD],
                                bank[b][0:TR, 0:2 * D].rearrange("p (s h d) -> p s h d", s=2, h=HEADS),
                                ACT.Copy)
                            ins.then_inc(hi_qk, 1)
                        b = banks.slot(("v", i))
                        banks.wait_full(act, ("v", i), it)
                        for t in range(2):
                            ins = act.activation(
                                va[i][:, t, :, 0:HD],
                                tok_view(bank[b])[:, t, :].rearrange("p (h d) -> p h d", h=HEADS),
                                ACT.Copy, scale=mask[:, t:t + 1])
                        banks.freed(ins, ("v", i))
                        evac_stack(["lT0", "lT1"], s, i, lT, it)
                        evac_stack(["rT0", "rT1"], s, i, rT, it)
                    elif s == "rowmax":
                        evac_stack(["mT0", "mT1"], s, i, mT, it)
                    elif s == "attend":
                        exps(s, i, it, ATT_SCALE)
                    elif s == "project":
                        hi_half("oT", s, i, it)
                        act.wait_ge(sn_done, it * 2 + i + 1)
                        for side in range(2):
                            ins = act.activation(st[i][:, :, side, :, 0:HD],
                                                 sn[:, :, :].rearrange("p t (h d) -> p t h d", h=HEADS),
                                                 ACT.Copy)
                        ins.then_inc(hi_done, 1)
                        evac_stack(["aT0", "aT1"], s, i, lT, it)
                        evac_stack(["bT0", "bT1"], s, i, rT, it)
                    elif s == "similar":
                        exps(s, i, it, SIM_SCALE)
                    else:
                        hi_half("o2T", s, i, it)
                        banks.wait_freed(act, ("proj2", i), it)
                        n = it * 2 + i
                        act.dma_start(h1[bass.ds(n * SEQ, TR), :], out[i][:, 0, :]).then_inc(stored[i], 16)
                        act.dma_start(h1[bass.ds(n * SEQ + TR, TR - 1), :],
                                      out[i][1:TR, 1, :]).then_inc(stored[i], 16)
            for i in range(2):
                act.wait_ge(stored[i], 16 * B + 32)

        @block.vector
        def _(dve):
            step = Steps(dve, dve_step)
            dve.wait_ge(act_setup, 1)
            dve.wait_ge(weights_in, 16 * 7)
            dve.tensor_tensor(wt[:, 1, :, :].rearrange("p k d -> p (k d)"), wt32[:, :],
                              wt[:, 0, :, :].rearrange("p k d -> p (k d)"), ALU.subtract).then_inc(dve_step, 1)
            for w, w32 in ((wq, wq32), (wp, wp32)):
                dve.tensor_tensor(w[:, 1, :, :], w32[:, :, :], w[:, 0, :, :], ALU.subtract)\
                   .then_inc(dve_step, 1)
            for i in range(2):
                dve.memset(th[i][DC:DC + 1, :, :], 1.0)
                dve.memset(tl[i][DC:DC + 1, :, :], 0.0)
            step.start(3)
            step(dve.tensor_tensor(base[:, :, :], base[:, :, :], pos_sb[:, :, :], ALU.add))
            for k in range(3):
                dve.sem_inc(bank_free[k], 1)
            for k in range(2):
                dve.sem_inc(score_free[k], 1)
            dve.sem_inc(xn_done, 1)
            dve.sem_inc(h_done, 2)
            for i in range(2):
                dve.sem_inc(stored[i], 32)
            SETUP = 4

            def layer_norm(i):
                for t in range(2):
                    ins = dve.bn_stats(stats[:, t, :], h[i][:, t, :])
                    if t == 0:
                        banks.freed(ins, ("tok", i))
                step(ins)
                dve.sem_inc(waited, 1)
                for t in range(2):
                    ins = dve.bn_aggr(mv[:, t, :], stats[:, t, :])
                step(ins)
                step(dve.tensor_scalar(var[:, 0:2], mv[:, :, 1], LN_EPS, None, ALU.add))
                rsqrt(dve, step, rstd[:, 0:2], var[:, 0:2], tmp[:, 0:2])

            def lo_half(name, s, i, it):
                b = banks.slot((name, i))
                dve.wait_ge(hi_T, cnt(HIS, (s, i), it))
                ins = dve.tensor_tensor(tl[i][0:DC, :, :], xT_view(bank[b]), th[i][0:DC, :, :],
                                        ALU.subtract)
                banks.freed(ins, (name, i))

            def normalise(s, i, it):
                probr.wait_freed(dve, (s, i, 5), it)
                step(dve.reciprocal(den[:, :, :], pv_view()[:, :, :, HD]))
                for t in range(2):
                    ins = dve.tensor_tensor(xn[i][:, t, :].rearrange("p (h d) -> p h d", h=HEADS),
                                            pv_view()[:, t, :, 0:HD],
                                            den[:, t, :].unsqueeze(2).broadcast_to([TR, HEADS, HD]),
                                            ALU.mult)
                ins.then_inc(xn_done, 1)

            def tokens(i, it):
                b = banks.slot(("tok", i))
                banks.wait_full(dve, ("tok", i), it)
                ins = dve.tensor_tensor(h[i][:, :, :], tok_view(bank[b]), base[:, :, :], ALU.add)
                ins.then_inc(h_done, 1)
                dve.wait_ge(h_done, it * 2 + i + 3)
                layer_norm(i)
                for t in range(2):
                    ins = dve.tensor_scalar(xn[i][:, t, :], h[i][:, t, :], mv[:, t, 0:1],
                                            rstd[:, t:t + 1], ALU.subtract, ALU.mult)
                ins.then_inc(xn_done, 1)
                lo_half("xnT", "tokens", i, it)

            def qkv(i, it):
                for t in range(2):
                    b = banks.slot((f"qk{t}", i))
                    dve.wait_ge(hi_qk, (it * 2 + i) * 2 + t + 1)
                    for side, lo in ((0, HD), (1, 2 * HD)):
                        ins = dve.tensor_tensor(
                            st[i][:, t, side, :, lo:lo + HD],
                            bank[b][0:TR, side * D:(side + 1) * D].rearrange("p (h d) -> p h d", h=HEADS),
                            st[i][:, t, side, :, 0:HD], ALU.subtract)
                    banks.freed(ins, (f"qk{t}", i))

            def rowmax(i, it):
                for u, (gp, j) in enumerate(UNITS):
                    k = scores.slot(("rowmax", i, u))
                    scores.wait_full(dve, ("rowmax", i, u), it)
                    dst = st[i][:, :, 0, :, 48].rearrange("p t (a b c) -> p t a b c", a=NG // 2, b=2)
                    ins = dve.tensor_reduce(dst[:, :, gp, :, j],
                                            score_view(k).rearrange("p t (g n) -> p t g n", g=2),
                                            AX.X, ALU.max, negate=True)
                    scores.freed(ins, ("rowmax", i, u))

            def project(i, it):
                lo_half("oT", "project", i, it)
                b = banks.slot(("proj", i))
                banks.wait_full(dve, ("proj", i), it)
                banks.freed(dve.tensor_copy(sn[:, :, :], tok_view(bank[b])), ("proj", i))
                banks.wait_freed(dve, ("proj", i), it)
                step(dve.tensor_tensor(sq[:, :, :], sn[:, :, :], sn[:, :, :], ALU.mult))
                step(dve.tensor_reduce(var[:, :], sq[:, :, :].rearrange("p t (h d) -> p (t h) d", h=HEADS),
                                       AX.X, ALU.add))
                step(dve.tensor_scalar(var[:, :], var[:, :], NORM_EPS2, None, ALU.max))
                rsqrt(dve, step, rstd[:, :], var[:, :], tmp[:, :])
                ins = dve.tensor_tensor(sn[:, :, :].rearrange("p t (h d) -> p (t h) d", h=HEADS),
                                        sn[:, :, :].rearrange("p t (h d) -> p (t h) d", h=HEADS),
                                        rstd[:, :].unsqueeze(2).broadcast_to([TR, 2 * HEADS, HD]),
                                        ALU.mult)
                ins.then_inc(sn_done, 1)
                dve.wait_ge(hi_done, it * 2 + i + 1)
                for side, lo in ((0, HD), (1, 2 * HD)):
                    for t in range(2):
                        ins = dve.tensor_tensor(st[i][:, t, side, :, lo:lo + HD],
                                                sn[:, t, :].rearrange("p (h d) -> p h d", h=HEADS),
                                                st[i][:, t, side, :, 0:HD], ALU.subtract)
                ins.then_inc(st_done, 1)

            def similar(i, it):
                for u in range(6):
                    k, q = scores.slot(("similar", i, u)), probr.slot(("similar", i, u))
                    dve.wait_ge(exp_done, cnt(EXPS, ("similar", i, u), it))
                    ins = dve.scalar_tensor_tensor(probs[q][:, :, :], score_view(k), 0.0,
                                                   probs[q][:, :, :], ALU.is_ge, ALU.mult)
                    probr.filled(ins, ("similar", i, u))

            def finish(i, it):
                lo_half("o2T", "finish", i, it)
                b = banks.slot(("proj2", i))
                banks.wait_full(dve, ("proj2", i), it)
                dve.wait_ge(stored[i], it * 32 + 32)
                ins = dve.tensor_tensor(out[i][:, :, :], tok_view(bank[b]), h[i][:, :, :], ALU.add)
                banks.freed(ins, ("proj2", i))

            with dve.Fori(0, B // 2) as it:
                step.start(it * STEPS_A + SETUP)
                for s, i in ORDER:
                    if s == "tokens":
                        tokens(i, it)
                    elif s == "qkv":
                        qkv(i, it)
                    elif s == "rowmax":
                        rowmax(i, it)
                    elif s == "attend":
                        normalise(s, i, it)
                    elif s == "project":
                        project(i, it)
                    elif s == "similar":
                        similar(i, it)
                        normalise(s, i, it)
                    elif s == "finish":
                        finish(i, it)
                assert step.n == STEPS_A, step.n


KS = 5
TT = GT // 128
NE = E + 1
JOBS = NE * KFF
STEPS_F = 36


def feed_forward_phase(nc, sems, h1, w_in, w_down, w_router, e_bias, eye, rank, out):
    with ExitStack() as ctx:
        def sb(name, shape, dt=F32):
            return ctx.enter_context(nc.sbuf_tensor(name, shape, dt))

        def ps(name, shape, dt=F32):
            return ctx.enter_context(nc.psum_tensor(name, shape, dt))

        def sem(name):
            return sems.enter_context(nc.semaphore(name))

        wi32 = [sb(f"wi32_{k}", [128, KS, 2 * FF]) for k in range(2)]
        wi = sb("wi", [128, NE, KS, 2 * FF], F16)
        wd32 = [sb(f"wd32_{k}", [128, KFF, D]) for k in range(2)]
        wd = sb("wd", [128, NE, 2, KFF, D], F16)
        wr32 = sb("wr32", [128, KS, E])
        wr = sb("wr", [128, KS, E], F16)
        wlo = sb("wlo", [128, 2, 2 * FF], F16)
        ebias = sb("ebias", [128, TT, E])
        rank_sb = sb("rank_sb", [128, TT, E])
        eye32 = sb("eye32f", [128, 128])
        eye16 = sb("eye16f", [128, 128], F16)
        acc = [sb(f"acc{i}", [128, TT, D]) for i in range(2)]
        xn = sb("xnf", [128, TT, D])
        xs = sb("xs", [128, TT, KS * 128], F16)
        xsT = [sb(f"xsT{i}", [128, KS, GT], F16) for i in range(2)]
        comb = [sb(f"comb{i}", [128, TT, E]) for i in range(2)]
        sg = [sb(f"sg{k}", [128, GT]) for k in range(3)]
        gu32 = [sb(f"gu32_{k}", [128, GT]) for k in range(3)]
        gh = [sb(f"gh{k}", [128, KFF, GT], F16) for k in range(2)]
        gl = [sb(f"gl{k}", [128, KFF, GT], F16) for k in range(2)]
        stats = sb("statsf", [128, TT, 6])
        mv = sb("mvf", [128, TT, 2])
        small = {n: sb(f"{n}_f", [128, TT]) for n in ("var", "rstd", "tmp", "red")}
        wide = {n: sb(f"{n}_f", [128, TT, E]) for n in ("lg", "sc", "sel", "eq", "oh1", "oh2", "sel2")}

        GU = [ps(f"GU{k}", [128, 2, 512]) for k in range(2)]
        Y = ps("Y", [128, 2, 512])
        T = [ps(f"T{k}", [128, 512]) for k in range(2)]

        consts_in = sem("consts_in")
        w_in_ld = [sem(f"w_in_ld{k}") for k in range(2)]
        w_hi = sem("w_hi")
        w_lo = sem("w_lo")
        xs_zero = sem("xs_zero")
        acc_in = [sem(f"acc_in{i}") for i in range(2)]
        acc_out = [sem(f"acc_out{i}") for i in range(2)]
        xn_ready = sem("xn_ready")
        xs_hi = sem("xs_hi")
        xs_done = sem("xs_done")
        t_full = [sem(f"t_full{k}") for k in range(2)]
        t_free = [sem(f"t_free{k}") for k in range(2)]
        ex_done = sem("ex_done")
        gu_full = sem("gu_full")
        waited = sem("waited_f")
        silu_done = sem("silu_done")
        mul_done = sem("mul_done")
        hi_done = sem("hi_donef")
        lo_done = sem("lo_donef")
        y_full = sem("y_full")
        y_used = sem("y_used")
        dstep = sem("dstep")

        WSETUP = 2 * NE + 1

        def y_view(t):
            return Y[:, t // 2, (t % 2) * D:(t % 2 + 1) * D]

        block = ctx.enter_context(nc.Block())

        def rows_of(f):
            return h1[bass.ds(f * GT, GT), :].rearrange("(t p) d -> p t d", p=128)

        @block.sync
        def _(sp):
            for dst, src in ((wr32[:, :, :], w_router), (ebias[:, :, :], e_bias), (rank_sb[:, :, :], rank),
                             (eye32[:, :], eye)):
                sp.dma_start(dst, src).then_inc(consts_in, 16)
            for e in range(NE):
                if e >= 2:
                    sp.wait_ge(w_lo, 2 * (e - 1) + 1)
                sp.dma_start(wi32[e % 2][:, :, :], w_in[e, :, :, :]).then_inc(w_in_ld[e % 2], 16)
                sp.dma_start(wd32[e % 2][:, :, :], w_down[e, :, :, :]).then_inc(w_in_ld[e % 2], 16)
                if e < 2:
                    sp.dma_start(acc[e][:, :, :], rows_of(e)).then_inc(acc_in[e], 16)

            def turn(n, i, tail):
                sp.wait_ge(y_used, n * NE + NE + 1)
                if tail:
                    sp.dma_start(out[n * GT:n * GT + 256, :].rearrange("(t p) d -> p t d", p=128),
                                 acc[i][:, 0:2, :]).then_inc(acc_out[i], 16)
                    sp.dma_start(out[n * GT + 256:TOK, :], acc[i][0:TAIL - 256, 2, :])\
                      .then_inc(acc_out[i], 16)
                else:
                    sp.dma_start(out[bass.ds(n * GT, GT), :].rearrange("(t p) d -> p t d", p=128),
                                 acc[i][:, :, :]).then_inc(acc_out[i], 16)

            def reload(n, i, it):
                sp.wait_ge(acc_out[i], it * 16 + 16)
                sp.dma_start(acc[i][:, :, :], rows_of(n + 2)).then_inc(acc_in[i], 16)

            with sp.Fori(0, GROUPS // 2 - 1) as it:
                for i in range(2):
                    turn(it * 2 + i, i, False)
                    reload(it * 2 + i, i, it)
            last = GROUPS // 2 - 1
            turn(2 * last, 0, False)
            reload(2 * last, 0, last)
            turn(2 * last + 1, 1, False)
            turn(2 * last + 2, 0, True)
            sp.wait_ge(acc_out[0], 16 * (last + 1) + 32)
            sp.wait_ge(acc_out[1], 16 * (last + 1))

        @block.gpsimd
        def _(pool):
            pool.memset(xs[:, :, 3 * D:KS * 128], 0.0).then_inc(xs_zero, 1)

            def front(f):
                pool.wait_ge(xs_hi, f + 1)
                pool.sem_inc(waited, 1)
                pool.tensor_copy(xs[:, :, 2 * D:3 * D], xs[:, :, 0:D])
                pool.tensor_tensor(xs[:, :, D:2 * D], xn[:, :, :], xs[:, :, 0:D],
                                   ALU.subtract).then_inc(xs_done, 1)

            def group(n, i, nt, nxt):
                for k in range(JOBS):
                    e, j = divmod(k, KFF)
                    pool.wait_ge(hi_done, n * JOBS + k + 1)
                    pool.tensor_tensor(gl[(i + e) % 2][:, j, 0:nt], gu32[j][:, 0:nt],
                                       gh[(i + e) % 2][:, j, 0:nt], ALU.subtract).then_inc(lo_done, 1)
                    if k == 11 and nxt:
                        front(n + 1)

            pool.sem_inc(lo_done, 3)
            front(0)
            with pool.Fori(0, GROUPS // 2) as it:
                for i in range(2):
                    group(it * 2 + i, i, GT, True)
            group(GROUPS - 1, 0, TAIL, False)

        @block.tensor
        def _(pe):
            pe.wait_ge(xs_zero, 1)
            pe.wait_ge(w_lo, WSETUP)
            pe.wait_ge(w_hi, WSETUP + 1)
            pe.sem_inc(y_full, 2)

            def transposes(f):
                pe.wait_ge(xs_done, f + 1)
                for k, blocks in enumerate(((0, 1), (2, 3), (4,))):
                    pe.wait_ge(t_free[k % 2], f * 2 + k // 2 + 1)
                    v = T[k % 2][:, :].bitcast(F16)
                    for m, b in enumerate(blocks):
                        for t in range(TT):
                            last = pe.transpose(v[:, m * GT + t * 128:m * GT + (t + 1) * 128],
                                                xs[:, t, b * 128:(b + 1) * 128], eye16[:, :])
                    last.then_inc(t_full[k % 2], 1)

            def logits(f, i):
                pe.wait_ge(t_free[0], f * 2 + 3)
                pe.wait_ge(t_free[1], f * 2 + 2)
                for t in range(TT):
                    for b in range(KS):
                        last = pe.matmul(T[1][:, t * E:(t + 1) * E], xsT[i][:, b, t * 128:(t + 1) * 128],
                                         wr[:, b, :], start=(b == 0), stop=(b == KS - 1))
                last.then_inc(t_full[1], 1)

            def hidden(n, i, e, nt):
                for j in range(KFF):
                    k = e * KFF + j
                    s = (i + k) % 2
                    pe.wait_ge(mul_done, n * JOBS + k + 2)
                    for half in range(2):
                        for b in range(KS):
                            last = pe.matmul(GU[s][:, half, 0:nt],
                                             wi[:, e, b, half * FF + j * 128:half * FF + (j + 1) * 128],
                                             xsT[i][:, b, 0:nt], start=(b == 0), stop=(b == KS - 1))
                    last.then_inc(gu_full, 1)

            def down(n, i, e, nt):
                s = (i + e) % 2
                pe.wait_ge(lo_done, n * JOBS + e * KFF + KFF + 3)
                pe.wait_ge(y_used, n * NE + e + 1)
                parts = [(gh, 0), (gh, 1), (gl, 0)]
                for t in range(-(-nt // 128)):
                    rows = min(128, nt - t * 128)
                    for j in range(KFF):
                        for g, x in parts:
                            last = pe.matmul(y_view(t)[0:rows, :], g[s][:, j, t * 128:t * 128 + rows],
                                             wd[:, e, x, j, :], start=(j == 0 and (g, x) == parts[0]),
                                             stop=(j == KFF - 1 and (g, x) == parts[2]))
                last.then_inc(y_full, 1)

            def group(n, i, nt, nxt):
                for e in range(NE):
                    hidden(n, i, e, nt)
                    if e >= 1:
                        down(n, i, e - 1, nt)
                    if e == 5 and nxt:
                        transposes(n + 1)
                if nxt:
                    logits(n + 1, 1 - i)
                down(n, i, NE - 1, nt)

            transposes(0)
            logits(0, 0)
            with pe.Fori(0, GROUPS // 2) as it:
                for i in range(2):
                    group(it * 2 + i, i, GT, True)
            group(GROUPS - 1, 0, TAIL, False)

        @block.scalar
        def _(act):
            act.wait_ge(consts_in, 16 * 4)
            act.activation(eye16[:, :], eye32[:, :], ACT.Copy).then_inc(w_hi, 1)
            act.activation(wr[:, :, :], wr32[:, :, :], ACT.Copy).then_inc(w_hi, 1)
            for e in range(NE):
                act.wait_ge(w_in_ld[e % 2], 32 * (e // 2 + 1))
                act.activation(wi[:, e, :, :], wi32[e % 2][:, :, :], ACT.Copy).then_inc(w_hi, 1)
                act.activation(wd[:, e, 0, :, :], wd32[e % 2][:, :, :], ACT.Copy).then_inc(w_hi, 1)

            def front_hi(f):
                act.wait_ge(xn_ready, f + 1)
                act.activation(xs[:, :, 0:D], xn[:, :, :], ACT.Copy).then_inc(xs_hi, 1)

            def front_T(f, i):
                for k, blocks in enumerate(((0, 2), (2, 4), (4, 5))):
                    act.wait_ge(t_full[k % 2], f * 2 + k // 2 + 1)
                    w = blocks[1] - blocks[0]
                    src = T[k % 2][:, :].bitcast(F16)[:, 0:w * GT].rearrange("p (b n) -> p b n", b=w)
                    ins = act.activation(xsT[i][:, blocks[0]:blocks[1], :], src, ACT.Copy)
                    ins.then_inc(t_free[k % 2], 1)

            def front_exp(f):
                act.wait_ge(t_free[1], f * 2 + 3)
                act.activation(wide["lg"][:, :, :], wide["lg"][:, :, :], ACT.Exp).then_inc(ex_done, 1)

            def hi(n, i, k, nt):
                e, j = divmod(k, KFF)
                act.wait_ge(mul_done, n * JOBS + k + 4)
                if j == 0:
                    act.wait_ge(y_full, n * NE + e + 1)
                act.activation(gh[(i + e) % 2][:, j, 0:nt], gu32[j][:, 0:nt], ACT.Copy).then_inc(hi_done, 1)

            def group(n, i, nt, nxt):
                for k in range(JOBS):
                    j = k % KFF
                    act.wait_ge(gu_full, n * JOBS + k + 1)
                    act.wait_ge(mul_done, n * JOBS + k + 1)
                    act.activation(sg[j][:, 0:nt], GU[(i + k) % 2][:, 0, 0:nt], ACT.Silu)\
                       .then_inc(silu_done, 1)
                    if k:
                        hi(n, i, k - 1, nt)
                    if k == 10 and nxt:
                        front_hi(n + 1)
                    if k == 17 and nxt:
                        front_T(n + 1, 1 - i)
                hi(n, i, JOBS - 1, nt)
                if nxt:
                    front_exp(n + 1)

            front_hi(0)
            front_T(0, 0)
            front_exp(0)
            with act.Fori(0, GROUPS // 2) as it:
                for i in range(2):
                    group(it * 2 + i, i, GT, True)
            group(GROUPS - 1, 0, TAIL, False)

        @block.vector
        def _(dve):
            step = Steps(dve, dstep)
            dve.sem_inc(mul_done, 3)
            dve.sem_inc(y_used, 1)
            for k in range(2):
                dve.sem_inc(t_free[k], 1)
            dve.wait_ge(w_hi, 2)
            lo_rows = slice(3, KS)
            dve.tensor_tensor(wr[:, lo_rows, :], wr32[:, lo_rows, :], wr[:, lo_rows, :],
                              ALU.subtract).then_inc(w_lo, 1)
            for e in range(NE):
                dve.wait_ge(w_hi, 2 * e + 4)
                dve.tensor_tensor(wi[:, e, lo_rows, :], wi32[e % 2][:, lo_rows, :], wi[:, e, lo_rows, :],
                                  ALU.subtract).then_inc(w_lo, 1)
                dve.tensor_tensor(wd[:, e, 1, :, :], wd32[e % 2][:, :, :], wd[:, e, 0, :, :],
                                  ALU.subtract).then_inc(w_lo, 1)

            def norm(f, i, it):
                step.start(f * STEPS_F)
                dve.wait_ge(acc_in[i], it * 16 + 16)
                for t in range(TT):
                    ins = dve.bn_stats(stats[:, t, :], acc[i][:, t, :])
                step(ins)
                dve.sem_inc(waited, 1)
                for t in range(TT):
                    ins = dve.bn_aggr(mv[:, t, :], stats[:, t, :])
                step(ins)
                v, y, tm = (small[x][:, :] for x in ("var", "rstd", "tmp"))
                step(dve.tensor_scalar(v, mv[:, :, 1], LN_EPS, None, ALU.add))
                rsqrt(dve, step, y, v, tm)
                for t in range(TT):
                    ins = dve.tensor_scalar(xn[:, t, :], acc[i][:, t, :], mv[:, t, 0:1],
                                            small["rstd"][:, t:t + 1], ALU.subtract, ALU.mult)
                ins.then_inc(xn_ready, 1)

            def route(f, i):
                step.start(f * STEPS_F + 14)
                w = {n: t[:, :, :] for n, t in wide.items()}
                red = small["red"]
                one = red[:, :].unsqueeze(2).broadcast_to([128, TT, E])
                lg_psum = T[1][:, 0:TT * E].rearrange("p (t e) -> p t e", t=TT)
                dve.wait_ge(t_full[1], f * 2 + 2)
                step(dve.tensor_reduce(red[:, :], lg_psum, AX.X, ALU.max))
                ins = dve.tensor_tensor(w["lg"], lg_psum, one, ALU.subtract)
                ins.then_inc(t_free[1], 1)
                dve.wait_ge(ex_done, f + 1)
                step(dve.tensor_reduce(red[:, :], w["lg"], AX.X, ALU.add))
                step(dve.reciprocal(red[:, :], red[:, :]))
                step(dve.tensor_tensor(w["sc"], w["lg"], one, ALU.mult))
                step(dve.tensor_tensor(w["sel"], w["sc"], ebias[:, :, :], ALU.add))
                for name, src in (("oh1", "sel"), ("oh2", "sel2")):
                    if name == "oh2":
                        step(dve.scalar_tensor_tensor(w["sel2"], w["oh1"], -1e30, w["sel"],
                                                      ALU.mult, ALU.add))
                    step(dve.tensor_reduce(red[:, :], w[src], AX.X, ALU.max))
                    step(dve.tensor_tensor(w["eq"], w[src], one, ALU.is_equal))
                    step(dve.tensor_tensor(w["eq"], w["eq"], rank_sb[:, :, :], ALU.mult))
                    step(dve.tensor_reduce(red[:, :], w["eq"], AX.X, ALU.max))
                    step(dve.tensor_tensor(w[name], w["eq"], one, ALU.is_equal))
                step(dve.tensor_tensor(w["eq"], w["oh1"], w["oh2"], ALU.add))
                step(dve.tensor_tensor(w["eq"], w["eq"], w["sc"], ALU.mult))
                step(dve.tensor_reduce(red[:, :], w["eq"], AX.X, ALU.add))
                step(dve.tensor_scalar(red[:, :], red[:, :], 1e-9, None, ALU.add))
                step(dve.reciprocal(red[:, :], red[:, :]))
                step(dve.tensor_tensor(comb[i][:, :, :], w["eq"], one, ALU.mult))
                assert step.n == STEPS_F - 14, step.n

            def add_expert(n, i, e, nt):
                dve.wait_ge(y_full, n * NE + e + 3)
                for t in range(-(-nt // 128)):
                    r = min(128, nt - t * 128)
                    a = acc[i][0:r, t, :]
                    if e == 0:
                        ins = dve.tensor_tensor(a, y_view(t)[0:r, :], a, ALU.add)
                    else:
                        ins = dve.scalar_tensor_tensor(a, y_view(t)[0:r, :], comb[i][0:r, t, e - 1:e], a,
                                                       ALU.mult, ALU.add)
                ins.then_inc(y_used, 1)
                if e < NE - 1:
                    dve.wait_ge(y_used, n * NE + e + 2)

            def group(n, i, nt, nxt, it):
                for k in range(JOBS):
                    e, j = divmod(k, KFF)
                    dve.wait_ge(silu_done, n * JOBS + k + 1)
                    dve.wait_ge(lo_done, n * JOBS + k + 1)
                    dve.tensor_tensor(gu32[j][:, 0:nt], GU[(i + k) % 2][:, 1, 0:nt], sg[j][:, 0:nt],
                                      ALU.mult).then_inc(mul_done, 1)
                    if k == 5 and nxt:
                        norm(n + 1, 1 - i, it + i)
                    if j == KFF - 1 and e >= 1:
                        add_expert(n, i, e - 1, nt)
                if nxt:
                    route(n + 1, 1 - i)
                add_expert(n, i, NE - 1, nt)

            norm(0, 0, 0)
            route(0, 0)
            with dve.Fori(0, GROUPS // 2) as it:
                for i in range(2):
                    group(it * 2 + i, i, GT, True, it)
            group(GROUPS - 1, 0, TAIL, False, GROUPS // 2)


def build(nc, xT, w_tok, addend, pos, w_qkv, w_proj, w_in, w_down, w_router, e_bias, eye, key_mask, rank,
          out):
    h1 = nc.dram_tensor("h1_scratch", (GROUPS * GT, D), F32, kind="Internal").ap()
    with ExitStack() as sems:
        attention_phase(nc, sems, xT, w_tok, addend, pos, w_qkv, w_proj, eye, key_mask, h1)
        feed_forward_phase(nc, sems, h1, w_in, w_down, w_router, e_bias, eye, rank, out)


def lay_out(inputs):
    import numpy as np

    def a(name):
        return np.ascontiguousarray(inputs[name])

    x = a("x").reshape(B, CH, SIDE, P, SIDE, P).transpose(0, 1, 3, 5, 2, 4).reshape(B, KF, 128, SEQ - 1)
    xT = np.zeros((B, 128, KF, SEQ), np.float32)
    xT[..., 1:] = x.transpose(0, 2, 1, 3)
    tiles = np.stack([np.arange(TR), np.arange(TR) + HALF], 1)
    w_tok = a("L0_tok_W").reshape(KF, 128, D).transpose(1, 0, 2).reshape(128, KF * D)
    addend = np.broadcast_to(a("L0_tok_b"), (TR, 2, D)).copy()
    addend[0, 0] = a("L0_tok_class_token").reshape(D)
    pos = a("L0_tok_pos_table")[tiles]

    def with_bias(w, b):
        r = np.zeros((DC + 1, 2, w.shape[0]), np.float32)
        r[:DC] = w.T.reshape(2, DC, -1).transpose(1, 0, 2)
        r[DC, 0] = b
        return r

    def stacked(w):
        r = np.zeros(w.shape[:-2] + (KS * 128, w.shape[-1]), np.float32)
        for k in range(3):
            r[..., k * D:(k + 1) * D, :] = w
        return np.moveaxis(r.reshape(w.shape[:-2] + (KS, 128, w.shape[-1])), -3, -2)

    gate = np.concatenate([a("L0_ffn_sg")[None], a("L0_ffn_Wg")])
    up = np.concatenate([a("L0_ffn_su")[None], a("L0_ffn_Wu")])
    down = np.concatenate([a("L0_ffn_sd")[None], a("L0_ffn_Wd")])
    w_in = stacked(np.concatenate([gate, up], 1).transpose(0, 2, 1))
    w_down = down.transpose(0, 2, 1).reshape(NE, KFF, 128, D).transpose(0, 2, 1, 3)
    mask = np.ones((TR, 2), np.float32)
    mask[0, 1] = 0.0
    return {
        "xT": xT, "w_tok": w_tok, "addend": addend, "pos": pos,
        "w_qkv": with_bias(a("L0_attn_qkv_w"), a("L0_attn_qkv_b")),
        "w_proj": with_bias(a("L0_attn_proj_w"), a("L0_attn_proj_b")),
        "w_in": w_in, "w_down": w_down, "w_router": stacked(a("L0_ffn_w_router").T),
        "e_bias": np.broadcast_to(a("L0_ffn_expert_bias"), (128, TT, E)),
        "eye": np.eye(128, dtype=np.float32), "key_mask": mask,
        "rank": np.broadcast_to(np.arange(E, 0, -1, dtype=np.float32), (128, TT, E)),
    }


def kernel(**inputs):
    import numpy as np
    import concourse.bacc as bacc
    from concourse.bass_utils import run_bass_kernel_spmd

    nc = bacc.Bacc("TRN2", target_bir_lowering=False, num_devices=1)
    arrays, args = {}, []
    for name, value in lay_out(inputs).items():
        value = np.ascontiguousarray(value)
        arrays[f"in_{name}"] = value
        args.append(nc.dram_tensor(f"in_{name}", value.shape, mybir.dt.from_np(value.dtype),
                                   kind="ExternalInput").ap())
    out = nc.dram_tensor("out", (TOK, D), F32, kind="ExternalOutput").ap()
    build(nc, *args, out)
    result = run_bass_kernel_spmd(nc, [arrays], core_ids=[0])
    return result.results[0]["out"].reshape(B, SEQ, D)
```

```python
from contextlib import ExitStack

import concourse.bass as bass
from concourse import mybir

F32 = mybir.dt.float32
F16 = mybir.dt.float16
I32 = mybir.dt.int32
ALU = mybir.AluOpType
ACT = mybir.ActivationFunctionType
AX = mybir.AxisListType

B, CH, IMG, P = 64, 3, 224, 16
D = 192
SIDE = IMG // P
SEQ = SIDE * SIDE + 1
FEAT = CH * P * P
KF = FEAT // 128
HEADS, HD = 12, 16
E, FF = 8, 384
DC = D // 2
HALF = 98
TR = SEQ - HALF
SP = SEQ + 1
QUAD = 32
SLOT = 64
NG = HEADS // 2
IMAGES = 3
TURNS = (B - 4) // IMAGES
ATT_SCALE, SIM_SCALE = HD ** -0.5, 10.0
NORM_EPS2, LN_EPS = 1e-24, 1e-5
RSQRT_MAGIC = 1597463007.0

TOK = B * SEQ
GT = 512
NT = GT // 128
GROUPS = -(-TOK // GT)
PAD = GROUPS * GT - TOK
TAIL = TOK - (GROUPS - 1) * GT
KFF = FF // 128


class Turn:

    def __init__(self, part, it=0):
        self.part, self.it = part, it

    def count(self, per, at):
        if self.part == "pro":
            return at
        if self.part == "body":
            return self.it * per["body"] + (per["pro"] + at)
        return per["pro"] + TURNS * per["body"] + at


class Ring:

    def __init__(self, full, free, order, parts, freeing=None):
        self.full, self.free, n = full, free, len(full)
        self.slots = {task: k % n for k, task in enumerate(order)}
        self.freeing = set(order if freeing is None else freeing)
        self.users = [[t for t in order if self.slots[t] == s] for s in range(n)]
        self.uses, self.frees = [{} for _ in range(n)], [{} for _ in range(n)]
        self.filled_by, self.freed_by, self.prior = {}, {}, {}
        for part, listed in parts.items():
            for s in range(n):
                fills = frees = 0
                before = None if part == "pro" else (self.users[s][-1], None)
                for task, m in listed:
                    if self.slots.get(task) == s:
                        self.filled_by[part, task, m], self.freed_by[part, task, m] = fills, frees
                        self.prior[part, task, m] = before
                        before = (task, m)
                        fills += 1
                        frees += task in self.freeing
                self.uses[s][part], self.frees[s][part] = fills, frees

    def slot(self, task):
        return self.slots[task]

    def place(self, counted, users, tn, job):
        task, m = job
        if m is not None and (tn.part, task, m) in counted:
            return counted[tn.part, task, m]
        return users.index(task) - len(users)

    def fills(self, tn, job):
        s = self.slots[job[0]]
        return tn.count(self.uses[s], self.place(self.filled_by, self.users[s], tn, job) + 1)

    def frees_by(self, tn, job, extra):
        s = self.slots[job[0]]
        users = [t for t in self.users[s] if t in self.freeing]
        return tn.count(self.frees[s], self.place(self.freed_by, users, tn, job) + extra)

    def before(self, tn, job):
        return self.prior[(tn.part,) + job]

    def wait_free(self, eng, job, tn):
        eng.wait_ge(self.free[self.slots[job[0]]], self.frees_by(tn, job, 1))

    def wait_freed(self, eng, job, tn):
        eng.wait_ge(self.free[self.slots[job[0]]], self.frees_by(tn, job, 2))

    def wait_full(self, eng, job, tn):
        eng.wait_ge(self.full[self.slots[job[0]]], self.fills(tn, job))

    def filled(self, ins, job):
        ins.then_inc(self.full[self.slots[job[0]]], 1)

    def freed(self, ins, job):
        ins.then_inc(self.free[self.slots[job[0]]], 1)


class Steps:

    def __init__(self, eng, sem):
        self.eng, self.sem, self.base, self.n = eng, sem, 0, 0

    def __call__(self, ins):
        ins.then_inc(self.sem, 1)
        self.n += 1
        self.eng.wait_ge(self.sem, self.base + self.n)

    def start(self, base):
        self.base, self.n = base, 0


def rsqrt(dve, step, y, v, tmp):
    step(dve.tensor_scalar(y.bitcast(I32), v.bitcast(I32), 1, None, ALU.logical_shift_right))
    step(dve.tensor_scalar(y.bitcast(I32), y.bitcast(I32), -1.0, RSQRT_MAGIC, ALU.mult, ALU.add))
    for _ in range(3):
        step(dve.scalar_tensor_tensor(tmp, y, -0.5, y, ALU.mult, ALU.mult))
        step(dve.tensor_tensor(tmp, tmp, v, ALU.mult))
        step(dve.scalar_tensor_tensor(y, tmp, 1.5, y, ALU.add, ALU.mult))


def attention_phase(nc, sems, xT, w_tok, addend, pos, w_qkv, w_proj, eye, key_mask, h1):
    with ExitStack() as ctx:
        def sb(name, shape, dt=F32):
            return ctx.enter_context(nc.sbuf_tensor(name, shape, dt))

        def ps(name, shape, dt=F32):
            return ctx.enter_context(nc.psum_tensor(name, shape, dt))

        def sem(name):
            return sems.enter_context(nc.semaphore(name))

        wt32 = sb("wt32", [128, KF * D])
        wt = sb("wt", [128, 2, KF, D], F16)
        wq32 = sb("wq32", [DC + 1, 2, 3 * D])
        wq = sb("wq", [DC + 1, 2, 2, 3 * D], F16)
        wp32 = sb("wp32", [DC + 1, 2, D])
        wp = sb("wp", [DC + 1, 2, 2, D], F16)
        base = sb("base", [TR, 2, D])
        pos_sb = sb("pos_sb", [TR, 2, D])
        eye32 = sb("eye32", [128, 128])
        eye16 = sb("eye16", [128, 128], F16)
        mask = sb("mask", [TR, 2])
        xt = [sb(f"xt{i}", [128, KF, SEQ]) for i in range(IMAGES)]
        xh = [sb(f"xh{i}", [128, KF, SEQ], F16) for i in range(IMAGES)]
        xl = [sb(f"xl{i}", [128, KF, SEQ], F16) for i in range(IMAGES)]
        h = [sb(f"h{i}", [TR, 2, D]) for i in range(IMAGES)]
        xn = [sb(f"xn{i}", [TR, 2, D]) for i in range(IMAGES)]
        th = [sb(f"th{i}", [DC + 1, 2, SEQ], F16) for i in range(IMAGES)]
        tl = [sb(f"tl{i}", [DC + 1, 2, SEQ], F16) for i in range(IMAGES)]
        st = [sb(f"st{i}", [TR, 2, 2, HEADS, SLOT], F16) for i in range(IMAGES)]
        lT = [sb(f"lT{i}", [128, NG, SP], F16) for i in range(IMAGES)]
        mT = [sb(f"mT{i}", [128, NG, SP], F16) for i in range(IMAGES)]
        rT = [sb(f"rT{i}", [128, NG, SP], F16) for i in range(IMAGES)]
        va = [sb(f"va{i}", [TR, 2, HEADS, QUAD]) for i in range(IMAGES)]
        pvs = [sb(f"pvs{i}", [128, HEADS // 4, SEQ]) for i in range(IMAGES)]
        out = [sb(f"out{i}", [TR, 2, D]) for i in range(IMAGES)]
        probs = [sb(f"probs{k}", [TR, 2, 2 * SEQ]) for k in range(3)]
        stats = sb("stats", [TR, 2, 6])
        mv = sb("mv", [TR, 2, 2])
        var = sb("var", [TR, 2 * HEADS])
        rstd = sb("rstd", [TR, 2 * HEADS])
        tmp = sb("tmp", [TR, 2 * HEADS])
        den = {n: sb(f"den_{n}", [TR, 2, HEADS]) for n in ("att", "sim")}
        sq = sb("sq", [TR, 2, D])
        sn = sb("sn", [TR, 2, D])
        mark = sb("mark", [1, 1])
        zrow = sb("zrow", [PAD // 2, 2 * D])

        bank = [ps(f"bank{k}", [128, 512]) for k in range(2)]
        score = [ps(f"score{k}", [128, 2, 512]) for k in range(2)]
        pv = [ps(f"pv{k}", [128, 512]) for k in range(2)]

        weights_in = sem("weights_in")
        consts_done = sem("consts_done")
        act_setup = sem("act_setup")
        x_in = [sem(f"x_in{i}") for i in range(IMAGES)]
        x_split = sem("x_split")
        x_hi = sem("x_hi")
        hi_T = {n: sem(f"hi_T_{n}") for n in ("tok", "att", "sim")}
        xn_done = {n: sem(f"xn_{n}") for n in ("tok", "att", "sim")}
        hi_qk = sem("hi_qk")
        sq_done = sem("sq_done")
        hi_sn = sem("hi_sn")
        lo_sn = sem("lo_sn")
        h_done = sem("h_done")
        waited = sem("waited")
        exp_done = sem("exp_done")
        stored = [sem(f"stored{i}") for i in range(IMAGES)]
        pad_in = sem("pad_in")
        dve_step = sem("dve_step")
        bank_full = [sem(f"bank_full{k}") for k in range(2)]
        bank_free = [sem(f"bank_free{k}") for k in range(2)]
        score_full = [sem(f"score_full{k}") for k in range(2)]
        score_free = [sem(f"score_free{k}") for k in range(2)]
        prob_full = [sem(f"prob_full{k}") for k in range(3)]
        prob_free = [sem(f"prob_free{k}") for k in range(3)]
        pv_full = [sem(f"pv_full{k}") for k in range(2)]
        pv_free = [sem(f"pv_free{k}") for k in range(2)]

        FRONT = {"tokens", "xnT", "qk0", "qk1", "v"}
        FRONT |= {f"stack{x}{k}" for x in "LRM" for k in range(2)} | {f"rm{u}" for u in range(NG)}
        SIM = {f"stack{x}{k}" for x in "AB" for k in range(2)} | {"divS"}
        SIM |= {f"{kind}{u}" for kind in ("sis", "si", "siv", "sip") for u in range(NG)}
        BACK = {"finT", "fin"}
        DENSE_N = 512
        DENSE = {"atv0": 1, "atv2": 1, "atv4": 1, "siv0": 1, "siv2": 1, "siv4": 1, "xnT": 3, "stackA0": 4,
                 "stackM0": 2, "proj": 1, "projT": 1}
        PE_ORDER = (
            "stackA0 ats0 stackB0 ats1 finT stackB1 stackA1 fin atv0 sis0 sis1 tokens atv1 ats2 "
            "siv0 siv1 ats3 ats4 atv2 atv3 ats5 atv4 xnT sis2 sis3 atv5 qk0 qk1 sis4 sis5 siv2 "
            "stackR0 stackL0 stackL1 stackR1 divA rm0 rm1 projT siv3 rm2 siv4 rm3 proj rm4 rm5 v "
            "siv5 stackM0 stackM1 divS").split()
        ACT_ORDER = (
            "stackA0 stackB0 finT stackB1 at0 stackA1 at1 si0 si1 atp0 at2 at3 at4 sip0 at5 xnT si2 "
            "atp1 si3 qk0 qk1 si4 si5 stackR0 stackL0 atp2 stackL1 stackR1 projT sip1 projsq sip2 v "
            "proj stackM0 stackM1").split()
        DVE_ORDER = (
            "finT si0 si1 fin tokens xnT si2 si3 qk0 qk1 si4 si5 divA rm0 rm1 projT rm2 rm3 rm4 "
            "proj rm5 projlo divS").split()

        def listed(order):
            def steps(cs):
                found = []
                for c in cs:
                    for s in order:
                        m = c + (1 if s in FRONT else -1 if s in SIM else -2 if s in BACK else 0)
                        if 0 <= m < B:
                            found.append((s, m))
                return found
            return {"pro": steps((-1, 0, 1)), "body": steps((2, 3, 4)), "epi": steps((B - 2, B - 1, B, B + 1))}

        def walk(eng, order, do):
            parts = listed(order)
            for s, m in parts["pro"]:
                do(Turn("pro"), s, m, m % IMAGES, m // IMAGES, (s, m))
            with eng.Fori(0, TURNS) as it:
                for s, c in parts["body"]:
                    do(Turn("body", it), s, it * IMAGES + c, c % IMAGES, it + c // IMAGES, (s, c))
            for s, m in parts["epi"]:
                do(Turn("epi"), s, m, m % IMAGES, m // IMAGES, (s, m))

        def ring(full, free, order, takes, freeing=None):
            chosen = [s for s in order if s in takes]
            return Ring(full, free, chosen, listed(order), freeing)

        units = range(NG)
        banks = ring(bank_full, bank_free, PE_ORDER,
                     FRONT - {f"rm{u}" for u in units} | {"projT", "proj"} | BACK | SIM & set(
                         f"stack{x}{k}" for x in "AB" for k in range(2)))
        own = {f"rm{u}" for u in units} | {"divA", "divS"}
        scores = ring(score_full, score_free, PE_ORDER,
                      own | {f"{kind}s{u}" for kind in ("at", "si") for u in units}, freeing=own)
        probr = ring(prob_full, prob_free, ACT_ORDER, {f"{kind}{u}" for kind in ("at", "si") for u in units})
        pvr = ring(pv_full, pv_free, PE_ORDER, {f"{kind}v{2 * g}" for kind in ("at", "si") for g in range(3)})

        def cols(t):
            return slice(HALF * t, HALF * t + TR)

        def tok_view(b):
            return b[0:TR, 0:2 * D].rearrange("p (t d) -> p t d", t=2)

        def xT_view(b):
            return b[0:DC, 0:2 * SEQ].rearrange("p (c n) -> p c n", c=2)

        def stack_view(b):
            return b[:, :].bitcast(F16)[:, 0:3 * SP].rearrange("p (g n) -> p g n", g=3)

        def sums_view(k):
            return score[k][0:TR, :, 0:HEADS * QUAD].rearrange("p t (h d) -> p t h d", h=HEADS)

        def score_view(k):
            return score[k][0:TR, :, 0:2 * SEQ]

        block = ctx.enter_context(nc.Block())

        @block.sync
        def _(sp):
            for dst, src in ((wt32[:, :], w_tok), (wq32[:, :, :], w_qkv), (wp32[:, :, :], w_proj),
                             (base[:, :, :], addend), (pos_sb[:, :, :], pos), (eye32[:, :], eye),
                             (mask[:, :], key_mask)):
                sp.dma_start(dst, src).then_inc(weights_in, 16)
            sp.wait_ge(consts_done, 1)
            sp.dma_start(h1[TOK:TOK + PAD, :].rearrange("(p a) d -> p (a d)", a=2), zrow[:, :]).then_inc(pad_in, 16)

            def load(n, i):
                sp.wait_ge(x_split, n + 1)
                sp.dma_start(xt[i][:, :, :], xT[n, :, :, :]).then_inc(x_in[i], 16)

            def store(tn, m, i, job):
                banks.wait_freed(sp, job, tn)
                sp.dma_start(h1[bass.ds(m * SEQ, TR), :], out[i][:, 0, :]).then_inc(stored[i], 16)
                sp.dma_start(h1[bass.ds(m * SEQ + TR, TR - 1), :],
                             out[i][1:TR, 1, :]).then_inc(stored[i], 16)

            for n in range(4):
                load(n, n % IMAGES)
            with sp.Fori(0, TURNS) as it:
                for c in (2, 3, 4):
                    store(Turn("body", it), it * IMAGES + (c - 2), (c - 2) % IMAGES, ("fin", c - 2))
                    load(it * IMAGES + (c + 2), (c + 2) % IMAGES)
            for m in range(B - 4, B):
                store(Turn("epi"), m, m % IMAGES, ("fin", m))
            for i in range(IMAGES):
                sp.wait_ge(stored[i], 32 * len(range(i, B, IMAGES)) + 32)
            sp.wait_ge(pad_in, 16)

        @block.gpsimd
        def _(pool):
            for i in range(IMAGES):
                pool.memset(st[i][:, :, :, :, :], 0.0)
                pool.memset(va[i][:, :, :, :], 0.0)
            pool.memset(zrow[:, :], 0.0).then_inc(consts_done, 1)
            pool.wait_ge(consts_done, 1)
            for i in range(IMAGES):
                last = pool.memset(st[i][:, :, 1, :, 48:49], 1.0)
            last.then_inc(consts_done, 1)
            pool.wait_ge(consts_done, 2)
            pool.wait_ge(act_setup, 1)
            pool.sem_inc(x_split, IMAGES)

            def split(m, i, turn):
                pool.wait_ge(x_in[i], turn * 16 + 16)
                pool.wait_ge(h_done, m + 1)
                pool.sem_inc(waited, 1)
                pool.tensor_copy(xh[i][:, :, :], xt[i][:, :, :]).then_inc(x_hi, 1)
                pool.wait_ge(x_hi, m + 1)
                pool.tensor_tensor(xl[i][:, :, :], xt[i][:, :, :], xh[i][:, :, :],
                                   ALU.subtract).then_inc(x_split, 1)

            with pool.Fori(0, B // IMAGES) as it:
                for i in range(IMAGES):
                    split(it * IMAGES + i, i, it)
            for m in range(B - B % IMAGES, B):
                split(m, m % IMAGES, m // IMAGES)

        @block.tensor
        def _(pe):
            pe.wait_ge(consts_done, 2)
            pe.wait_ge(act_setup, 1)
            pe.wait_ge(dve_step, 4)
            for k in range(3):
                pe.sem_inc(prob_free[k], 1)

            def hold_clock(task, buffer):
                for _ in range(DENSE.get(task, 0)):
                    pe.matmul(buffer[:, 0:DENSE_N], wt[:, 0, 0, 0:128], dense, start=True, stop=True)

            dense = wt[:, 0, :, :].rearrange("p k d -> p (k d)")[:, 0:DENSE_N]

            def transposed(job, name, i, m, tn):
                banks.wait_free(pe, job, tn)
                hold_clock(job[0], bank[banks.slot(job[0])])
                pe.wait_ge(xn_done[name], m + 1)
                for t in range(2):
                    for c in range(2):
                        last = pe.transpose(xT_view(bank[banks.slot(job[0])])[:, c, cols(t)],
                                            xn[i][:, t, c * DC:(c + 1) * DC], eye32[0:TR, 0:TR])
                banks.filled(last, job)

            def product(dst, w, i, t, lo, hi):
                parts = [(th, 0), (th, 1), (tl, 0)]
                for c in range(2):
                    rows = DC + 1 if c == 0 else DC
                    for a, x in parts:
                        last = pe.matmul(dst, a[i][0:rows, c, cols(t)], w[0:rows, x, c, lo:hi],
                                         start=(c == 0 and (a, x) == parts[0]),
                                         stop=(c == 1 and (a, x) == parts[2]))
                return last

            def stack_T(job, i, side, tn):
                half = int(job[0][-1])
                for t in range(2):
                    src = st[i][:, t, side, :, :].rearrange("p (g x) s -> p g (x s)", g=NG)
                    for g in range(3):
                        last = pe.transpose(stack_view(bank[banks.slot(job[0])])[:, g, cols(t)],
                                            src[:, 3 * half + g, :], eye16[0:TR, 0:TR])
                banks.filled(last, job)

            def four_heads(job, tn, stationary, moving, rows_n):
                gp, t = divmod(int(job[0][-1]), 2)
                k = scores.slot(job[0])
                last_job = scores.before(tn, job)
                if last_job and last_job[0] not in scores.freeing:
                    probr.wait_full(pe, (last_job[0][:2] + last_job[0][-1], last_job[1]), tn)
                else:
                    scores.wait_free(pe, job, tn)
                for gg in range(2):
                    for j in range(2):
                        rows = slice(SLOT * j, SLOT * j + rows_n)
                        g = 2 * gp + gg
                        last = pe.matmul(score_view(k)[:, j, gg * SEQ:(gg + 1) * SEQ],
                                         stationary[rows, g, cols(t)], moving[rows, g, 0:SEQ],
                                         start=True, stop=True)
                scores.filled(last, job)

            def values(kind, i, u, m, tn):
                gp, kt = divmod(u, 2)
                job, sums = (f"{kind}{u}", m), (f"{kind}v{2 * gp}", m)
                k, b = probr.slot(job[0]), pvr.slot(sums[0])
                if kt == 0:
                    pvr.wait_free(pe, sums, tn)
                    hold_clock(f"{kind}v{u}", pv[b])
                probr.wait_full(pe, job, tn)
                for q in range(4):
                    gg, j = divmod(q, 2)
                    last = pe.matmul(pv[b][QUAD * q:QUAD * (q + 1), 0:SEQ], va[i][:, kt, 4 * gp + q, :],
                                     probs[k][:, j, gg * SEQ:(gg + 1) * SEQ],
                                     start=(kt == 0), stop=(kt == 1))
                probr.freed(last, job)

            def do(tn, s, m, i, turn, job):
                n = job[1]
                if s == "tokens":
                    pe.wait_ge(x_split, m + 4)
                    banks.wait_free(pe, job, tn)
                    parts = [(xh, 0), (xh, 1), (xl, 0)]
                    for t in range(2):
                        for k in range(KF):
                            for a, x in parts:
                                last = pe.matmul(tok_view(bank[banks.slot(s)])[:, t, :], a[i][:, k, cols(t)],
                                                 wt[:, x, k, :], start=(k == 0 and (a, x) == parts[0]),
                                                 stop=(k == KF - 1 and (a, x) == parts[2]))
                    banks.filled(last, job)
                elif s == "xnT":
                    transposed(job, "tok", i, m, tn)
                elif s in ("qk0", "qk1"):
                    banks.wait_free(pe, job, tn)
                    hold_clock(s, bank[banks.slot(s)])
                    banks.wait_freed(pe, ("xnT", n), tn)
                    banks.filled(product(bank[banks.slot(s)][0:TR, 0:2 * D], wq, i, int(s[2]), 0, 2 * D), job)
                elif s == "v":
                    banks.wait_freed(pe, ("xnT", n), tn)
                    banks.wait_free(pe, job, tn)
                    for t in range(2):
                        last = product(tok_view(bank[banks.slot(s)])[:, t, :], wq, i, t, 2 * D, 3 * D)
                    banks.filled(last, job)
                elif s[:-1] in ("stackL", "stackR"):
                    banks.wait_free(pe, job, tn)
                    hold_clock(s, bank[banks.slot(s)])
                    banks.wait_freed(pe, ("qk0", n), tn)
                    banks.wait_freed(pe, ("qk1", n), tn)
                    stack_T(job, i, 0 if s[5] == "L" else 1, tn)
                elif s[:-1] == "stackM":
                    banks.wait_free(pe, job, tn)
                    hold_clock(s, bank[banks.slot(s)])
                    scores.wait_freed(pe, ("rm4", n), tn)
                    scores.wait_freed(pe, ("rm5", n), tn)
                    stack_T(job, i, 0, tn)
                elif s[:-1] in ("stackA", "stackB"):
                    banks.wait_free(pe, job, tn)
                    hold_clock(s, bank[banks.slot(s)])
                    pe.wait_ge(lo_sn, m + 1)
                    stack_T(job, i, 0 if s[5] == "A" else 1, tn)
                elif s[:-1] == "rm":
                    if s == "rm0":
                        for x in ("L0", "L1", "R0", "R1"):
                            banks.wait_freed(pe, ("stack" + x, n), tn)
                    four_heads(job, tn, lT[i], rT[i], 48)
                elif s[:-1] == "ats":
                    if s == "ats0":
                        for x in ("stackM0", "stackM1", "v"):
                            banks.wait_freed(pe, (x, n), tn)
                    four_heads(job, tn, rT[i], mT[i], SLOT)
                elif s[:-1] == "sis":
                    if s == "sis0":
                        for x in ("A0", "A1", "B0", "B1"):
                            banks.wait_freed(pe, ("stack" + x, n), tn)
                    four_heads(job, tn, rT[i], lT[i], 48)
                elif s[:-1] in ("atv", "siv"):
                    values(s[:2], i, int(s[3]), n, tn)
                elif s in ("divA", "divS"):
                    kind = "at" if s == "divA" else "si"
                    for g in range(3):
                        pvr.wait_freed(pe, (f"{kind}v{2 * g}", n), tn)
                    k = scores.slot(s)
                    last_job = scores.before(tn, job)
                    if last_job and last_job[0] not in scores.freeing:
                        probr.wait_full(pe, (last_job[0][:2] + last_job[0][-1], last_job[1]), tn)
                    else:
                        scores.wait_free(pe, job, tn)
                    for t in range(2):
                        for gp in range(3):
                            last = pe.transpose(score[k][0:TR, t, gp * 128:(gp + 1) * 128],
                                                pvs[i][:, gp, cols(t)], eye32[:, :])
                    scores.filled(last, job)
                elif s in ("projT", "finT"):
                    transposed(job, "att" if s == "projT" else "sim", i, m, tn)
                elif s in ("proj", "fin"):
                    banks.wait_free(pe, job, tn)
                    hold_clock(s, bank[banks.slot(s)])
                    banks.wait_freed(pe, (s + "T", n), tn)
                    for t in range(2):
                        last = product(tok_view(bank[banks.slot(s)])[:, t, :], wp, i, t, 0, D)
                    banks.filled(last, job)

            walk(pe, PE_ORDER, do)

        @block.scalar
        def _(act):
            act.wait_ge(weights_in, 16 * 7)
            act.wait_ge(consts_done, 1)
            act.activation(wt[:, 0, :, :].rearrange("p k d -> p (k d)"), wt32[:, :], ACT.Copy)
            act.activation(wq[:, 0, :, :], wq32[:, :, :], ACT.Copy)
            act.activation(wp[:, 0, :, :], wp32[:, :, :], ACT.Copy)
            for i in range(IMAGES):
                for t in range(2):
                    act.activation(va[i][:, t, :, HD], eye32[0:TR, 0:HEADS], ACT.Identity,
                                   bias=mask[:, t:t + 1], scale=0.0)
            act.activation(eye16[:, :], eye32[:, :], ACT.Copy).then_inc(act_setup, 1)

            def hi_half(job, name, i, tn):
                banks.wait_full(act, job, tn)
                act.activation(th[i][0:DC, :, :], xT_view(bank[banks.slot(job[0])]), ACT.Copy)\
                   .then_inc(hi_T[name], 1)

            STACKS = {"L": lT, "A": lT, "R": rT, "B": rT, "M": mT}

            def do(tn, s, m, i, turn, job):
                n = job[1]
                if s == "xnT":
                    hi_half(job, "tok", i, tn)
                elif s in ("qk0", "qk1"):
                    banks.wait_full(act, job, tn)
                    src = bank[banks.slot(s)][0:TR, 0:2 * D]
                    act.activation(st[i][:, int(s[2]), :, :, 0:HD],
                                   src.rearrange("p (s h d) -> p s h d", s=2, h=HEADS),
                                   ACT.Copy).then_inc(hi_qk, 1)
                elif s == "v":
                    banks.wait_full(act, job, tn)
                    src = tok_view(bank[banks.slot(s)])
                    for t in range(2):
                        ins = act.activation(va[i][:, t, :, 0:HD],
                                             src[:, t, :].rearrange("p (h d) -> p h d", h=HEADS),
                                             ACT.Copy, scale=mask[:, t:t + 1])
                    banks.freed(ins, job)
                elif s[:5] == "stack":
                    half = int(s[-1])
                    banks.wait_full(act, job, tn)
                    ins = act.activation(STACKS[s[5]][i][:, 3 * half:3 * half + 3, 0:SEQ],
                                         stack_view(bank[banks.slot(s)])[:, :, 0:SEQ], ACT.Copy)
                    banks.freed(ins, job)
                elif s[:-1] in ("at", "si"):
                    kind, u = s[:2], s[2]
                    score_job = (f"{kind}s{u}", n)
                    scores.wait_full(act, score_job, tn)
                    probr.wait_free(act, job, tn)
                    ins = act.activation(probs[probr.slot(s)][:, :, :], score_view(scores.slot(score_job[0])),
                                         ACT.Exp, scale=ATT_SCALE if kind == "at" else SIM_SCALE)
                    if kind == "at":
                        probr.filled(ins, job)
                    else:
                        ins.then_inc(exp_done, 1)
                elif s[:-1] in ("atp", "sip"):
                    kind, g = s[:2], int(s[3])
                    sums = (f"{kind}v{2 * g}", n)
                    probr.wait_freed(act, (f"{kind}{2 * g + 1}", n), tn)
                    ins = act.activation(pvs[i][:, g, :], pv[pvr.slot(sums[0])][:, 0:SEQ], ACT.Copy)
                    pvr.freed(ins, sums)
                elif s in ("projT", "finT"):
                    hi_half(job, "att" if s == "projT" else "sim", i, tn)
                elif s == "projsq":
                    banks.wait_full(act, ("proj", n), tn)
                    act.activation(sq[:, :, :], tok_view(bank[banks.slot("proj")]), ACT.Square)\
                       .then_inc(sq_done, 1)
                elif s == "proj":
                    banks.wait_freed(act, job, tn)
                    for side in range(2):
                        ins = act.activation(st[i][:, :, side, :, 0:HD],
                                             sn[:, :, :].rearrange("p t (h d) -> p t h d", h=HEADS),
                                             ACT.Copy)
                    ins.then_inc(hi_sn, 1)

            walk(act, ACT_ORDER, do)

        @block.vector
        def _(dve):
            step = Steps(dve, dve_step)
            dve.wait_ge(act_setup, 1)
            dve.wait_ge(weights_in, 16 * 7)
            dve.tensor_tensor(wt[:, 1, :, :].rearrange("p k d -> p (k d)"), wt32[:, :],
                              wt[:, 0, :, :].rearrange("p k d -> p (k d)"), ALU.subtract).then_inc(dve_step, 1)
            for w, w32 in ((wq, wq32), (wp, wp32)):
                dve.tensor_tensor(w[:, 1, :, :], w32[:, :, :], w[:, 0, :, :], ALU.subtract)\
                   .then_inc(dve_step, 1)
            for i in range(IMAGES):
                dve.memset(th[i][DC:DC + 1, :, :], 1.0)
                dve.memset(tl[i][DC:DC + 1, :, :], 0.0)
            step.start(3)
            step(dve.tensor_tensor(base[:, :, :], base[:, :, :], pos_sb[:, :, :], ALU.add))
            for k in range(2):
                dve.sem_inc(bank_free[k], 1)
                dve.sem_inc(score_free[k], 1)
                dve.sem_inc(pv_free[k], 1)
            dve.sem_inc(h_done, IMAGES)
            for i in range(IMAGES):
                dve.sem_inc(stored[i], 32)

            def heads(ap):
                return ap.rearrange("p t (h d) -> p (t h) d", h=HEADS)

            def by_head(ap):
                return ap.rearrange("p (h d) -> p h d", h=HEADS)

            STEPS = {"tokens": 14, "divA": 1, "divS": 1, "proj": 13}

            def do(tn, s, m, i, turn, job):
                n = job[1]
                if s == "tokens":
                    banks.wait_full(dve, job, tn)
                    if tn.part != "pro":
                        banks.wait_freed(dve, ("fin", n - IMAGES), tn)
                    dve.tensor_tensor(h[i][:, :, :], tok_view(bank[banks.slot(s)]), base[:, :, :], ALU.add)\
                       .then_inc(h_done, 1)
                    dve.wait_ge(h_done, m + 4)
                    for t in range(2):
                        ins = dve.bn_stats(stats[:, t, :], h[i][:, t, :])
                        if t == 0:
                            banks.freed(ins, job)
                    step(ins)
                    dve.sem_inc(waited, 1)
                    for t in range(2):
                        ins = dve.bn_aggr(mv[:, t, :], stats[:, t, :])
                    step(ins)
                    step(dve.tensor_scalar(var[:, 0:2], mv[:, :, 1], LN_EPS, None, ALU.add))
                    rsqrt(dve, step, rstd[:, 0:2], var[:, 0:2], tmp[:, 0:2])
                    for t in range(2):
                        ins = dve.tensor_scalar(xn[i][:, t, :], h[i][:, t, :], mv[:, t, 0:1],
                                                rstd[:, t:t + 1], ALU.subtract, ALU.mult)
                    ins.then_inc(xn_done["tok"], 1)
                elif s in ("xnT", "projT", "finT"):
                    name = {"xnT": "tok", "projT": "att", "finT": "sim"}[s]
                    dve.wait_ge(hi_T[name], m + 1)
                    ins = dve.tensor_tensor(tl[i][0:DC, :, :], xT_view(bank[banks.slot(s)]),
                                            th[i][0:DC, :, :], ALU.subtract)
                    banks.freed(ins, job)
                elif s in ("qk0", "qk1"):
                    t = int(s[2])
                    src = bank[banks.slot(s)]
                    dve.wait_ge(hi_qk, m * 2 + t + 1)
                    for side, lo, copy in ((0, HD, 2 * HD), (1, 2 * HD, HD)):
                        hi = st[i][:, t, side, :, 0:HD]
                        dve.tensor_copy(st[i][:, t, side, :, copy:copy + HD], hi)
                        ins = dve.tensor_tensor(st[i][:, t, side, :, lo:lo + HD],
                                                by_head(src[0:TR, side * D:(side + 1) * D]), hi,
                                                ALU.subtract)
                    banks.freed(ins, job)
                elif s[:-1] == "rm":
                    gp, t = divmod(int(s[-1]), 2)
                    scores.wait_full(dve, job, tn)
                    dst = st[i][:, t, 0, 4 * gp:4 * gp + 4, 48].rearrange("p (a b) -> p b a", a=2)
                    ins = dve.tensor_reduce(dst, score_view(scores.slot(s))
                                            .rearrange("p j (g n) -> p j g n", g=2),
                                            AX.X, ALU.max, negate=True)
                    scores.freed(ins, job)
                elif s in ("divA", "divS"):
                    name = "att" if s == "divA" else "sim"
                    v = sums_view(scores.slot(s))
                    scores.wait_full(dve, job, tn)
                    step(dve.reciprocal(den[name][:, :, :], v[:, :, :, HD]))
                    for t in range(2):
                        ins = dve.tensor_tensor(by_head(xn[i][:, t, :]), v[:, t, :, 0:HD],
                                                den[name][:, t, :].unsqueeze(2).broadcast_to([TR, HEADS, HD]),
                                                ALU.mult)
                    ins.then_inc(xn_done[name], 1)
                    scores.freed(dve.memset(mark[:, :], 0.0), job)
                elif s == "proj":
                    dve.wait_ge(sq_done, m + 1)
                    step(dve.tensor_reduce(var[:, :], heads(sq[:, :, :]), AX.X, ALU.add))
                    step(dve.tensor_scalar(var[:, :], var[:, :], NORM_EPS2, None, ALU.max))
                    rsqrt(dve, step, rstd[:, :], var[:, :], tmp[:, :])
                    ins = dve.tensor_tensor(heads(sn[:, :, :]), heads(tok_view(bank[banks.slot(s)])),
                                            rstd[:, :].unsqueeze(2).broadcast_to([TR, 2 * HEADS, HD]),
                                            ALU.mult)
                    banks.freed(ins, job)
                elif s == "projlo":
                    dve.wait_ge(hi_sn, m + 1)
                    for side, lo, copy in ((0, HD, 2 * HD), (1, 2 * HD, HD)):
                        hi = st[i][:, :, side, :, 0:HD]
                        dve.tensor_copy(st[i][:, :, side, :, copy:copy + HD], hi)
                        ins = dve.tensor_tensor(st[i][:, :, side, :, lo:lo + HD],
                                                sn[:, :, :].rearrange("p t (h d) -> p t h d", h=HEADS),
                                                hi, ALU.subtract)
                    ins.then_inc(lo_sn, 1)
                elif s[:-1] == "si":
                    w = probs[probr.slot(s)][:, :, :]
                    dve.wait_ge(exp_done, m * NG + int(s[2]) + 1)
                    probr.filled(dve.scalar_tensor_tensor(w, score_view(scores.slot("sis" + s[2])), 0.0, w,
                                                          ALU.is_ge, ALU.mult), job)
                elif s == "fin":
                    banks.wait_full(dve, job, tn)
                    dve.wait_ge(stored[i], turn * 32 + 32)
                    banks.freed(dve.tensor_tensor(out[i][:, :, :], tok_view(bank[banks.slot(s)]),
                                                  h[i][:, :, :], ALU.add), job)

            SETUP = 4
            steps = {part: sum(STEPS.get(s, 0) for s, _ in tasks) for part, tasks in listed(DVE_ORDER).items()}
            started = set()

            def do_counted(tn, s, m, i, turn, job):
                if tn.part not in started:
                    started.add(tn.part)
                    step.start(tn.count(steps, 0) + SETUP)
                do(tn, s, m, i, turn, job)

            walk(dve, DVE_ORDER, do_counted)


KS = 5
TT = GT // 128
NE = E + 1
JOBS = NE * KFF
STEPS_F = 36


def feed_forward_phase(nc, sems, h1, w_in, w_down, w_router, e_bias, eye, rank, out):
    with ExitStack() as ctx:
        def sb(name, shape, dt=F32):
            return ctx.enter_context(nc.sbuf_tensor(name, shape, dt))

        def ps(name, shape, dt=F32):
            return ctx.enter_context(nc.psum_tensor(name, shape, dt))

        def sem(name):
            return sems.enter_context(nc.semaphore(name))

        wi32 = [sb(f"wi32_{k}", [128, KS, 2 * FF]) for k in range(2)]
        wi = sb("wi", [128, NE, KS, 2 * FF], F16)
        wd32 = [sb(f"wd32_{k}", [128, KFF, D]) for k in range(2)]
        wd = sb("wd", [128, NE, 2, KFF, D], F16)
        wr32 = sb("wr32", [128, KS, E])
        wr = sb("wr", [128, KS, E], F16)
        wlo = sb("wlo", [128, 2, 2 * FF], F16)
        ebias = sb("ebias", [128, TT, E])
        rank_sb = sb("rank_sb", [128, TT, E])
        eye32 = sb("eye32f", [128, 128])
        eye16 = sb("eye16f", [128, 128], F16)
        acc = [sb(f"acc{i}", [128, TT, D]) for i in range(2)]
        xn = sb("xnf", [128, TT, D])
        xs = sb("xs", [128, TT, KS * 128], F16)
        xsT = [sb(f"xsT{i}", [128, KS, GT], F16) for i in range(2)]
        comb = [sb(f"comb{i}", [128, TT, E]) for i in range(2)]
        sg = [sb(f"sg{k}", [128, GT]) for k in range(3)]
        gu32 = [sb(f"gu32_{k}", [128, GT]) for k in range(3)]
        gh = [sb(f"gh{k}", [128, KFF, GT], F16) for k in range(2)]
        gl = [sb(f"gl{k}", [128, KFF, GT], F16) for k in range(2)]
        stats = sb("statsf", [128, TT, 6])
        mv = sb("mvf", [128, TT, 2])
        small = {n: sb(f"{n}_f", [128, TT]) for n in ("var", "rstd", "tmp", "red")}
        wide = {n: sb(f"{n}_f", [128, TT, E]) for n in ("lg", "sc", "sel", "eq", "oh1", "oh2", "sel2")}

        GU = [ps(f"GU{k}", [128, 2, 512]) for k in range(2)]
        Y = ps("Y", [128, 2, 512])
        T = [ps(f"T{k}", [128, 512]) for k in range(2)]

        consts_in = sem("consts_in")
        w_in_ld = [sem(f"w_in_ld{k}") for k in range(2)]
        w_hi = sem("w_hi")
        w_lo = sem("w_lo")
        xs_zero = sem("xs_zero")
        acc_in = [sem(f"acc_in{i}") for i in range(2)]
        acc_out = [sem(f"acc_out{i}") for i in range(2)]
        xn_ready = sem("xn_ready")
        xs_hi = sem("xs_hi")
        xs_done = sem("xs_done")
        t_full = [sem(f"t_full{k}") for k in range(2)]
        t_free = [sem(f"t_free{k}") for k in range(2)]
        ex_done = sem("ex_done")
        gu_full = sem("gu_full")
        waited = sem("waited_f")
        silu_done = sem("silu_done")
        mul_done = sem("mul_done")
        hi_done = sem("hi_donef")
        lo_done = sem("lo_donef")
        y_full = sem("y_full")
        y_used = sem("y_used")
        dstep = sem("dstep")

        WSETUP = 2 * NE + 1

        def y_view(t):
            return Y[:, t // 2, (t % 2) * D:(t % 2 + 1) * D]

        block = ctx.enter_context(nc.Block())

        def rows_of(f):
            return h1[bass.ds(f * GT, GT), :].rearrange("(t p) d -> p t d", p=128)

        @block.sync
        def _(sp):
            for dst, src in ((wr32[:, :, :], w_router), (ebias[:, :, :], e_bias), (rank_sb[:, :, :], rank),
                             (eye32[:, :], eye)):
                sp.dma_start(dst, src).then_inc(consts_in, 16)
            for e in range(NE):
                if e >= 2:
                    sp.wait_ge(w_lo, 2 * (e - 1) + 1)
                sp.dma_start(wi32[e % 2][:, :, :], w_in[e, :, :, :]).then_inc(w_in_ld[e % 2], 16)
                sp.dma_start(wd32[e % 2][:, :, :], w_down[e, :, :, :]).then_inc(w_in_ld[e % 2], 16)
                if e < 2:
                    sp.dma_start(acc[e][:, :, :], rows_of(e)).then_inc(acc_in[e], 16)

            def turn(n, i, tail):
                sp.wait_ge(y_used, n * NE + NE + 1)
                if tail:
                    sp.dma_start(out[n * GT:n * GT + 256, :].rearrange("(t p) d -> p t d", p=128),
                                 acc[i][:, 0:2, :]).then_inc(acc_out[i], 16)
                    sp.dma_start(out[n * GT + 256:TOK, :], acc[i][0:TAIL - 256, 2, :])\
                      .then_inc(acc_out[i], 16)
                else:
                    sp.dma_start(out[bass.ds(n * GT, GT), :].rearrange("(t p) d -> p t d", p=128),
                                 acc[i][:, :, :]).then_inc(acc_out[i], 16)

            def reload(n, i, it):
                sp.wait_ge(acc_out[i], it * 16 + 16)
                sp.dma_start(acc[i][:, :, :], rows_of(n + 2)).then_inc(acc_in[i], 16)

            with sp.Fori(0, GROUPS // 2 - 1) as it:
                for i in range(2):
                    turn(it * 2 + i, i, False)
                    reload(it * 2 + i, i, it)
            last = GROUPS // 2 - 1
            turn(2 * last, 0, False)
            reload(2 * last, 0, last)
            turn(2 * last + 1, 1, False)
            turn(2 * last + 2, 0, True)
            sp.wait_ge(acc_out[0], 16 * (last + 1) + 32)
            sp.wait_ge(acc_out[1], 16 * (last + 1))

        @block.gpsimd
        def _(pool):
            pool.memset(xs[:, :, 3 * D:KS * 128], 0.0).then_inc(xs_zero, 1)

            def front(f):
                pool.wait_ge(xs_hi, f + 1)
                pool.sem_inc(waited, 1)
                pool.tensor_copy(xs[:, :, 2 * D:3 * D], xs[:, :, 0:D])
                pool.tensor_tensor(xs[:, :, D:2 * D], xn[:, :, :], xs[:, :, 0:D],
                                   ALU.subtract).then_inc(xs_done, 1)

            def group(n, i, nt, nxt):
                for k in range(JOBS):
                    e, j = divmod(k, KFF)
                    pool.wait_ge(hi_done, n * JOBS + k + 1)
                    pool.tensor_tensor(gl[(i + e) % 2][:, j, 0:nt], gu32[j][:, 0:nt],
                                       gh[(i + e) % 2][:, j, 0:nt], ALU.subtract).then_inc(lo_done, 1)
                    if k == 11 and nxt:
                        front(n + 1)

            pool.sem_inc(lo_done, 3)
            front(0)
            with pool.Fori(0, GROUPS // 2) as it:
                for i in range(2):
                    group(it * 2 + i, i, GT, True)
            group(GROUPS - 1, 0, TAIL, False)

        @block.tensor
        def _(pe):
            pe.wait_ge(xs_zero, 1)
            pe.wait_ge(w_lo, WSETUP)
            pe.wait_ge(w_hi, WSETUP + 1)
            pe.sem_inc(y_full, 2)

            def transposes(f):
                pe.wait_ge(xs_done, f + 1)
                for k, blocks in enumerate(((0, 1), (2, 3), (4,))):
                    pe.wait_ge(t_free[k % 2], f * 2 + k // 2 + 1)
                    v = T[k % 2][:, :].bitcast(F16)
                    for m, b in enumerate(blocks):
                        for t in range(TT):
                            last = pe.transpose(v[:, m * GT + t * 128:m * GT + (t + 1) * 128],
                                                xs[:, t, b * 128:(b + 1) * 128], eye16[:, :])
                    last.then_inc(t_full[k % 2], 1)

            def logits(f, i):
                pe.wait_ge(t_free[0], f * 2 + 3)
                pe.wait_ge(t_free[1], f * 2 + 2)
                for t in range(TT):
                    for b in range(KS):
                        last = pe.matmul(T[1][:, t * E:(t + 1) * E], xsT[i][:, b, t * 128:(t + 1) * 128],
                                         wr[:, b, :], start=(b == 0), stop=(b == KS - 1))
                last.then_inc(t_full[1], 1)

            def hidden(n, i, e, nt):
                for j in range(KFF):
                    k = e * KFF + j
                    s = (i + k) % 2
                    pe.wait_ge(mul_done, n * JOBS + k + 2)
                    for half in range(2):
                        for b in range(KS):
                            last = pe.matmul(GU[s][:, half, 0:nt],
                                             wi[:, e, b, half * FF + j * 128:half * FF + (j + 1) * 128],
                                             xsT[i][:, b, 0:nt], start=(b == 0), stop=(b == KS - 1))
                    last.then_inc(gu_full, 1)

            def down(n, i, e, nt):
                s = (i + e) % 2
                pe.wait_ge(lo_done, n * JOBS + e * KFF + KFF + 3)
                pe.wait_ge(y_used, n * NE + e + 1)
                parts = [(gh, 0), (gh, 1), (gl, 0)]
                for t in range(-(-nt // 128)):
                    rows = min(128, nt - t * 128)
                    for j in range(KFF):
                        for g, x in parts:
                            last = pe.matmul(y_view(t)[0:rows, :], g[s][:, j, t * 128:t * 128 + rows],
                                             wd[:, e, x, j, :], start=(j == 0 and (g, x) == parts[0]),
                                             stop=(j == KFF - 1 and (g, x) == parts[2]))
                last.then_inc(y_full, 1)

            def group(n, i, nt, nxt):
                for e in range(NE):
                    hidden(n, i, e, nt)
                    if e >= 1:
                        down(n, i, e - 1, nt)
                    if e == 5 and nxt:
                        transposes(n + 1)
                if nxt:
                    logits(n + 1, 1 - i)
                down(n, i, NE - 1, nt)

            transposes(0)
            logits(0, 0)
            with pe.Fori(0, GROUPS // 2) as it:
                for i in range(2):
                    group(it * 2 + i, i, GT, True)
            group(GROUPS - 1, 0, TAIL, False)

        @block.scalar
        def _(act):
            act.wait_ge(consts_in, 16 * 4)
            act.activation(eye16[:, :], eye32[:, :], ACT.Copy).then_inc(w_hi, 1)
            act.activation(wr[:, :, :], wr32[:, :, :], ACT.Copy).then_inc(w_hi, 1)
            for e in range(NE):
                act.wait_ge(w_in_ld[e % 2], 32 * (e // 2 + 1))
                act.activation(wi[:, e, :, :], wi32[e % 2][:, :, :], ACT.Copy).then_inc(w_hi, 1)
                act.activation(wd[:, e, 0, :, :], wd32[e % 2][:, :, :], ACT.Copy).then_inc(w_hi, 1)

            def front_hi(f):
                act.wait_ge(xn_ready, f + 1)
                act.activation(xs[:, :, 0:D], xn[:, :, :], ACT.Copy).then_inc(xs_hi, 1)

            def front_T(f, i):
                for k, blocks in enumerate(((0, 2), (2, 4), (4, 5))):
                    act.wait_ge(t_full[k % 2], f * 2 + k // 2 + 1)
                    w = blocks[1] - blocks[0]
                    src = T[k % 2][:, :].bitcast(F16)[:, 0:w * GT].rearrange("p (b n) -> p b n", b=w)
                    ins = act.activation(xsT[i][:, blocks[0]:blocks[1], :], src, ACT.Copy)
                    ins.then_inc(t_free[k % 2], 1)

            def front_exp(f):
                act.wait_ge(t_free[1], f * 2 + 3)
                act.activation(wide["lg"][:, :, :], wide["lg"][:, :, :], ACT.Exp).then_inc(ex_done, 1)

            def hi(n, i, k, nt):
                e, j = divmod(k, KFF)
                act.wait_ge(mul_done, n * JOBS + k + 4)
                if j == 0:
                    act.wait_ge(y_full, n * NE + e + 1)
                act.activation(gh[(i + e) % 2][:, j, 0:nt], gu32[j][:, 0:nt], ACT.Copy).then_inc(hi_done, 1)

            def group(n, i, nt, nxt):
                for k in range(JOBS):
                    j = k % KFF
                    act.wait_ge(gu_full, n * JOBS + k + 1)
                    act.wait_ge(mul_done, n * JOBS + k + 1)
                    act.activation(sg[j][:, 0:nt], GU[(i + k) % 2][:, 0, 0:nt], ACT.Silu)\
                       .then_inc(silu_done, 1)
                    if k:
                        hi(n, i, k - 1, nt)
                    if k == 10 and nxt:
                        front_hi(n + 1)
                    if k == 17 and nxt:
                        front_T(n + 1, 1 - i)
                hi(n, i, JOBS - 1, nt)
                if nxt:
                    front_exp(n + 1)

            front_hi(0)
            front_T(0, 0)
            front_exp(0)
            with act.Fori(0, GROUPS // 2) as it:
                for i in range(2):
                    group(it * 2 + i, i, GT, True)
            group(GROUPS - 1, 0, TAIL, False)

        @block.vector
        def _(dve):
            step = Steps(dve, dstep)
            dve.sem_inc(mul_done, 3)
            dve.sem_inc(y_used, 1)
            for k in range(2):
                dve.sem_inc(t_free[k], 1)
            dve.wait_ge(w_hi, 2)
            lo_rows = slice(3, KS)
            dve.tensor_tensor(wr[:, lo_rows, :], wr32[:, lo_rows, :], wr[:, lo_rows, :],
                              ALU.subtract).then_inc(w_lo, 1)
            for e in range(NE):
                dve.wait_ge(w_hi, 2 * e + 4)
                dve.tensor_tensor(wi[:, e, lo_rows, :], wi32[e % 2][:, lo_rows, :], wi[:, e, lo_rows, :],
                                  ALU.subtract).then_inc(w_lo, 1)
                dve.tensor_tensor(wd[:, e, 1, :, :], wd32[e % 2][:, :, :], wd[:, e, 0, :, :],
                                  ALU.subtract).then_inc(w_lo, 1)

            def norm(f, i, it):
                step.start(f * STEPS_F)
                dve.wait_ge(acc_in[i], it * 16 + 16)
                for t in range(TT):
                    ins = dve.bn_stats(stats[:, t, :], acc[i][:, t, :])
                step(ins)
                dve.sem_inc(waited, 1)
                for t in range(TT):
                    ins = dve.bn_aggr(mv[:, t, :], stats[:, t, :])
                step(ins)
                v, y, tm = (small[x][:, :] for x in ("var", "rstd", "tmp"))
                step(dve.tensor_scalar(v, mv[:, :, 1], LN_EPS, None, ALU.add))
                rsqrt(dve, step, y, v, tm)
                for t in range(TT):
                    ins = dve.tensor_scalar(xn[:, t, :], acc[i][:, t, :], mv[:, t, 0:1],
                                            small["rstd"][:, t:t + 1], ALU.subtract, ALU.mult)
                ins.then_inc(xn_ready, 1)

            def route(f, i):
                step.start(f * STEPS_F + 14)
                w = {n: t[:, :, :] for n, t in wide.items()}
                red = small["red"]
                one = red[:, :].unsqueeze(2).broadcast_to([128, TT, E])
                lg_psum = T[1][:, 0:TT * E].rearrange("p (t e) -> p t e", t=TT)
                dve.wait_ge(t_full[1], f * 2 + 2)
                step(dve.tensor_reduce(red[:, :], lg_psum, AX.X, ALU.max))
                ins = dve.tensor_tensor(w["lg"], lg_psum, one, ALU.subtract)
                ins.then_inc(t_free[1], 1)
                dve.wait_ge(ex_done, f + 1)
                step(dve.tensor_reduce(red[:, :], w["lg"], AX.X, ALU.add))
                step(dve.reciprocal(red[:, :], red[:, :]))
                step(dve.tensor_tensor(w["sc"], w["lg"], one, ALU.mult))
                step(dve.tensor_tensor(w["sel"], w["sc"], ebias[:, :, :], ALU.add))
                for name, src in (("oh1", "sel"), ("oh2", "sel2")):
                    if name == "oh2":
                        step(dve.scalar_tensor_tensor(w["sel2"], w["oh1"], -1e30, w["sel"],
                                                      ALU.mult, ALU.add))
                    step(dve.tensor_reduce(red[:, :], w[src], AX.X, ALU.max))
                    step(dve.tensor_tensor(w["eq"], w[src], one, ALU.is_equal))
                    step(dve.tensor_tensor(w["eq"], w["eq"], rank_sb[:, :, :], ALU.mult))
                    step(dve.tensor_reduce(red[:, :], w["eq"], AX.X, ALU.max))
                    step(dve.tensor_tensor(w[name], w["eq"], one, ALU.is_equal))
                step(dve.tensor_tensor(w["eq"], w["oh1"], w["oh2"], ALU.add))
                step(dve.tensor_tensor(w["eq"], w["eq"], w["sc"], ALU.mult))
                step(dve.tensor_reduce(red[:, :], w["eq"], AX.X, ALU.add))
                step(dve.tensor_scalar(red[:, :], red[:, :], 1e-9, None, ALU.add))
                step(dve.reciprocal(red[:, :], red[:, :]))
                step(dve.tensor_tensor(comb[i][:, :, :], w["eq"], one, ALU.mult))
                assert step.n == STEPS_F - 14, step.n

            def add_expert(n, i, e, nt):
                dve.wait_ge(y_full, n * NE + e + 3)
                for t in range(-(-nt // 128)):
                    r = min(128, nt - t * 128)
                    a = acc[i][0:r, t, :]
                    if e == 0:
                        ins = dve.tensor_tensor(a, y_view(t)[0:r, :], a, ALU.add)
                    else:
                        ins = dve.scalar_tensor_tensor(a, y_view(t)[0:r, :], comb[i][0:r, t, e - 1:e], a,
                                                       ALU.mult, ALU.add)
                ins.then_inc(y_used, 1)
                if e < NE - 1:
                    dve.wait_ge(y_used, n * NE + e + 2)

            def group(n, i, nt, nxt, it):
                for k in range(JOBS):
                    e, j = divmod(k, KFF)
                    dve.wait_ge(silu_done, n * JOBS + k + 1)
                    dve.wait_ge(lo_done, n * JOBS + k + 1)
                    dve.tensor_tensor(gu32[j][:, 0:nt], GU[(i + k) % 2][:, 1, 0:nt], sg[j][:, 0:nt],
                                      ALU.mult).then_inc(mul_done, 1)
                    if k == 5 and nxt:
                        norm(n + 1, 1 - i, it + i)
                    if j == KFF - 1 and e >= 1:
                        add_expert(n, i, e - 1, nt)
                if nxt:
                    route(n + 1, 1 - i)
                add_expert(n, i, NE - 1, nt)

            norm(0, 0, 0)
            route(0, 0)
            with dve.Fori(0, GROUPS // 2) as it:
                for i in range(2):
                    group(it * 2 + i, i, GT, True, it)
            group(GROUPS - 1, 0, TAIL, False, GROUPS // 2)


def build(nc, xT, w_tok, addend, pos, w_qkv, w_proj, w_in, w_down, w_router, e_bias, eye, key_mask, rank,
          out):
    h1 = nc.dram_tensor("h1_scratch", (GROUPS * GT, D), F32, kind="Internal").ap()
    with ExitStack() as sems:
        attention_phase(nc, sems, xT, w_tok, addend, pos, w_qkv, w_proj, eye, key_mask, h1)
        feed_forward_phase(nc, sems, h1, w_in, w_down, w_router, e_bias, eye, rank, out)


def lay_out(inputs):
    import numpy as np

    def a(name):
        return np.ascontiguousarray(inputs[name])

    x = a("x").reshape(B, CH, SIDE, P, SIDE, P).transpose(0, 1, 3, 5, 2, 4).reshape(B, KF, 128, SEQ - 1)
    xT = np.zeros((B, 128, KF, SEQ), np.float32)
    xT[..., 1:] = x.transpose(0, 2, 1, 3)
    tiles = np.stack([np.arange(TR), np.arange(TR) + HALF], 1)
    w_tok = a("L0_tok_W").reshape(KF, 128, D).transpose(1, 0, 2).reshape(128, KF * D)
    addend = np.broadcast_to(a("L0_tok_b"), (TR, 2, D)).copy()
    addend[0, 0] = a("L0_tok_class_token").reshape(D)
    pos = a("L0_tok_pos_table")[tiles]

    def with_bias(w, b):
        r = np.zeros((DC + 1, 2, w.shape[0]), np.float32)
        r[:DC] = w.T.reshape(2, DC, -1).transpose(1, 0, 2)
        r[DC, 0] = b
        return r

    def stacked(w):
        r = np.zeros(w.shape[:-2] + (KS * 128, w.shape[-1]), np.float32)
        for k in range(3):
            r[..., k * D:(k + 1) * D, :] = w
        return np.moveaxis(r.reshape(w.shape[:-2] + (KS, 128, w.shape[-1])), -3, -2)

    gate = np.concatenate([a("L0_ffn_sg")[None], a("L0_ffn_Wg")])
    up = np.concatenate([a("L0_ffn_su")[None], a("L0_ffn_Wu")])
    down = np.concatenate([a("L0_ffn_sd")[None], a("L0_ffn_Wd")])
    w_in = stacked(np.concatenate([gate, up], 1).transpose(0, 2, 1))
    w_down = down.transpose(0, 2, 1).reshape(NE, KFF, 128, D).transpose(0, 2, 1, 3)
    mask = np.ones((TR, 2), np.float32)
    mask[0, 1] = 0.0
    return {
        "xT": xT, "w_tok": w_tok, "addend": addend, "pos": pos,
        "w_qkv": with_bias(a("L0_attn_qkv_w"), a("L0_attn_qkv_b")),
        "w_proj": with_bias(a("L0_attn_proj_w"), a("L0_attn_proj_b")),
        "w_in": w_in, "w_down": w_down, "w_router": stacked(a("L0_ffn_w_router").T),
        "e_bias": np.broadcast_to(a("L0_ffn_expert_bias"), (128, TT, E)),
        "eye": np.eye(128, dtype=np.float32), "key_mask": mask,
        "rank": np.broadcast_to(np.arange(E, 0, -1, dtype=np.float32), (128, TT, E)),
    }


def kernel(**inputs):
    import numpy as np
    import concourse.bacc as bacc
    from concourse.bass_utils import run_bass_kernel_spmd

    nc = bacc.Bacc("TRN2", target_bir_lowering=False, num_devices=1)
    arrays, args = {}, []
    for name, value in lay_out(inputs).items():
        value = np.ascontiguousarray(value)
        arrays[f"in_{name}"] = value
        args.append(nc.dram_tensor(f"in_{name}", value.shape, mybir.dt.from_np(value.dtype),
                                   kind="ExternalInput").ap())
    out = nc.dram_tensor("out", (TOK, D), F32, kind="ExternalOutput").ap()
    build(nc, *args, out)
    result = run_bass_kernel_spmd(nc, [arrays], core_ids=[0])
    return result.results[0]["out"].reshape(B, SEQ, D)
```

```python
from contextlib import ExitStack

import concourse.bass as bass
from concourse import mybir

F32 = mybir.dt.float32
F16 = mybir.dt.float16
I32 = mybir.dt.int32
ALU = mybir.AluOpType
ACT = mybir.ActivationFunctionType
AX = mybir.AxisListType

B, CH, IMG, P = 64, 3, 224, 16
D = 192
SIDE = IMG // P
SEQ = SIDE * SIDE + 1
FEAT = CH * P * P
KF = FEAT // 128
HEADS, HD = 12, 16
E, FF = 8, 384
DC = D // 2
HALF = 98
TR = SEQ - HALF
SP = SEQ + 1
QUAD = 32
SLOT = 64
NG = HEADS // 2
IMAGES = 3
TURNS = (B - 4) // IMAGES
ATT_SCALE, SIM_SCALE = HD ** -0.5, 10.0
NORM_EPS2, LN_EPS = 1e-24, 1e-5
RSQRT_MAGIC = 1597463007.0

TOK = B * SEQ
GT = 512
NT = GT // 128
GROUPS = -(-TOK // GT)
PAD = GROUPS * GT - TOK
TAIL = TOK - (GROUPS - 1) * GT
KFF = FF // 128


class Turn:

    def __init__(self, part, it=0):
        self.part, self.it = part, it

    def count(self, per, at):
        if self.part == "pro":
            return at
        if self.part == "body":
            return self.it * per["body"] + (per["pro"] + at)
        return per["pro"] + TURNS * per["body"] + at


class Ring:

    def __init__(self, full, free, order, parts, freeing=None):
        self.full, self.free, n = full, free, len(full)
        self.slots = {task: k % n for k, task in enumerate(order)}
        self.freeing = set(order if freeing is None else freeing)
        self.users = [[t for t in order if self.slots[t] == s] for s in range(n)]
        self.uses, self.frees = [{} for _ in range(n)], [{} for _ in range(n)]
        self.filled_by, self.freed_by, self.prior = {}, {}, {}
        for part, listed in parts.items():
            for s in range(n):
                fills = frees = 0
                before = None if part == "pro" else (self.users[s][-1], None)
                for task, m in listed:
                    if self.slots.get(task) == s:
                        self.filled_by[part, task, m], self.freed_by[part, task, m] = fills, frees
                        self.prior[part, task, m] = before
                        before = (task, m)
                        fills += 1
                        frees += task in self.freeing
                self.uses[s][part], self.frees[s][part] = fills, frees

    def slot(self, task):
        return self.slots[task]

    def place(self, counted, users, tn, job):
        task, m = job
        if m is not None and (tn.part, task, m) in counted:
            return counted[tn.part, task, m]
        return users.index(task) - len(users)

    def fills(self, tn, job):
        s = self.slots[job[0]]
        return tn.count(self.uses[s], self.place(self.filled_by, self.users[s], tn, job) + 1)

    def frees_by(self, tn, job, extra):
        s = self.slots[job[0]]
        users = [t for t in self.users[s] if t in self.freeing]
        return tn.count(self.frees[s], self.place(self.freed_by, users, tn, job) + extra)

    def before(self, tn, job):
        return self.prior[(tn.part,) + job]

    def wait_free(self, eng, job, tn):
        eng.wait_ge(self.free[self.slots[job[0]]], self.frees_by(tn, job, 1))

    def wait_freed(self, eng, job, tn):
        eng.wait_ge(self.free[self.slots[job[0]]], self.frees_by(tn, job, 2))

    def wait_full(self, eng, job, tn):
        eng.wait_ge(self.full[self.slots[job[0]]], self.fills(tn, job))

    def filled(self, ins, job):
        ins.then_inc(self.full[self.slots[job[0]]], 1)

    def freed(self, ins, job):
        ins.then_inc(self.free[self.slots[job[0]]], 1)


class Steps:

    def __init__(self, eng, sem):
        self.eng, self.sem, self.base, self.n = eng, sem, 0, 0

    def __call__(self, ins):
        ins.then_inc(self.sem, 1)
        self.n += 1
        self.eng.wait_ge(self.sem, self.base + self.n)

    def start(self, base):
        self.base, self.n = base, 0


def rsqrt(dve, step, y, v, tmp):
    step(dve.tensor_scalar(y.bitcast(I32), v.bitcast(I32), 1, None, ALU.logical_shift_right))
    step(dve.tensor_scalar(y.bitcast(I32), y.bitcast(I32), -1.0, RSQRT_MAGIC, ALU.mult, ALU.add))
    for _ in range(3):
        step(dve.scalar_tensor_tensor(tmp, y, -0.5, y, ALU.mult, ALU.mult))
        step(dve.tensor_tensor(tmp, tmp, v, ALU.mult))
        step(dve.scalar_tensor_tensor(y, tmp, 1.5, y, ALU.add, ALU.mult))


def attention_phase(nc, sems, xT, w_tok, addend, pos, w_qkv, w_proj, eye, key_mask, h1):
    with ExitStack() as ctx:
        def sb(name, shape, dt=F32):
            return ctx.enter_context(nc.sbuf_tensor(name, shape, dt))

        def ps(name, shape, dt=F32):
            return ctx.enter_context(nc.psum_tensor(name, shape, dt))

        def sem(name):
            return sems.enter_context(nc.semaphore(name))

        wt32 = sb("wt32", [128, KF * D])
        wt = sb("wt", [128, 2, KF, D], F16)
        wq32 = sb("wq32", [DC + 1, 2, 3 * D])
        wq = sb("wq", [DC + 1, 2, 2, 3 * D], F16)
        wp32 = sb("wp32", [DC + 1, 2, D])
        wp = sb("wp", [DC + 1, 2, 2, D], F16)
        base = sb("base", [TR, 2, D])
        pos_sb = sb("pos_sb", [TR, 2, D])
        eye32 = sb("eye32", [128, 128])
        eye16 = sb("eye16", [128, 128], F16)
        mask = sb("mask", [TR, 2])
        xt = [sb(f"xt{i}", [128, KF, SEQ]) for i in range(IMAGES)]
        xh = [sb(f"xh{i}", [128, KF, SEQ], F16) for i in range(IMAGES)]
        xl = [sb(f"xl{i}", [128, KF, SEQ], F16) for i in range(IMAGES)]
        h = [sb(f"h{i}", [TR, 2, D]) for i in range(IMAGES)]
        xn = [sb(f"xn{i}", [TR, 2, D]) for i in range(IMAGES)]
        th = [sb(f"th{i}", [DC + 1, 2, SEQ], F16) for i in range(IMAGES)]
        tl = [sb(f"tl{i}", [DC + 1, 2, SEQ], F16) for i in range(IMAGES)]
        st = [sb(f"st{i}", [TR, 2, 2, HEADS, SLOT], F16) for i in range(IMAGES)]
        lT = [sb(f"lT{i}", [128, NG, SP], F16) for i in range(IMAGES)]
        mT = [sb(f"mT{i}", [128, NG, SP], F16) for i in range(IMAGES)]
        rT = [sb(f"rT{i}", [128, NG, SP], F16) for i in range(IMAGES)]
        va = [sb(f"va{i}", [TR, 2, HEADS, QUAD]) for i in range(IMAGES)]
        pvs = [sb(f"pvs{i}", [128, HEADS // 4, SEQ]) for i in range(IMAGES)]
        out = [sb(f"out{i}", [TR, 2, D]) for i in range(IMAGES)]
        probs = [sb(f"probs{k}", [TR, 2, 2 * SEQ]) for k in range(3)]
        stats = sb("stats", [TR, 2, 6])
        mv = sb("mv", [TR, 2, 2])
        var = sb("var", [TR, 2 * HEADS])
        rstd = sb("rstd", [TR, 2 * HEADS])
        tmp = sb("tmp", [TR, 2 * HEADS])
        den = {n: sb(f"den_{n}", [TR, 2, HEADS]) for n in ("att", "sim")}
        sq = sb("sq", [TR, 2, D])
        sn = sb("sn", [TR, 2, D])
        mark = sb("mark", [1, 1])
        zrow = sb("zrow", [PAD // 2, 2 * D])

        bank = [ps(f"bank{k}", [128, 512]) for k in range(2)]
        score = [ps(f"score{k}", [128, 2, 512]) for k in range(2)]
        pv = [ps(f"pv{k}", [128, 512]) for k in range(2)]

        weights_in = sem("weights_in")
        consts_done = sem("consts_done")
        act_setup = sem("act_setup")
        x_in = [sem(f"x_in{i}") for i in range(IMAGES)]
        x_split = sem("x_split")
        x_hi = sem("x_hi")
        hi_T = {n: sem(f"hi_T_{n}") for n in ("tok", "att", "sim")}
        xn_done = {n: sem(f"xn_{n}") for n in ("tok", "att", "sim")}
        hi_qk = sem("hi_qk")
        sq_done = sem("sq_done")
        hi_sn = sem("hi_sn")
        lo_sn = sem("lo_sn")
        h_done = sem("h_done")
        waited = sem("waited")
        exp_done = sem("exp_done")
        stored = [sem(f"stored{i}") for i in range(IMAGES)]
        pad_in = sem("pad_in")
        dve_step = sem("dve_step")
        bank_full = [sem(f"bank_full{k}") for k in range(2)]
        bank_free = [sem(f"bank_free{k}") for k in range(2)]
        score_full = [sem(f"score_full{k}") for k in range(2)]
        score_free = [sem(f"score_free{k}") for k in range(2)]
        prob_full = [sem(f"prob_full{k}") for k in range(3)]
        prob_free = [sem(f"prob_free{k}") for k in range(3)]
        pv_full = [sem(f"pv_full{k}") for k in range(2)]
        pv_free = [sem(f"pv_free{k}") for k in range(2)]

        FRONT = {"tokens", "xnT", "qk0", "qk1", "v"}
        FRONT |= {f"stack{x}{k}" for x in "LRM" for k in range(2)} | {f"rm{u}" for u in range(NG)}
        SIM = {f"stack{x}{k}" for x in "AB" for k in range(2)} | {"divS"}
        SIM |= {f"{kind}{u}" for kind in ("sis", "si", "siv", "sip") for u in range(NG)}
        BACK = {"finT", "fin"}
        DENSE_N = 512
        DENSE = {"atv0": 1, "atv2": 1, "atv4": 1, "siv0": 1, "siv2": 1, "siv4": 1, "xnT": 3, "stackA0": 4,
                 "stackM0": 2, "proj": 1, "projT": 1}
        PE_ORDER = (
            "stackA0 ats0 stackB0 ats1 finT stackB1 stackA1 fin atv0 sis0 sis1 tokens atv1 ats2 "
            "siv0 siv1 ats3 ats4 atv2 atv3 ats5 atv4 xnT sis2 sis3 atv5 qk0 qk1 sis4 sis5 siv2 "
            "stackR0 stackL0 stackL1 stackR1 divA rm0 rm1 projT siv3 rm2 siv4 rm3 proj rm4 rm5 v "
            "siv5 stackM0 stackM1 divS").split()
        ACT_ORDER = (
            "stackA0 stackB0 finT stackB1 at0 stackA1 at1 si0 si1 atp0 at2 at3 at4 sip0 at5 xnT si2 "
            "atp1 si3 qk0 qk1 si4 si5 stackR0 stackL0 atp2 stackL1 stackR1 projT sip1 projsq sip2 v "
            "proj stackM0 stackM1").split()
        DVE_ORDER = (
            "finT si0 si1 fin tokens xnT si2 si3 qk0 qk1 si4 si5 divA rm0 rm1 projT rm2 rm3 rm4 "
            "proj rm5 projlo divS").split()

        def listed(order):
            def steps(cs):
                found = []
                for c in cs:
                    for s in order:
                        m = c + (1 if s in FRONT else -1 if s in SIM else -2 if s in BACK else 0)
                        if 0 <= m < B:
                            found.append((s, m))
                return found
            return {"pro": steps((-1, 0, 1)), "body": steps((2, 3, 4)), "epi": steps((B - 2, B - 1, B, B + 1))}

        def walk(eng, order, do):
            parts = listed(order)
            for s, m in parts["pro"]:
                do(Turn("pro"), s, m, m % IMAGES, m // IMAGES, (s, m))
            with eng.Fori(0, TURNS) as it:
                for s, c in parts["body"]:
                    do(Turn("body", it), s, it * IMAGES + c, c % IMAGES, it + c // IMAGES, (s, c))
            for s, m in parts["epi"]:
                do(Turn("epi"), s, m, m % IMAGES, m // IMAGES, (s, m))

        def ring(full, free, order, takes, freeing=None):
            chosen = [s for s in order if s in takes]
            return Ring(full, free, chosen, listed(order), freeing)

        units = range(NG)
        banks = ring(bank_full, bank_free, PE_ORDER,
                     FRONT - {f"rm{u}" for u in units} | {"projT", "proj"} | BACK | SIM & set(
                         f"stack{x}{k}" for x in "AB" for k in range(2)))
        own = {f"rm{u}" for u in units} | {"divA", "divS"}
        scores = ring(score_full, score_free, PE_ORDER,
                      own | {f"{kind}s{u}" for kind in ("at", "si") for u in units}, freeing=own)
        probr = ring(prob_full, prob_free, ACT_ORDER, {f"{kind}{u}" for kind in ("at", "si") for u in units})
        pvr = ring(pv_full, pv_free, PE_ORDER, {f"{kind}v{2 * g}" for kind in ("at", "si") for g in range(3)})

        def cols(t):
            return slice(HALF * t, HALF * t + TR)

        def tok_view(b):
            return b[0:TR, 0:2 * D].rearrange("p (t d) -> p t d", t=2)

        def xT_view(b):
            return b[0:DC, 0:2 * SEQ].rearrange("p (c n) -> p c n", c=2)

        def stack_view(b):
            return b[:, :].bitcast(F16)[:, 0:3 * SP].rearrange("p (g n) -> p g n", g=3)

        def sums_view(k):
            return score[k][0:TR, :, 0:HEADS * QUAD].rearrange("p t (h d) -> p t h d", h=HEADS)

        def score_view(k):
            return score[k][0:TR, :, 0:2 * SEQ]

        block = ctx.enter_context(nc.Block())

        @block.sync
        def _(sp):
            for dst, src in ((wt32[:, :], w_tok), (wq32[:, :, :], w_qkv), (wp32[:, :, :], w_proj),
                             (base[:, :, :], addend), (pos_sb[:, :, :], pos), (eye32[:, :], eye),
                             (mask[:, :], key_mask)):
                sp.dma_start(dst, src).then_inc(weights_in, 16)
            sp.wait_ge(consts_done, 1)
            sp.dma_start(h1[TOK:TOK + PAD, :].rearrange("(p a) d -> p (a d)", a=2), zrow[:, :]).then_inc(pad_in, 16)

            def load(n, i):
                sp.wait_ge(x_split, n + 1)
                sp.dma_start(xt[i][:, :, :], xT[n, :, :, :]).then_inc(x_in[i], 16)

            def store(tn, m, i, job):
                banks.wait_freed(sp, job, tn)
                sp.dma_start(h1[bass.ds(m * SEQ, TR), :], out[i][:, 0, :]).then_inc(stored[i], 16)
                sp.dma_start(h1[bass.ds(m * SEQ + TR, TR - 1), :],
                             out[i][1:TR, 1, :]).then_inc(stored[i], 16)

            for n in range(4):
                load(n, n % IMAGES)
            with sp.Fori(0, TURNS) as it:
                for c in (2, 3, 4):
                    store(Turn("body", it), it * IMAGES + (c - 2), (c - 2) % IMAGES, ("fin", c - 2))
                    load(it * IMAGES + (c + 2), (c + 2) % IMAGES)
            for m in range(B - 4, B):
                store(Turn("epi"), m, m % IMAGES, ("fin", m))
            for i in range(IMAGES):
                sp.wait_ge(stored[i], 32 * len(range(i, B, IMAGES)) + 32)
            sp.wait_ge(pad_in, 16)

        @block.gpsimd
        def _(pool):
            for i in range(IMAGES):
                pool.memset(st[i][:, :, :, :, :], 0.0)
                pool.memset(va[i][:, :, :, :], 0.0)
            pool.memset(zrow[:, :], 0.0).then_inc(consts_done, 1)
            pool.wait_ge(consts_done, 1)
            for i in range(IMAGES):
                last = pool.memset(st[i][:, :, 1, :, 48:49], 1.0)
            last.then_inc(consts_done, 1)
            pool.wait_ge(consts_done, 2)
            pool.wait_ge(act_setup, 1)
            pool.sem_inc(x_split, IMAGES)

            def split(m, i, turn):
                pool.wait_ge(x_in[i], turn * 16 + 16)
                pool.wait_ge(h_done, m + 1)
                pool.sem_inc(waited, 1)
                pool.tensor_copy(xh[i][:, :, :], xt[i][:, :, :]).then_inc(x_hi, 1)
                pool.wait_ge(x_hi, m + 1)
                pool.tensor_tensor(xl[i][:, :, :], xt[i][:, :, :], xh[i][:, :, :],
                                   ALU.subtract).then_inc(x_split, 1)

            with pool.Fori(0, B // IMAGES) as it:
                for i in range(IMAGES):
                    split(it * IMAGES + i, i, it)
            for m in range(B - B % IMAGES, B):
                split(m, m % IMAGES, m // IMAGES)

        @block.tensor
        def _(pe):
            pe.wait_ge(consts_done, 2)
            pe.wait_ge(act_setup, 1)
            pe.wait_ge(dve_step, 4)
            for k in range(3):
                pe.sem_inc(prob_free[k], 1)

            def hold_clock(task, buffer):
                for _ in range(DENSE.get(task, 0)):
                    pe.matmul(buffer[:, 0:DENSE_N], wt[:, 0, 0, 0:128], dense, start=True, stop=True)

            dense = wt[:, 0, :, :].rearrange("p k d -> p (k d)")[:, 0:DENSE_N]

            def transposed(job, name, i, m, tn):
                banks.wait_free(pe, job, tn)
                hold_clock(job[0], bank[banks.slot(job[0])])
                pe.wait_ge(xn_done[name], m + 1)
                for t in range(2):
                    for c in range(2):
                        last = pe.transpose(xT_view(bank[banks.slot(job[0])])[:, c, cols(t)],
                                            xn[i][:, t, c * DC:(c + 1) * DC], eye32[0:TR, 0:TR])
                banks.filled(last, job)

            def product(dst, w, i, t, lo, hi):
                parts = [(th, 0), (th, 1), (tl, 0)]
                for c in range(2):
                    rows = DC + 1 if c == 0 else DC
                    for a, x in parts:
                        last = pe.matmul(dst, a[i][0:rows, c, cols(t)], w[0:rows, x, c, lo:hi],
                                         start=(c == 0 and (a, x) == parts[0]),
                                         stop=(c == 1 and (a, x) == parts[2]))
                return last

            def stack_T(job, i, side, tn):
                half = int(job[0][-1])
                for t in range(2):
                    src = st[i][:, t, side, :, :].rearrange("p (g x) s -> p g (x s)", g=NG)
                    for g in range(3):
                        last = pe.transpose(stack_view(bank[banks.slot(job[0])])[:, g, cols(t)],
                                            src[:, 3 * half + g, :], eye16[0:TR, 0:TR])
                banks.filled(last, job)

            def four_heads(job, tn, stationary, moving, rows_n):
                gp, t = divmod(int(job[0][-1]), 2)
                k = scores.slot(job[0])
                last_job = scores.before(tn, job)
                if last_job and last_job[0] not in scores.freeing:
                    probr.wait_full(pe, (last_job[0][:2] + last_job[0][-1], last_job[1]), tn)
                else:
                    scores.wait_free(pe, job, tn)
                for gg in range(2):
                    for j in range(2):
                        rows = slice(SLOT * j, SLOT * j + rows_n)
                        g = 2 * gp + gg
                        last = pe.matmul(score_view(k)[:, j, gg * SEQ:(gg + 1) * SEQ],
                                         stationary[rows, g, cols(t)], moving[rows, g, 0:SEQ],
                                         start=True, stop=True)
                scores.filled(last, job)

            def values(kind, i, u, m, tn):
                gp, kt = divmod(u, 2)
                job, sums = (f"{kind}{u}", m), (f"{kind}v{2 * gp}", m)
                k, b = probr.slot(job[0]), pvr.slot(sums[0])
                if kt == 0:
                    pvr.wait_free(pe, sums, tn)
                    hold_clock(f"{kind}v{u}", pv[b])
                probr.wait_full(pe, job, tn)
                for q in range(4):
                    gg, j = divmod(q, 2)
                    last = pe.matmul(pv[b][QUAD * q:QUAD * (q + 1), 0:SEQ], va[i][:, kt, 4 * gp + q, :],
                                     probs[k][:, j, gg * SEQ:(gg + 1) * SEQ],
                                     start=(kt == 0), stop=(kt == 1))
                probr.freed(last, job)

            def do(tn, s, m, i, turn, job):
                n = job[1]
                if s == "tokens":
                    pe.wait_ge(x_split, m + 4)
                    banks.wait_free(pe, job, tn)
                    parts = [(xh, 0), (xh, 1), (xl, 0)]
                    for t in range(2):
                        for k in range(KF):
                            for a, x in parts:
                                last = pe.matmul(tok_view(bank[banks.slot(s)])[:, t, :], a[i][:, k, cols(t)],
                                                 wt[:, x, k, :], start=(k == 0 and (a, x) == parts[0]),
                                                 stop=(k == KF - 1 and (a, x) == parts[2]))
                    banks.filled(last, job)
                elif s == "xnT":
                    transposed(job, "tok", i, m, tn)
                elif s in ("qk0", "qk1"):
                    banks.wait_free(pe, job, tn)
                    hold_clock(s, bank[banks.slot(s)])
                    banks.wait_freed(pe, ("xnT", n), tn)
                    banks.filled(product(bank[banks.slot(s)][0:TR, 0:2 * D], wq, i, int(s[2]), 0, 2 * D), job)
                elif s == "v":
                    banks.wait_freed(pe, ("xnT", n), tn)
                    banks.wait_free(pe, job, tn)
                    for t in range(2):
                        last = product(tok_view(bank[banks.slot(s)])[:, t, :], wq, i, t, 2 * D, 3 * D)
                    banks.filled(last, job)
                elif s[:-1] in ("stackL", "stackR"):
                    banks.wait_free(pe, job, tn)
                    hold_clock(s, bank[banks.slot(s)])
                    banks.wait_freed(pe, ("qk0", n), tn)
                    banks.wait_freed(pe, ("qk1", n), tn)
                    stack_T(job, i, 0 if s[5] == "L" else 1, tn)
                elif s[:-1] == "stackM":
                    banks.wait_free(pe, job, tn)
                    hold_clock(s, bank[banks.slot(s)])
                    scores.wait_freed(pe, ("rm4", n), tn)
                    scores.wait_freed(pe, ("rm5", n), tn)
                    stack_T(job, i, 0, tn)
                elif s[:-1] in ("stackA", "stackB"):
                    banks.wait_free(pe, job, tn)
                    hold_clock(s, bank[banks.slot(s)])
                    pe.wait_ge(lo_sn, m + 1)
                    stack_T(job, i, 0 if s[5] == "A" else 1, tn)
                elif s[:-1] == "rm":
                    if s == "rm0":
                        for x in ("L0", "L1", "R0", "R1"):
                            banks.wait_freed(pe, ("stack" + x, n), tn)
                    four_heads(job, tn, lT[i], rT[i], 48)
                elif s[:-1] == "ats":
                    if s == "ats0":
                        for x in ("stackM0", "stackM1", "v"):
                            banks.wait_freed(pe, (x, n), tn)
                    four_heads(job, tn, rT[i], mT[i], SLOT)
                elif s[:-1] == "sis":
                    if s == "sis0":
                        for x in ("A0", "A1", "B0", "B1"):
                            banks.wait_freed(pe, ("stack" + x, n), tn)
                    four_heads(job, tn, rT[i], lT[i], 48)
                elif s[:-1] in ("atv", "siv"):
                    values(s[:2], i, int(s[3]), n, tn)
                elif s in ("divA", "divS"):
                    kind = "at" if s == "divA" else "si"
                    for g in range(3):
                        pvr.wait_freed(pe, (f"{kind}v{2 * g}", n), tn)
                    k = scores.slot(s)
                    last_job = scores.before(tn, job)
                    if last_job and last_job[0] not in scores.freeing:
                        probr.wait_full(pe, (last_job[0][:2] + last_job[0][-1], last_job[1]), tn)
                    else:
                        scores.wait_free(pe, job, tn)
                    for t in range(2):
                        for gp in range(3):
                            last = pe.transpose(score[k][0:TR, t, gp * 128:(gp + 1) * 128],
                                                pvs[i][:, gp, cols(t)], eye32[:, :])
                    scores.filled(last, job)
                elif s in ("projT", "finT"):
                    transposed(job, "att" if s == "projT" else "sim", i, m, tn)
                elif s in ("proj", "fin"):
                    banks.wait_free(pe, job, tn)
                    hold_clock(s, bank[banks.slot(s)])
                    banks.wait_freed(pe, (s + "T", n), tn)
                    for t in range(2):
                        last = product(tok_view(bank[banks.slot(s)])[:, t, :], wp, i, t, 0, D)
                    banks.filled(last, job)

            walk(pe, PE_ORDER, do)

        @block.scalar
        def _(act):
            act.wait_ge(weights_in, 16 * 7)
            act.wait_ge(consts_done, 1)
            act.activation(wt[:, 0, :, :].rearrange("p k d -> p (k d)"), wt32[:, :], ACT.Copy)
            act.activation(wq[:, 0, :, :], wq32[:, :, :], ACT.Copy)
            act.activation(wp[:, 0, :, :], wp32[:, :, :], ACT.Copy)
            for i in range(IMAGES):
                for t in range(2):
                    act.activation(va[i][:, t, :, HD], eye32[0:TR, 0:HEADS], ACT.Identity,
                                   bias=mask[:, t:t + 1], scale=0.0)
            act.activation(eye16[:, :], eye32[:, :], ACT.Copy).then_inc(act_setup, 1)

            def hi_half(job, name, i, tn):
                banks.wait_full(act, job, tn)
                act.activation(th[i][0:DC, :, :], xT_view(bank[banks.slot(job[0])]), ACT.Copy)\
                   .then_inc(hi_T[name], 1)

            STACKS = {"L": lT, "A": lT, "R": rT, "B": rT, "M": mT}

            def do(tn, s, m, i, turn, job):
                n = job[1]
                if s == "xnT":
                    hi_half(job, "tok", i, tn)
                elif s in ("qk0", "qk1"):
                    banks.wait_full(act, job, tn)
                    src = bank[banks.slot(s)][0:TR, 0:2 * D]
                    act.activation(st[i][:, int(s[2]), :, :, 0:HD],
                                   src.rearrange("p (s h d) -> p s h d", s=2, h=HEADS),
                                   ACT.Copy).then_inc(hi_qk, 1)
                elif s == "v":
                    banks.wait_full(act, job, tn)
                    src = tok_view(bank[banks.slot(s)])
                    for t in range(2):
                        ins = act.activation(va[i][:, t, :, 0:HD],
                                             src[:, t, :].rearrange("p (h d) -> p h d", h=HEADS),
                                             ACT.Copy, scale=mask[:, t:t + 1])
                    banks.freed(ins, job)
                elif s[:5] == "stack":
                    half = int(s[-1])
                    banks.wait_full(act, job, tn)
                    ins = act.activation(STACKS[s[5]][i][:, 3 * half:3 * half + 3, 0:SEQ],
                                         stack_view(bank[banks.slot(s)])[:, :, 0:SEQ], ACT.Copy)
                    banks.freed(ins, job)
                elif s[:-1] in ("at", "si"):
                    kind, u = s[:2], s[2]
                    score_job = (f"{kind}s{u}", n)
                    scores.wait_full(act, score_job, tn)
                    probr.wait_free(act, job, tn)
                    ins = act.activation(probs[probr.slot(s)][:, :, :], score_view(scores.slot(score_job[0])),
                                         ACT.Exp, scale=ATT_SCALE if kind == "at" else SIM_SCALE)
                    if kind == "at":
                        probr.filled(ins, job)
                    else:
                        ins.then_inc(exp_done, 1)
                elif s[:-1] in ("atp", "sip"):
                    kind, g = s[:2], int(s[3])
                    sums = (f"{kind}v{2 * g}", n)
                    probr.wait_freed(act, (f"{kind}{2 * g + 1}", n), tn)
                    ins = act.activation(pvs[i][:, g, :], pv[pvr.slot(sums[0])][:, 0:SEQ], ACT.Copy)
                    pvr.freed(ins, sums)
                elif s in ("projT", "finT"):
                    hi_half(job, "att" if s == "projT" else "sim", i, tn)
                elif s == "projsq":
                    banks.wait_full(act, ("proj", n), tn)
                    act.activation(sq[:, :, :], tok_view(bank[banks.slot("proj")]), ACT.Square)\
                       .then_inc(sq_done, 1)
                elif s == "proj":
                    banks.wait_freed(act, job, tn)
                    for side in range(2):
                        ins = act.activation(st[i][:, :, side, :, 0:HD],
                                             sn[:, :, :].rearrange("p t (h d) -> p t h d", h=HEADS),
                                             ACT.Copy)
                    ins.then_inc(hi_sn, 1)

            walk(act, ACT_ORDER, do)

        @block.vector
        def _(dve):
            step = Steps(dve, dve_step)
            dve.wait_ge(act_setup, 1)
            dve.wait_ge(weights_in, 16 * 7)
            dve.tensor_tensor(wt[:, 1, :, :].rearrange("p k d -> p (k d)"), wt32[:, :],
                              wt[:, 0, :, :].rearrange("p k d -> p (k d)"), ALU.subtract).then_inc(dve_step, 1)
            for w, w32 in ((wq, wq32), (wp, wp32)):
                dve.tensor_tensor(w[:, 1, :, :], w32[:, :, :], w[:, 0, :, :], ALU.subtract)\
                   .then_inc(dve_step, 1)
            for i in range(IMAGES):
                dve.memset(th[i][DC:DC + 1, :, :], 1.0)
                dve.memset(tl[i][DC:DC + 1, :, :], 0.0)
            step.start(3)
            step(dve.tensor_tensor(base[:, :, :], base[:, :, :], pos_sb[:, :, :], ALU.add))
            for k in range(2):
                dve.sem_inc(bank_free[k], 1)
                dve.sem_inc(score_free[k], 1)
                dve.sem_inc(pv_free[k], 1)
            dve.sem_inc(h_done, IMAGES)
            for i in range(IMAGES):
                dve.sem_inc(stored[i], 32)

            def heads(ap):
                return ap.rearrange("p t (h d) -> p (t h) d", h=HEADS)

            def by_head(ap):
                return ap.rearrange("p (h d) -> p h d", h=HEADS)

            STEPS = {"tokens": 14, "divA": 1, "divS": 1, "proj": 13}

            def do(tn, s, m, i, turn, job):
                n = job[1]
                if s == "tokens":
                    banks.wait_full(dve, job, tn)
                    if tn.part != "pro":
                        banks.wait_freed(dve, ("fin", n - IMAGES), tn)
                    dve.tensor_tensor(h[i][:, :, :], tok_view(bank[banks.slot(s)]), base[:, :, :], ALU.add)\
                       .then_inc(h_done, 1)
                    dve.wait_ge(h_done, m + 4)
                    for t in range(2):
                        ins = dve.bn_stats(stats[:, t, :], h[i][:, t, :])
                        if t == 0:
                            banks.freed(ins, job)
                    step(ins)
                    dve.sem_inc(waited, 1)
                    for t in range(2):
                        ins = dve.bn_aggr(mv[:, t, :], stats[:, t, :])
                    step(ins)
                    step(dve.tensor_scalar(var[:, 0:2], mv[:, :, 1], LN_EPS, None, ALU.add))
                    rsqrt(dve, step, rstd[:, 0:2], var[:, 0:2], tmp[:, 0:2])
                    for t in range(2):
                        ins = dve.tensor_scalar(xn[i][:, t, :], h[i][:, t, :], mv[:, t, 0:1],
                                                rstd[:, t:t + 1], ALU.subtract, ALU.mult)
                    ins.then_inc(xn_done["tok"], 1)
                elif s in ("xnT", "projT", "finT"):
                    name = {"xnT": "tok", "projT": "att", "finT": "sim"}[s]
                    dve.wait_ge(hi_T[name], m + 1)
                    ins = dve.tensor_tensor(tl[i][0:DC, :, :], xT_view(bank[banks.slot(s)]),
                                            th[i][0:DC, :, :], ALU.subtract)
                    banks.freed(ins, job)
                elif s in ("qk0", "qk1"):
                    t = int(s[2])
                    src = bank[banks.slot(s)]
                    dve.wait_ge(hi_qk, m * 2 + t + 1)
                    for side, lo, copy in ((0, HD, 2 * HD), (1, 2 * HD, HD)):
                        hi = st[i][:, t, side, :, 0:HD]
                        dve.tensor_copy(st[i][:, t, side, :, copy:copy + HD], hi)
                        ins = dve.tensor_tensor(st[i][:, t, side, :, lo:lo + HD],
                                                by_head(src[0:TR, side * D:(side + 1) * D]), hi,
                                                ALU.subtract)
                    banks.freed(ins, job)
                elif s[:-1] == "rm":
                    gp, t = divmod(int(s[-1]), 2)
                    scores.wait_full(dve, job, tn)
                    dst = st[i][:, t, 0, 4 * gp:4 * gp + 4, 48].rearrange("p (a b) -> p b a", a=2)
                    ins = dve.tensor_reduce(dst, score_view(scores.slot(s))
                                            .rearrange("p j (g n) -> p j g n", g=2),
                                            AX.X, ALU.max, negate=True)
                    scores.freed(ins, job)
                elif s in ("divA", "divS"):
                    name = "att" if s == "divA" else "sim"
                    v = sums_view(scores.slot(s))
                    scores.wait_full(dve, job, tn)
                    step(dve.reciprocal(den[name][:, :, :], v[:, :, :, HD]))
                    for t in range(2):
                        ins = dve.tensor_tensor(by_head(xn[i][:, t, :]), v[:, t, :, 0:HD],
                                                den[name][:, t, :].unsqueeze(2).broadcast_to([TR, HEADS, HD]),
                                                ALU.mult)
                    ins.then_inc(xn_done[name], 1)
                    scores.freed(dve.memset(mark[:, :], 0.0), job)
                elif s == "proj":
                    dve.wait_ge(sq_done, m + 1)
                    step(dve.tensor_reduce(var[:, :], heads(sq[:, :, :]), AX.X, ALU.add))
                    step(dve.tensor_scalar(var[:, :], var[:, :], NORM_EPS2, None, ALU.max))
                    rsqrt(dve, step, rstd[:, :], var[:, :], tmp[:, :])
                    ins = dve.tensor_tensor(heads(sn[:, :, :]), heads(tok_view(bank[banks.slot(s)])),
                                            rstd[:, :].unsqueeze(2).broadcast_to([TR, 2 * HEADS, HD]),
                                            ALU.mult)
                    banks.freed(ins, job)
                elif s == "projlo":
                    dve.wait_ge(hi_sn, m + 1)
                    for side, lo, copy in ((0, HD, 2 * HD), (1, 2 * HD, HD)):
                        hi = st[i][:, :, side, :, 0:HD]
                        dve.tensor_copy(st[i][:, :, side, :, copy:copy + HD], hi)
                        ins = dve.tensor_tensor(st[i][:, :, side, :, lo:lo + HD],
                                                sn[:, :, :].rearrange("p t (h d) -> p t h d", h=HEADS),
                                                hi, ALU.subtract)
                    ins.then_inc(lo_sn, 1)
                elif s[:-1] == "si":
                    w = probs[probr.slot(s)][:, :, :]
                    dve.wait_ge(exp_done, m * NG + int(s[2]) + 1)
                    probr.filled(dve.scalar_tensor_tensor(w, score_view(scores.slot("sis" + s[2])), 0.0, w,
                                                          ALU.is_ge, ALU.mult), job)
                elif s == "fin":
                    banks.wait_full(dve, job, tn)
                    dve.wait_ge(stored[i], turn * 32 + 32)
                    banks.freed(dve.tensor_tensor(out[i][:, :, :], tok_view(bank[banks.slot(s)]),
                                                  h[i][:, :, :], ALU.add), job)

            SETUP = 4
            steps = {part: sum(STEPS.get(s, 0) for s, _ in tasks) for part, tasks in listed(DVE_ORDER).items()}
            started = set()

            def do_counted(tn, s, m, i, turn, job):
                if tn.part not in started:
                    started.add(tn.part)
                    step.start(tn.count(steps, 0) + SETUP)
                do(tn, s, m, i, turn, job)

            walk(dve, DVE_ORDER, do_counted)


KS = 5
TT = GT // 128
NE = E + 1
CHOICES = 2
ROWS = GROUPS * GT
TILES = CHOICES * GROUPS + E
LISTED = TILES + 2
INDEX_TILES = (E - 1) * GROUPS + LISTED
STEPS_TURN = 2 * (14 + 24 + 9)


class Expert:

    def __init__(self, nc, ctx, sems, tag):
        def sb(name, shape, dt=F32):
            return ctx.enter_context(nc.sbuf_tensor(f"{name}_{tag}", shape, dt))

        def sem(name):
            return sems.enter_context(nc.semaphore(f"{name}_{tag}"))

        self.xsT = [sb(f"xsT{i}", [128, KS, GT], F16) for i in range(2)]
        self.sg = [sb(f"sg{k}", [128, GT]) for k in range(KFF)]
        self.gu32 = [sb(f"gu32{k}", [128, GT]) for k in range(KFF)]
        self.gh = [sb(f"gh{k}", [128, KFF, GT], F16) for k in range(2)]
        self.gl = [sb(f"gl{k}", [128, KFF, GT], F16) for k in range(2)]
        self.GU = [ctx.enter_context(nc.psum_tensor(f"GU{k}_{tag}", [128, 2, 512], F32)) for k in range(2)]
        self.Y = ctx.enter_context(nc.psum_tensor(f"Y_{tag}", [128, 2, 512], F32))
        self.T = [ctx.enter_context(nc.psum_tensor(f"T{k}_{tag}", [128, 512], F32)) for k in range(2)]
        self.gu_full = sem("gu_full")
        self.silu_done = sem("silu_done")
        self.mul_done = sem("mul_done")
        self.hi_done = sem("hi_done")
        self.lo_done = sem("lo_done")
        self.y_full = sem("y_full")
        self.y_used = sem("y_used")

    def y_view(self, t):
        return self.Y[:, t // 2, (t % 2) * D:(t % 2 + 1) * D]

    def hidden(self, pe, n, i, k, w):
        pe.wait_ge(self.mul_done, n * KFF + k + 2)
        for half in range(2):
            for b in range(KS):
                last = pe.matmul(self.GU[(i + k) % 2][:, half, :],
                                 w(b, slice(half * FF + k * 128, half * FF + (k + 1) * 128)),
                                 self.xsT[i][:, b, :], start=(b == 0), stop=(b == KS - 1))
        last.then_inc(self.gu_full, 1)

    def down(self, pe, n, i, w):
        pe.wait_ge(self.lo_done, n * KFF + KFF + 3)
        pe.wait_ge(self.y_used, n + 1)
        parts = [(self.gh, 0), (self.gh, 1), (self.gl, 0)]
        for t in range(TT):
            for j in range(KFF):
                for g, x in parts:
                    last = pe.matmul(self.y_view(t), g[i][:, j, t * 128:(t + 1) * 128], w(x, j),
                                     start=(j == 0 and (g, x) == parts[0]),
                                     stop=(j == KFF - 1 and (g, x) == parts[2]))
        last.then_inc(self.y_full, 1)

    def silu(self, act, n, i, k):
        act.wait_ge(self.gu_full, n * KFF + k + 1)
        act.wait_ge(self.mul_done, n * KFF + k + 1)
        act.activation(self.sg[k][:, :], self.GU[(i + k) % 2][:, 0, :], ACT.Silu).then_inc(self.silu_done, 1)

    def mul(self, dve, n, i, k):
        dve.wait_ge(self.silu_done, n * KFF + k + 1)
        dve.wait_ge(self.lo_done, n * KFF + k + 1)
        dve.tensor_tensor(self.gu32[k][:, :], self.GU[(i + k) % 2][:, 1, :], self.sg[k][:, :],
                          ALU.mult).then_inc(self.mul_done, 1)

    def hi(self, act, n, i, k):
        act.wait_ge(self.mul_done, n * KFF + k + 4)
        if k == 0:
            act.wait_ge(self.y_full, n + 1)
        act.activation(self.gh[i][:, k, :], self.gu32[k][:, :], ACT.Copy).then_inc(self.hi_done, 1)

    def lo(self, pool, n, i, k):
        pool.wait_ge(self.hi_done, n * KFF + k + 1)
        pool.tensor_tensor(self.gl[i][:, k, :], self.gu32[k][:, :], self.gh[i][:, k, :],
                           ALU.subtract).then_inc(self.lo_done, 1)

    def transpose(self, pe, T, rows, blocks, eye16):
        v = T[:, :].bitcast(F16)
        for m, b in enumerate(blocks):
            for t in range(TT):
                last = pe.transpose(v[:, m * GT + t * 128:m * GT + (t + 1) * 128],
                                    rows[:, t, b * 128:(b + 1) * 128], eye16[:, :])
        return last

    def evacuate(self, act, T, i, lo, hi):
        src = T[:, :].bitcast(F16)[:, 0:(hi - lo) * GT].rearrange("p (b n) -> p b n", b=hi - lo)
        return act.activation(self.xsT[i][:, lo:hi, :], src, ACT.Copy)


def feed_forward_phase(nc, sems, h1, w_in, w_down, w_router, e_bias, eye, rank, before, first, token, tile_no, out):
    def dram(name, shape, dt=F32):
        return nc.dram_tensor(name, shape, dt, kind="Internal").ap()

    partial = dram("partial", (ROWS, D))
    split = dram("split", (ROWS, KS * 128), F16)
    lists = dram("lists", (INDEX_TILES * GT, 1), I32)
    routed = dram("routed", (TILES * GT, D))
    with ExitStack() as ctx:
        def sb(name, shape, dt=F32):
            return ctx.enter_context(nc.sbuf_tensor(name, shape, dt))

        weights = {"wi": sb("wi", [128, NE, KS, 2 * FF], F16),
                   "wd": sb("wd", [128, NE, 2, KFF, D], F16),
                   "eye16": sb("eye16f", [128, 128], F16)}
        slots = sb("slots", [128, GROUPS * TT, CHOICES])
        share = sb("share", [128, GROUPS * TT, CHOICES])
        ends = sb("ends", [128, TT + 1, E])
        starts = sb("starts", [128, E])
        place = sb("place", [128, GROUPS * TT, CHOICES], I32)
        shared_stage(nc, sems, weights, slots, share, ends, starts, h1, w_in, w_down, w_router,
                     e_bias, eye, rank, before, first, token, partial, split, lists)
        routed_stage(nc, sems, weights, slots, ends, starts, place, tile_no, split, lists, routed)
        combine_stage(nc, sems, share, place, partial, routed, out)


def shared_stage(nc, sems, weights, slots, share, ends, starts, h1, w_in, w_down, w_router, e_bias, eye,
                 rank, before, first, token, partial, split, lists):
    with ExitStack() as ctx:
        def sb(name, shape, dt=F32):
            return ctx.enter_context(nc.sbuf_tensor(name, shape, dt))

        def sem(name):
            return sems.enter_context(nc.semaphore(name))

        wi, wd, eye16 = weights["wi"], weights["wd"], weights["eye16"]
        ex = Expert(nc, ctx, sems, "sh")
        T = ex.T
        wi32 = [sb(f"wi32_{k}", [128, KS, 2 * FF]) for k in range(2)]
        wd32 = [sb(f"wd32_{k}", [128, KFF, D]) for k in range(2)]
        wr32 = sb("wr32", [128, KS, E])
        wr = sb("wr", [128, KS, E], F16)
        ebias = sb("ebias", [128, TT, E])
        rank_sb = sb("rank_sb", [128, TT, E])
        eye32 = sb("eye32f", [128, 128])
        before32 = sb("before32", [128, 2, 128])
        before16 = sb("before16", [128, 2, 128], F16)
        acc = [sb(f"acc{i}", [128, TT, D]) for i in range(2)]
        xn = sb("xnf", [128, TT, D])
        xs = sb("xs", [128, TT, KS * 128], F16)
        zeros = sb("zeros", [128, INDEX_TILES * GT // 128], I32)
        stats = sb("statsf", [128, TT, 6])
        mv = sb("mvf", [128, TT, 2])
        small = {n: sb(f"{n}_f", [128, TT]) for n in ("var", "rstd", "tmp", "red")}
        wide = {n: sb(f"{n}_f", [128, TT, E]) for n in ("lg", "sc", "sel", "eq", "oh1", "oh2", "sel2", "at")}
        chosen = sb("chosen", [128, TT, E], F16)
        score2 = sb("score2", [128, TT, CHOICES])
        token_f = sb("token_f", [128, TT])
        slot_i = [sb(f"slot_i{i}", [128, TT * CHOICES], I32) for i in range(2)]
        token_i = [sb(f"token_i{i}", [128, TT], I32) for i in range(2)]

        consts_in = sem("consts_in")
        w_in_ld = [sem(f"w_in_ld{k}") for k in range(2)]
        w_hi = sem("w_hi")
        w_lo = sem("w_lo")
        xs_zero = sem("xs_zero")
        lists_zero = sem("lists_zero")
        acc_in = [sem(f"acc_in{i}") for i in range(2)]
        acc_out = [sem(f"acc_out{i}") for i in range(2)]
        xn_ready = sem("xn_ready")
        xs_hi = sem("xs_hi")
        xs_done = sem("xs_done")
        xs_out = sem("xs_out")
        t_full = [sem(f"t_full{k}") for k in range(2)]
        t_free = [sem(f"t_free{k}") for k in range(2)]
        ex_done = sem("ex_done")
        chosen_done = sem("chosen_done")
        rk_full = sem("rk_full")
        rk_free = sem("rk_free")
        slot_ready = sem("slot_ready")
        listed = sem("listed")
        lists_free = sem("lists_free")
        waited = sem("waited_f")
        dstep = sem("dstep")

        block = ctx.enter_context(nc.Block())

        def rows_of(a, f):
            return a[bass.ds(f * GT, GT), :].rearrange("(t p) d -> p t d", p=128)

        @block.sync
        def _(sp):
            for dst, src in ((wr32[:, :, :], w_router), (ebias[:, :, :], e_bias), (rank_sb[:, :, :], rank),
                             (eye32[:, :], eye), (before32[:, :, :], before), (starts[:, :], first),
                             (token_f[:, :], token)):
                sp.dma_start(dst, src).then_inc(consts_in, 16)
            for e in range(NE):
                if e >= 2:
                    sp.wait_ge(w_lo, 2 * (e - 1) + 1)
                sp.dma_start(wi32[e % 2][:, :, :], w_in[e, :, :, :]).then_inc(w_in_ld[e % 2], 16)
                sp.dma_start(wd32[e % 2][:, :, :], w_down[e, :, :, :]).then_inc(w_in_ld[e % 2], 16)
                if e < 2:
                    sp.dma_start(acc[e][:, :, :], rows_of(h1, e)).then_inc(acc_in[e], 16)

            def store_split(f):
                sp.wait_ge(xs_done, f + 1)
                sp.dma_start(rows_of(split, f), xs[:, :, :]).then_inc(xs_out, 16)

            def turn(n, i, it, reload):
                sp.wait_ge(ex.y_used, n + 2)
                sp.dma_start(rows_of(partial, n), acc[i][:, :, :]).then_inc(acc_out[i], 16)
                if reload:
                    sp.wait_ge(acc_out[i], it * 16 + 16)
                    sp.dma_start(acc[i][:, :, :], rows_of(h1, n + 2)).then_inc(acc_in[i], 16)

            store_split(0)
            with sp.Fori(0, GROUPS // 2 - 1) as it:
                for i in range(2):
                    store_split(it * 2 + (i + 1))
                    turn(it * 2 + i, i, it, True)
            last = GROUPS // 2 - 1
            store_split(2 * last + 1)
            turn(2 * last, 0, last, True)
            store_split(2 * last + 2)
            turn(2 * last + 1, 1, last, False)
            turn(2 * last + 2, 0, last + 1, False)
            sp.wait_ge(acc_out[0], 16 * (last + 2))
            sp.wait_ge(acc_out[1], 16 * (last + 1))
            sp.wait_ge(xs_out, 16 * GROUPS + 16)

        @block.gpsimd
        def _(pool):
            pool.memset(zeros[:, :], 0).then_inc(xs_zero, 1)
            pool.wait_ge(xs_zero, 1)
            pool.dma_start(lists[:, :].rearrange("(p a) o -> p (a o)", p=128), zeros[:, :])\
                .then_inc(lists_zero, 16)
            pool.memset(xs[:, :, 3 * D:KS * 128], 0.0).then_inc(xs_zero, 1)
            pool.sem_inc(ex.lo_done, 3)
            pool.wait_ge(lists_zero, 16)

            def front(f):
                pool.wait_ge(xs_hi, f + 1)
                pool.sem_inc(waited, 1)
                pool.tensor_copy(xs[:, :, 2 * D:3 * D], xs[:, :, 0:D])
                pool.tensor_tensor(xs[:, :, D:2 * D], xn[:, :, :], xs[:, :, 0:D],
                                   ALU.subtract).then_inc(xs_done, 1)

            def list_tokens(n, i):
                pool.wait_ge(slot_ready, n + 1)
                pool.sem_inc(waited, 1)
                for t in range(TT):
                    for c in range(CHOICES):
                        k = t * CHOICES + c
                        pool.indirect_dma_start(lists[:, :], bass.IndirectOffsetOnAxis(slot_i[i][:, k:k + 1], 0),
                                                token_i[i][:, t:t + 1], None).then_inc(listed, 16)
                pool.wait_ge(listed, n * 16 * TT * CHOICES + 16 * TT * CHOICES)
                pool.sem_inc(lists_free, 1)

            def group(n, i, nxt):
                ex.lo(pool, n, i, 0)
                if nxt:
                    front(n + 1)
                ex.lo(pool, n, i, 1)
                ex.lo(pool, n, i, 2)
                list_tokens(n, i)

            front(0)
            with pool.Fori(0, GROUPS // 2) as it:
                for i in range(2):
                    group(it * 2 + i, i, True)
            group(GROUPS - 1, 0, False)

        @block.tensor
        def _(pe):
            pe.wait_ge(xs_zero, 2)
            pe.wait_ge(w_lo, 3)
            pe.wait_ge(w_hi, 5)
            pe.sem_inc(ex.y_full, 2)

            def w_up(b, cols):
                return wi[:, 0, b, cols]

            def w_dn(x, j):
                return wd[:, 0, x, j, :]

            def transposes_ab(f):
                pe.wait_ge(xs_done, f + 1)
                pe.wait_ge(t_free[0], f * 3 + 1)
                ex.transpose(pe, T[0], xs, (0, 1), eye16).then_inc(t_full[0], 1)
                pe.wait_ge(t_free[1], f + 1)
                pe.wait_ge(rk_free, f + 1)
                ex.transpose(pe, T[1], xs, (2, 3), eye16).then_inc(t_full[1], 1)

            def transposes_c(f):
                pe.wait_ge(t_free[0], f * 3 + 2)
                ex.transpose(pe, T[0], xs, (4,), eye16).then_inc(t_full[0], 1)

            def logits(f, i):
                pe.wait_ge(t_free[0], f * 3 + 3)
                pe.wait_ge(t_free[1], f + 2)
                for t in range(TT):
                    for b in range(KS):
                        last = pe.matmul(T[0][:, t * E:(t + 1) * E], ex.xsT[i][:, b, t * 128:(t + 1) * 128],
                                         wr[:, b, :], start=(b == 0), stop=(b == KS - 1))
                last.then_inc(t_full[0], 1)

            def counts(n, nxt):
                pe.wait_ge(chosen_done, n + 1)
                pe.wait_ge(t_free[1], n + (3 if nxt else 2))
                rhs = chosen[:, :, :].rearrange("p t e -> p (t e)")
                for k in range(2):
                    last = pe.matmul(T[1][:, k * TT * E:(k + 1) * TT * E], before16[:, k, :], rhs,
                                     start=True, stop=True)
                last.then_inc(rk_full, 1)

            def group(n, i, nxt):
                ex.hidden(pe, n, i, 0, w_up)
                ex.hidden(pe, n, i, 1, w_up)
                if nxt:
                    transposes_ab(n + 1)
                ex.hidden(pe, n, i, 2, w_up)
                if nxt:
                    transposes_c(n + 1)
                counts(n, nxt)
                ex.down(pe, n, i, w_dn)
                if nxt:
                    logits(n + 1, 1 - i)

            transposes_ab(0)
            transposes_c(0)
            logits(0, 0)
            with pe.Fori(0, GROUPS // 2) as it:
                for i in range(2):
                    group(it * 2 + i, i, True)
            group(GROUPS - 1, 0, False)

        @block.scalar
        def _(act):
            act.wait_ge(consts_in, 16 * 7)
            act.activation(eye16[:, :], eye32[:, :], ACT.Copy).then_inc(w_hi, 1)
            act.activation(before16[:, :, :], before32[:, :, :], ACT.Copy).then_inc(w_hi, 1)
            act.activation(wr[:, :, :], wr32[:, :, :], ACT.Copy).then_inc(w_hi, 1)

            def weights_hi(e):
                act.wait_ge(w_in_ld[e % 2], 32 * (e // 2 + 1))
                act.activation(wi[:, e, :, :], wi32[e % 2][:, :, :], ACT.Copy).then_inc(w_hi, 1)
                act.activation(wd[:, e, 0, :, :], wd32[e % 2][:, :, :], ACT.Copy).then_inc(w_hi, 1)

            for e in range(NE):
                weights_hi(e)

            def front_hi(f):
                act.wait_ge(xn_ready, f + 1)
                act.wait_ge(xs_out, f * 16 + 16)
                act.activation(xs[:, :, 0:D], xn[:, :, :], ACT.Copy).then_inc(xs_hi, 1)

            def front_ab(f, i):
                act.wait_ge(t_full[0], f * 3 + 1)
                ex.evacuate(act, T[0], i, 0, 2).then_inc(t_free[0], 1)
                act.wait_ge(t_full[1], f + 1)
                ex.evacuate(act, T[1], i, 2, 4).then_inc(t_free[1], 1)

            def front_c(f, i):
                act.wait_ge(t_full[0], f * 3 + 2)
                ex.evacuate(act, T[0], i, 4, 5).then_inc(t_free[0], 1)

            def front_exp(f):
                act.wait_ge(t_free[0], f * 3 + 4)
                act.activation(wide["lg"][:, :, :], wide["lg"][:, :, :], ACT.Exp).then_inc(ex_done, 1)

            def group(n, i, nxt):
                ex.silu(act, n, i, 0)
                ex.silu(act, n, i, 1)
                ex.hi(act, n, i, 0)
                if nxt:
                    front_hi(n + 1)
                ex.hi(act, n, i, 1)
                if nxt:
                    front_ab(n + 1, 1 - i)
                ex.silu(act, n, i, 2)
                if nxt:
                    front_c(n + 1, 1 - i)
                ex.hi(act, n, i, 2)
                if nxt:
                    front_exp(n + 1)

            front_hi(0)
            front_ab(0, 0)
            front_c(0, 0)
            front_exp(0)
            with act.Fori(0, GROUPS // 2) as it:
                for i in range(2):
                    group(it * 2 + i, i, True)
            group(GROUPS - 1, 0, False)

        @block.vector
        def _(dve):
            step = Steps(dve, dstep)
            dve.sem_inc(ex.mul_done, 3)
            dve.sem_inc(ex.y_used, 1)
            dve.sem_inc(rk_free, 2)
            dve.sem_inc(xs_out, 16)
            dve.sem_inc(lists_free, 2)
            for k in range(2):
                dve.sem_inc(t_free[k], 1)
            dve.wait_ge(w_hi, 3)
            lo_rows = slice(3, KS)
            dve.tensor_tensor(wr[:, lo_rows, :], wr32[:, lo_rows, :], wr[:, lo_rows, :],
                              ALU.subtract).then_inc(w_lo, 1)

            def weights_lo(e):
                dve.wait_ge(w_hi, 2 * e + 5)
                dve.tensor_tensor(wi[:, e, lo_rows, :], wi32[e % 2][:, lo_rows, :], wi[:, e, lo_rows, :],
                                  ALU.subtract).then_inc(w_lo, 1)
                dve.tensor_tensor(wd[:, e, 1, :, :], wd32[e % 2][:, :, :], wd[:, e, 0, :, :],
                                  ALU.subtract).then_inc(w_lo, 1)

            for e in range(NE):
                weights_lo(e)
            step(dve.tensor_copy(ends[:, 0, :], starts[:, :]))

            def norm(f, i, turn):
                dve.wait_ge(acc_in[i], turn * 16 + 16)
                for t in range(TT):
                    ins = dve.bn_stats(stats[:, t, :], acc[i][:, t, :])
                step(ins)
                dve.sem_inc(waited, 1)
                for t in range(TT):
                    ins = dve.bn_aggr(mv[:, t, :], stats[:, t, :])
                step(ins)
                v, y, tm = (small[x][:, :] for x in ("var", "rstd", "tmp"))
                step(dve.tensor_scalar(v, mv[:, :, 1], LN_EPS, None, ALU.add))
                rsqrt(dve, step, y, v, tm)
                for t in range(TT):
                    ins = dve.tensor_scalar(xn[:, t, :], acc[i][:, t, :], mv[:, t, 0:1],
                                            small["rstd"][:, t:t + 1], ALU.subtract, ALU.mult)
                ins.then_inc(xn_ready, 1)

            w = {n: t[:, :, :] for n, t in wide.items()}
            red = small["red"]
            one = red[:, :].unsqueeze(2).broadcast_to([128, TT, E])

            def route(f):
                lg_psum = T[0][:, 0:TT * E].rearrange("p (t e) -> p t e", t=TT)
                dve.wait_ge(t_full[0], f * 3 + 3)
                step(dve.tensor_reduce(red[:, :], lg_psum, AX.X, ALU.max))
                ins = dve.tensor_tensor(w["lg"], lg_psum, one, ALU.subtract)
                ins.then_inc(t_free[0], 1)
                dve.wait_ge(ex_done, f + 1)
                step(dve.tensor_reduce(red[:, :], w["lg"], AX.X, ALU.add))
                step(dve.reciprocal(red[:, :], red[:, :]))
                step(dve.tensor_tensor(w["sc"], w["lg"], one, ALU.mult))
                step(dve.tensor_tensor(w["sel"], w["sc"], ebias[:, :, :], ALU.add))
                for name, src in (("oh1", "sel"), ("oh2", "sel2")):
                    if name == "oh2":
                        step(dve.scalar_tensor_tensor(w["sel2"], w["oh1"], -1e30, w["sel"],
                                                      ALU.mult, ALU.add))
                    step(dve.tensor_reduce(red[:, :], w[src], AX.X, ALU.max))
                    step(dve.tensor_tensor(w["eq"], w[src], one, ALU.is_equal))
                    step(dve.tensor_tensor(w["eq"], w["eq"], rank_sb[:, :, :], ALU.mult))
                    step(dve.tensor_reduce(red[:, :], w["eq"], AX.X, ALU.max))
                    step(dve.tensor_tensor(w[name], w["eq"], one, ALU.is_equal))
                dve.tensor_tensor(chosen[:, :, :], w["oh1"], w["oh2"], ALU.add).then_inc(chosen_done, 1)
                for c, oh in enumerate(("oh1", "oh2")):
                    step(dve.tensor_tensor(w["eq"], w[oh], w["sc"], ALU.mult))
                    step(dve.tensor_reduce(score2[:, :, c], w["eq"], AX.X, ALU.add))
                step(dve.tensor_tensor(red[:, :], score2[:, :, 0], score2[:, :, 1], ALU.add))
                step(dve.tensor_scalar(red[:, :], red[:, :], 1e-9, None, ALU.add))
                step(dve.reciprocal(red[:, :], red[:, :]))
                step(dve.tensor_tensor(share[:, bass.ds(f * TT, TT), :], score2[:, :, :],
                                       red[:, :].unsqueeze(2).broadcast_to([128, TT, CHOICES]), ALU.mult))

            def places(n, i, turn):
                pre, tot = (T[1][:, k * TT * E:(k + 1) * TT * E].rearrange("p (t e) -> p t e", t=TT)
                            for k in range(2))
                dve.wait_ge(rk_full, n + 1)
                for t in range(TT):
                    step(dve.tensor_tensor(ends[:, t + 1, :], ends[:, t, :], tot[:, t, :], ALU.add))
                dve.tensor_tensor(w["at"], pre, ends[:, 0:TT, :], ALU.add).then_inc(rk_free, 1)
                dve.wait_ge(rk_free, n + 3)
                mine = slots[:, bass.ds(n * TT, TT), :]
                for c, oh in enumerate(("oh1", "oh2")):
                    step(dve.tensor_tensor(w["eq"], w[oh], w["at"], ALU.mult))
                    step(dve.tensor_reduce(mine[:, :, c], w["eq"], AX.X, ALU.add))
                dve.wait_ge(lists_free, n + 1)
                dve.tensor_copy(token_i[i][:, :], token_f[:, :])
                dve.tensor_copy(slot_i[i][:, :], mine.rearrange("p t c -> p (t c)")).then_inc(slot_ready, 1)
                dve.wait_ge(slot_ready, n + 1)
                dve.tensor_copy(ends[:, 0, :], ends[:, TT, :])
                step(dve.tensor_scalar(token_f[:, :], token_f[:, :], float(GT), None, ALU.add))

            def add_shared(n, i):
                dve.wait_ge(ex.y_full, n + 3)
                for t in range(TT):
                    a = acc[i][:, t, :]
                    ins = dve.tensor_tensor(a, ex.y_view(t), a, ALU.add)
                ins.then_inc(ex.y_used, 1)

            def group(n, i, nxt, turn):
                ex.mul(dve, n, i, 0)
                if nxt:
                    norm(n + 1, 1 - i, turn + i)
                ex.mul(dve, n, i, 1)
                ex.mul(dve, n, i, 2)
                places(n, i, turn)
                add_shared(n, i)
                if nxt:
                    route(n + 1)

            norm(0, 0, 0)
            route(0)
            begun = step.n
            with dve.Fori(0, GROUPS // 2) as it:
                step.start(it * STEPS_TURN + begun)
                for i in range(2):
                    group(it * 2 + i, i, True, it)
                assert step.n == STEPS_TURN, step.n
            step.start(GROUPS // 2 * STEPS_TURN + begun)
            group(GROUPS - 1, 0, False, GROUPS // 2)


def routed_stage(nc, sems, weights, slots, ends, starts, place, tile_no, split, lists, routed):
    with ExitStack() as ctx:
        def sb(name, shape, dt=F32):
            return ctx.enter_context(nc.sbuf_tensor(name, shape, dt))

        def sem(name):
            return sems.enter_context(nc.semaphore(name))

        wi, wd, eye16 = weights["wi"], weights["wd"], weights["eye16"]
        ex = Expert(nc, ctx, sems, "ro")
        T = ex.T
        number = sb("number", [128, LISTED])
        tiles_i = sb("tiles_i", [128, E], I32)
        tiles = sb("tiles", [128, E])
        start = sb("start", [128, E])
        gap_t = sb("gap_t", [128, E])
        gap_r = sb("gap_r", [128, E])
        count = sb("count", [128, E])
        expert_f = sb("expert_f", [128, LISTED])
        from_f = sb("from_f", [128, LISTED])
        part = sb("part", [128, LISTED])
        place_f = sb("place_f", [128, GROUPS * TT * CHOICES])
        part_p = sb("part_p", [128, GROUPS * TT * CHOICES])
        table = sb("table", [128, 2, LISTED], I32)
        picks = [sb(f"picks{i}", [128, TT], I32) for i in range(2)]
        xg = [sb(f"xg{i}", [128, TT, KS * 128], F16) for i in range(2)]
        ysb = [sb(f"ysb{i}", [128, TT, D]) for i in range(2)]

        number_in = sem("number_in")
        table_done = sem("table_done")
        picks_in = [sem(f"picks_in{i}") for i in range(2)]
        fetched = [sem(f"fetched{i}") for i in range(2)]
        picks_free = sem("picks_free")
        r_full = [sem(f"r_full{k}") for k in range(2)]
        r_free = [sem(f"r_free{k}") for k in range(2)]
        y_out = [sem(f"y_out{i}") for i in range(2)]
        dstep = sem("dstep_r")
        waited = sem("waited_r")

        block = ctx.enter_context(nc.Block())

        @block.sync
        def _(sp):
            sp.dma_start(number[:, :], tile_no).then_inc(number_in, 16)
            sp.wait_ge(table_done, 1)
            with sp.Fori(0, LISTED // 2) as it:
                for i in range(2):
                    j = it * 2 + i
                    at = sp.value_load(table[0:1, 1, bass.ds(j, 1)], min_val=0, max_val=INDEX_TILES - 1)
                    sp.wait_ge(picks_free, j + 1)
                    sp.dma_start(picks[i][:, :], lists[bass.ds(at * GT, GT), :]
                                 .rearrange("(p t) o -> p (t o)", p=128)).then_inc(picks_in[i], 16)
            for i in range(2):
                sp.wait_ge(picks_in[i], LISTED // 2 * 16)

        @block.gpsimd
        def _(pool):
            pool.sem_inc(ex.lo_done, 3)

            def fetch(j, i, turn, again=True):
                pool.wait_ge(picks_in[i], turn * 16 + 16)
                if again:
                    pool.wait_ge(r_full[0], j * 2 - 2)
                pool.sem_inc(waited, 1)
                for t in range(TT):
                    pool.indirect_dma_start(xg[i][:, t, :], None, split[:, :],
                                            bass.IndirectOffsetOnAxis(picks[i][:, t:t + 1], 0))\
                        .then_inc(fetched[i], 16)

            def fetch_done(i, turn):
                pool.wait_ge(fetched[i], turn * 64 + 64)
                pool.sem_inc(picks_free, 1)

            for i in range(2):
                fetch(i, i, 0, False)
            for i in range(2):
                fetch_done(i, 0)
            with pool.Fori(0, TILES // 2) as it:
                for i in range(2):
                    fetch(it * 2 + (i + 2), i, it + 1)
                    for k in range(KFF):
                        ex.lo(pool, it * 2 + i, i, k)
                    fetch_done(i, it + 1)

        @block.tensor
        def _(pe):
            pe.sem_inc(ex.y_full, 2)
            pe.wait_ge(table_done, 1)

            def transposes_ab(j, i, turn):
                pe.wait_ge(fetched[i], turn * 64 + 64)
                pe.wait_ge(r_free[0], j * 2 + 1)
                ex.transpose(pe, T[0], xg[i], (0, 1), eye16).then_inc(r_full[0], 1)
                pe.wait_ge(r_free[1], j + 1)
                ex.transpose(pe, T[1], xg[i], (2, 3), eye16).then_inc(r_full[1], 1)

            def transposes_c(j, i):
                pe.wait_ge(r_free[0], j * 2 + 2)
                ex.transpose(pe, T[0], xg[i], (4,), eye16).then_inc(r_full[0], 1)

            transposes_ab(0, 0, 0)
            transposes_c(0, 0)

            def tile(j, i, turn, before):
                e = pe.value_load(table[0:1, 0, bass.ds(j, 1)], min_val=1, max_val=E)

                def w_up(b, cols):
                    return wi[:, bass.ds(e, 1), b, cols].rearrange("p o m -> p (o m)")

                pe.wait_ge(r_free[0], j * 2 + 3)
                pe.wait_ge(r_free[1], j + 2)
                ex.hidden(pe, j, i, 0, w_up)
                transposes_ab(j + 1, 1 - i, turn + i)
                ex.hidden(pe, j, i, 1, w_up)
                transposes_c(j + 1, 1 - i)
                ex.hidden(pe, j, i, 2, w_up)
                if before:
                    output(j - 1, 1 - i)

            def output(j, i):
                e = pe.value_load(table[0:1, 0, bass.ds(j, 1)], min_val=1, max_val=E)
                ex.down(pe, j, i, lambda x, k: wd[:, bass.ds(e, 1), x, k, :].rearrange("p o m -> p (o m)"))

            tile(0, 0, 0, False)
            tile(1, 1, 0, True)
            with pe.Fori(1, TILES // 2) as it:
                for i in range(2):
                    tile(it * 2 + i, i, it, True)
            output(TILES - 1, 1)

        @block.scalar
        def _(act):
            def front_ab(j, i):
                act.wait_ge(r_full[0], j * 2 + 1)
                ex.evacuate(act, T[0], i, 0, 2).then_inc(r_free[0], 1)
                act.wait_ge(r_full[1], j + 1)
                ex.evacuate(act, T[1], i, 2, 4).then_inc(r_free[1], 1)

            def front_c(j, i):
                act.wait_ge(r_full[0], j * 2 + 2)
                ex.evacuate(act, T[0], i, 4, 5).then_inc(r_free[0], 1)

            def store(j, i):
                act.wait_ge(ex.y_used, j + 2)
                act.dma_start(routed[bass.ds(j * GT, GT), :].rearrange("(p t) d -> p t d", p=128),
                              ysb[i][:, :, :]).then_inc(y_out[i], 16)

            def tile(j, i, stores):
                ex.silu(act, j, i, 0)
                if stores:
                    store(j - 2, i)
                front_ab(j + 1, 1 - i)
                ex.silu(act, j, i, 1)
                ex.hi(act, j, i, 0)
                front_c(j + 1, 1 - i)
                ex.silu(act, j, i, 2)
                ex.hi(act, j, i, 1)
                ex.hi(act, j, i, 2)

            front_ab(0, 0)
            front_c(0, 0)
            tile(0, 0, False)
            tile(1, 1, False)
            with act.Fori(1, TILES // 2) as it:
                for i in range(2):
                    tile(it * 2 + i, i, True)
            store(TILES - 2, 0)
            store(TILES - 1, 1)
            for i in range(2):
                act.wait_ge(y_out[i], TILES // 2 * 16 + 16)

        @block.vector
        def _(dve):
            step = Steps(dve, dstep)
            dve.sem_inc(ex.mul_done, 3)
            dve.sem_inc(ex.y_used, 1)
            dve.sem_inc(picks_free, 2)
            for k in range(2):
                dve.sem_inc(r_free[k], 1)
                dve.sem_inc(y_out[k], 16)
            step(dve.tensor_tensor(count[:, :], ends[:, 0, :], starts[:, :], ALU.subtract))
            step(dve.tensor_scalar(tiles_i[:, :], count[:, :], float(GT - 1), None, ALU.add))
            step(dve.tensor_scalar(tiles_i[:, :], tiles_i[:, :], GT.bit_length() - 1, None,
                                   ALU.logical_shift_right))
            step(dve.tensor_copy(tiles[:, :], tiles_i[:, :]))
            step(dve.memset(start[:, :], 0.0))
            for e in range(1, E):
                step(dve.tensor_tensor(start[:, e:e + 1], start[:, e - 1:e], tiles[:, e - 1:e], ALU.add))
            step(dve.tensor_scalar(gap_t[:, :], tiles[:, :], -1.0, float(GROUPS), ALU.mult, ALU.add))
            step(dve.tensor_scalar(gap_r[:, :], gap_t[:, :], float(-GT), None, ALU.mult))
            dve.wait_ge(number_in, 16)
            step(dve.memset(expert_f[:, :], 1.0))
            step(dve.tensor_copy(from_f[:, :], number[:, :]))
            for e in range(1, E):
                step(dve.scalar_tensor_tensor(expert_f[:, :], number[:, :], start[:, e:e + 1],
                                              expert_f[:, :], ALU.is_ge, ALU.add))
                step(dve.tensor_scalar(part[:, :], number[:, :], start[:, e:e + 1], gap_t[:, e - 1:e],
                                       ALU.is_ge, ALU.mult))
                step(dve.tensor_tensor(from_f[:, :], from_f[:, :], part[:, :], ALU.add))
            dve.tensor_copy(table[:, 0, :], expert_f[:, :])
            dve.tensor_copy(table[:, 1, :], from_f[:, :]).then_inc(table_done, 1)
            places = slots[:, :, :].rearrange("p t c -> p (t c)")
            step(dve.tensor_copy(place_f[:, :], places))
            for e in range(1, E):
                step(dve.tensor_scalar(part_p[:, :], places, starts[:, e:e + 1], gap_r[:, e - 1:e],
                                       ALU.is_ge, ALU.mult))
                step(dve.tensor_tensor(place_f[:, :], place_f[:, :], part_p[:, :], ALU.add))
            step(dve.tensor_copy(place[:, :, :].rearrange("p t c -> p (t c)"), place_f[:, :]))

            def output(j, i, turn):
                dve.wait_ge(ex.y_full, j + 3)
                dve.wait_ge(y_out[i], turn * 16 + 16)
                for half in range(2):
                    ins = dve.tensor_copy(ysb[i][:, 2 * half:2 * half + 2, :],
                                          ex.Y[:, half, 0:2 * D].rearrange("p (t d) -> p t d", t=2))
                ins.then_inc(ex.y_used, 1)

            def tile(j, i, turn, before):
                for k in range(KFF):
                    ex.mul(dve, j, i, k)
                if before:
                    output(j - 1, 1 - i, turn + i - 1)

            tile(0, 0, 0, False)
            tile(1, 1, 0, True)
            with dve.Fori(1, TILES // 2) as it:
                for i in range(2):
                    tile(it * 2 + i, i, it, True)
            output(TILES - 1, 1, TILES // 2 - 1)


def combine_stage(nc, sems, share, place, partial, routed, out):
    with ExitStack() as ctx:
        def sb(name, shape, dt=F32):
            return ctx.enter_context(nc.sbuf_tensor(name, shape, dt))

        def sem(name):
            return sems.enter_context(nc.semaphore(name))

        N = 3 if GROUPS % 3 == 1 else 2
        acc = [sb(f"sum{i}", [128, TT, D]) for i in range(N)]
        rows = [sb(f"rows{i}", [128, TT, CHOICES, D]) for i in range(N)]
        at = [sb(f"at{i}", [128, TT * CHOICES], I32) for i in range(N)]
        by = [sb(f"by{i}", [128, TT, CHOICES]) for i in range(N)]
        sum_in = [sem(f"sum_in{i}") for i in range(N)]
        at_done = sem("at_done")
        rows_in = [sem(f"rows_in{i}") for i in range(N)]
        sums_done = sem("sums_done")
        added = sem("added")
        waited = sem("waited_c")
        sum_out = [sem(f"sum_out{i}") for i in range(N)]

        block = ctx.enter_context(nc.Block())

        def rows_of(a, f):
            return a[bass.ds(f * GT, GT), :].rearrange("(t p) d -> p t d", p=128)

        @block.sync
        def _(sp):
            for i in range(N):
                sp.dma_start(acc[i][:, :, :], rows_of(partial, i)).then_inc(sum_in[i], 16)

            def store(n, i):
                sp.wait_ge(sums_done, n + N + 1)
                sp.dma_start(rows_of(out, n), acc[i][:, :, :]).then_inc(sum_out[i], 16)

            with sp.Fori(0, GROUPS // N - 1) as it:
                for i in range(N):
                    store(it * N + i, i)
                    sp.wait_ge(sum_out[i], it * 16 + 16)
                    sp.dma_start(acc[i][:, :, :], rows_of(partial, it * N + (i + N))).then_inc(sum_in[i], 16)
            for n in range(GROUPS - 1 - N, GROUPS - 1):
                store(n, n % N)
                if n == GROUPS - 1 - N:
                    sp.wait_ge(sum_out[0], GROUPS // N * 16)
                    sp.dma_start(acc[0][:, :, :], rows_of(partial, GROUPS - 1)).then_inc(sum_in[0], 16)
            n = GROUPS - 1
            sp.wait_ge(sums_done, n + N + 1)
            whole = TAIL // 128
            sp.dma_start(out[n * GT:n * GT + whole * 128, :].rearrange("(t p) d -> p t d", p=128),
                         acc[0][:, 0:whole, :]).then_inc(sum_out[0], 16)
            sp.dma_start(out[n * GT + whole * 128:TOK, :], acc[0][0:TAIL - whole * 128, whole, :])\
              .then_inc(sum_out[0], 16)
            for i in range(N):
                sp.wait_ge(sum_out[i], 16 * (GROUPS // N) + (32 if i == 0 else 0))

        @block.gpsimd
        def _(pool):
            def fetch(n, i):
                pool.wait_ge(at_done, n + 1)
                pool.sem_inc(waited, 1)
                for k in range(TT * CHOICES):
                    pool.indirect_dma_start(rows[i][:, k // CHOICES, k % CHOICES, :], None, routed[:, :],
                                            bass.IndirectOffsetOnAxis(at[i][:, k:k + 1], 0))\
                        .then_inc(rows_in[i], 16)

            with pool.Fori(0, GROUPS // N) as it:
                for i in range(N):
                    fetch(it * N + i, i)
            fetch(GROUPS - 1, 0)

        @block.vector
        def _(dve):
            dve.sem_inc(sums_done, N)

            def name_rows(n, i, turn):
                dve.wait_ge(sums_done, n + 1)
                span = bass.ds(n * TT, TT)
                dve.tensor_copy(by[i][:, :, :], share[:, span, :])
                dve.tensor_copy(at[i][:, :], place[:, span, :].rearrange("p t c -> p (t c)"))\
                   .then_inc(at_done, 1)

            def combine(n, i, turn):
                dve.wait_ge(sum_in[i], turn * 16 + 16)
                dve.wait_ge(at_done, n + 1)
                dve.wait_ge(rows_in[i], turn * 128 + 128)
                for c in range(CHOICES):
                    for t in range(TT):
                        a = acc[i][:, t, :]
                        ins = dve.scalar_tensor_tensor(a, rows[i][:, t, c, :], by[i][:, t, c:c + 1], a,
                                                       ALU.mult, ALU.add)
                    if c == 0:
                        ins.then_inc(added, 1)
                        dve.wait_ge(added, n + 1)
                ins.then_inc(sums_done, 1)

            for i in range(N):
                name_rows(i, i, 0)
            with dve.Fori(0, GROUPS // N - 1) as it:
                for i in range(N):
                    combine(it * N + i, i, it)
                    name_rows(it * N + (i + N), i, it + 1)
            for n in range(GROUPS - 1 - N, GROUPS):
                combine(n, n % N, n // N)
                if n == GROUPS - 1 - N:
                    name_rows(GROUPS - 1, 0, GROUPS // N)


def build(nc, xT, w_tok, addend, pos, w_qkv, w_proj, w_in, w_down, w_router, e_bias, eye, key_mask, rank,
          before, first, token, tile_no, out):
    h1 = nc.dram_tensor("h1_scratch", (GROUPS * GT, D), F32, kind="Internal").ap()
    with ExitStack() as sems:
        attention_phase(nc, sems, xT, w_tok, addend, pos, w_qkv, w_proj, eye, key_mask, h1)
        feed_forward_phase(nc, sems, h1, w_in, w_down, w_router, e_bias, eye, rank, before, first,
                           token, tile_no, out)


def lay_out(inputs):
    import numpy as np

    def a(name):
        return np.ascontiguousarray(inputs[name])

    x = a("x").reshape(B, CH, SIDE, P, SIDE, P).transpose(0, 1, 3, 5, 2, 4).reshape(B, KF, 128, SEQ - 1)
    xT = np.zeros((B, 128, KF, SEQ), np.float32)
    xT[..., 1:] = x.transpose(0, 2, 1, 3)
    tiles = np.stack([np.arange(TR), np.arange(TR) + HALF], 1)
    w_tok = a("L0_tok_W").reshape(KF, 128, D).transpose(1, 0, 2).reshape(128, KF * D)
    addend = np.broadcast_to(a("L0_tok_b"), (TR, 2, D)).copy()
    addend[0, 0] = a("L0_tok_class_token").reshape(D)
    pos = a("L0_tok_pos_table")[tiles]

    def with_bias(w, b):
        r = np.zeros((DC + 1, 2, w.shape[0]), np.float32)
        r[:DC] = w.T.reshape(2, DC, -1).transpose(1, 0, 2)
        r[DC, 0] = b
        return r

    def stacked(w):
        r = np.zeros(w.shape[:-2] + (KS * 128, w.shape[-1]), np.float32)
        for k in range(3):
            r[..., k * D:(k + 1) * D, :] = w
        return np.moveaxis(r.reshape(w.shape[:-2] + (KS, 128, w.shape[-1])), -3, -2)

    gate = np.concatenate([a("L0_ffn_sg")[None], a("L0_ffn_Wg")])
    up = np.concatenate([a("L0_ffn_su")[None], a("L0_ffn_Wu")])
    down = np.concatenate([a("L0_ffn_sd")[None], a("L0_ffn_Wd")])
    w_in = stacked(np.concatenate([gate, up], 1).transpose(0, 2, 1))
    w_down = down.transpose(0, 2, 1).reshape(NE, KFF, 128, D).transpose(0, 2, 1, 3)
    mask = np.ones((TR, 2), np.float32)
    mask[0, 1] = 0.0
    before = np.ones((128, 2, 128), np.float32)
    before[:, 0] = np.triu(before[:, 0], 1)
    return {
        "xT": xT, "w_tok": w_tok, "addend": addend, "pos": pos,
        "w_qkv": with_bias(a("L0_attn_qkv_w"), a("L0_attn_qkv_b")),
        "w_proj": with_bias(a("L0_attn_proj_w"), a("L0_attn_proj_b")),
        "w_in": w_in, "w_down": w_down, "w_router": stacked(a("L0_ffn_w_router").T),
        "e_bias": np.broadcast_to(a("L0_ffn_expert_bias"), (128, TT, E)),
        "eye": np.eye(128, dtype=np.float32), "key_mask": mask,
        "rank": np.broadcast_to(np.arange(E, 0, -1, dtype=np.float32), (128, TT, E)),
        "before": before,
        "first": np.broadcast_to(np.arange(E, dtype=np.float32) * ROWS, (128, E)),
        "token": (np.arange(GT, dtype=np.float32).reshape(TT, 128).T),
        "tile_no": np.broadcast_to(np.arange(LISTED, dtype=np.float32), (128, LISTED)),
    }


def kernel(**inputs):
    import numpy as np
    import concourse.bacc as bacc
    from concourse.bass_utils import run_bass_kernel_spmd

    nc = bacc.Bacc("TRN2", target_bir_lowering=False, num_devices=1)
    arrays, args = {}, []
    for name, value in lay_out(inputs).items():
        value = np.ascontiguousarray(value)
        arrays[f"in_{name}"] = value
        args.append(nc.dram_tensor(f"in_{name}", value.shape, mybir.dt.from_np(value.dtype),
                                   kind="ExternalInput").ap())
    out = nc.dram_tensor("out", (TOK, D), F32, kind="ExternalOutput").ap()
    build(nc, *args, out)
    result = run_bass_kernel_spmd(nc, [arrays], core_ids=[0])
    return result.results[0]["out"].reshape(B, SEQ, D)
```
